# Optimizing a Trainium2 kernel written in Bass

```python
import numpy as np
import jax
import jax.numpy as jnp

def _softmax(x, axis=-1):
    return jax.nn.softmax(x, axis=axis)

def _gelu(x):
    return jax.nn.gelu(x, approximate=True)

def _silu(x):
    return jax.nn.silu(x)

def _sigmoid(x):
    return jax.nn.sigmoid(x)

def _layernorm(x, axis=-1, eps=1e-05):
    m = jnp.mean(x, axis=axis, keepdims=True)
    v = jnp.var(x, axis=axis, keepdims=True)
    return (x - m) / jnp.sqrt(v + eps)

def _scatter_add(tgt, idx, src, axis=0):
    return tgt.at[idx].add(src)

def _segment_sum(src, seg, n):
    return jax.ops.segment_sum(src, seg, n)
kernel_name = 'mk_macaron_d1_jaxref_r8_8e13c1'

def setup_inputs(seed: int=0):
    np.random.seed(seed)
    _w = jnp.asarray

    def _L0_attn_setup():
        import jax, jax.numpy as jnp
        import numpy as np
        D_MODEL = 256
        D_STATE = 128
        D_CONV = 4
        EXPAND = 2
        HEADDIM = 64
        NGROUPS = 1
        CHUNK = 32
        D_INNER = EXPAND * D_MODEL
        NHEADS = D_INNER // HEADDIM
        HG = NHEADS // NGROUPS
        CONV_DIM = D_INNER + 2 * NGROUPS * D_STATE
        D_IN_PROJ = 2 * D_INNER + 2 * NGROUPS * D_STATE + NHEADS
        BATCH = 2
        SEQLEN = 256
        EPS = 1e-05

        def _mamba2(u, in_proj_w, conv_w, conv_b, dt_bias, A_log, D_skip, norm_w, out_proj_w):
            b, l, _ = u.shape
            nc = l // CHUNK
            zxbcdt = u @ in_proj_w.T
            z = zxbcdt[..., :D_INNER]
            xBC = zxbcdt[..., D_INNER:D_INNER + CONV_DIM]
            dt = jax.nn.softplus(zxbcdt[..., D_INNER + CONV_DIM:] + dt_bias)
            xp = jnp.pad(xBC, ((0, 0), (D_CONV - 1, 0), (0, 0)))
            conv = conv_b + sum((conv_w[:, k] * xp[:, k:k + l, :] for k in range(D_CONV)))
            xBC = jax.nn.silu(conv)
            x = xBC[..., :D_INNER].reshape(b, l, NHEADS, HEADDIM)
            Bm = xBC[..., D_INNER:D_INNER + NGROUPS * D_STATE].reshape(b, l, NGROUPS, D_STATE)
            Cm = xBC[..., D_INNER + NGROUPS * D_STATE:].reshape(b, l, NGROUPS, D_STATE)
            A = -jnp.exp(A_log)
            xc = x.reshape(b, nc, CHUNK, NGROUPS, HG, HEADDIM)
            dtc = dt.reshape(b, nc, CHUNK, NGROUPS, HG)
            Bc = Bm.reshape(b, nc, CHUNK, NGROUPS, D_STATE)
            Cc = Cm.reshape(b, nc, CHUNK, NGROUPS, D_STATE)
            dA = jnp.transpose(dtc * A.reshape(NGROUPS, HG), (0, 3, 4, 1, 2))
            dA_cs = jnp.cumsum(dA, axis=-1)
            seg = dA_cs[..., :, None] - dA_cs[..., None, :]
            tri = jnp.tril(jnp.ones((CHUNK, CHUNK), bool))
            Lmat = jnp.where(tri, jnp.exp(seg), 0.0)
            xdt = xc * dtc[..., None]
            CB = jnp.einsum('bclgn,bcsgn->bcgls', Cc, Bc)
            Y_diag = jnp.einsum('bcgls,bgHcls,bcsgHp->bclgHp', CB, Lmat, xdt)
            decay_states = jnp.exp(dA_cs[..., -1:] - dA_cs)
            states = jnp.einsum('bcsgn,bgHcs,bcsgHp->bcgHpn', Bc, decay_states, xdt)
            chunk_decay = jnp.exp(dA_cs[..., -1])

            def step(carry, inp):
                st, dec = inp
                return (carry * dec[..., None, None] + st, carry)
            _, prev = jax.lax.scan(step, jnp.zeros_like(states[:, 0]), (jnp.moveaxis(states, 1, 0), jnp.moveaxis(chunk_decay, -1, 0)))
            prev = jnp.moveaxis(prev, 0, 1)
            Y_off = jnp.einsum('bclgn,bcgHpn,bgHcl->bclgHp', Cc, prev, jnp.exp(dA_cs))
            y = (Y_diag + Y_off).reshape(b, l, NHEADS, HEADDIM) + x * D_skip[None, None, :, None]
            y = y.reshape(b, l, D_INNER)
            y = y * jax.nn.silu(z)
            yg = y.reshape(b, l, NGROUPS, D_INNER // NGROUPS)
            yg = yg * jax.lax.rsqrt(jnp.mean(yg * yg, axis=-1, keepdims=True) + EPS)
            y = yg.reshape(b, l, D_INNER) * norm_w
            return y @ out_proj_w.T
        ks = jax.random.split(jax.random.key(seed), 8)
        u = jax.random.normal(ks[0], (BATCH, SEQLEN, D_MODEL), jnp.float32)
        in_proj_w = jax.random.normal(ks[1], (D_IN_PROJ, D_MODEL), jnp.float32) * D_MODEL ** (-0.5)
        conv_w = jax.random.normal(ks[2], (CONV_DIM, D_CONV), jnp.float32) * D_CONV ** (-0.5)
        conv_b = jax.random.normal(ks[3], (CONV_DIM,), jnp.float32) * 0.1
        dt = jnp.exp(jax.random.uniform(ks[4], (NHEADS,), jnp.float32) * (np.float32(np.log(0.1)) - np.float32(np.log(0.001))) + np.float32(np.log(0.001)))
        dt = jnp.clip(dt, 0.0001, None)
        dt_bias = dt + jnp.log(-jnp.expm1(-dt))
        A_log = jnp.log(jax.random.uniform(ks[5], (NHEADS,), jnp.float32, minval=1.0, maxval=16.0))
        D_skip = jnp.ones((NHEADS,), jnp.float32)
        norm_w = jnp.ones((D_INNER,), jnp.float32)
        out_proj_w = jax.random.normal(ks[6], (D_MODEL, D_INNER), jnp.float32) * D_INNER ** (-0.5)
        return dict(u=u, in_proj_w=in_proj_w, conv_w=conv_w, conv_b=conv_b, dt_bias=dt_bias, A_log=A_log, D_skip=D_skip, norm_w=norm_w, out_proj_w=out_proj_w)
    _L0_attn_in = _L0_attn_setup()

    def _L0_ffn_setup():
        import jax, jax.numpy as jnp
        import numpy as np
        BLOCK_SIZE = 32
        HIDDEN_SIZE = 256
        MLP_DIM = 2048
        NVFP4_LUT = jnp.array([0.0, 0.5, 1.0, 1.5, 2.0, 3.0, 4.0, 6.0, 0.0, -0.5, -1.0, -1.5, -2.0, -3.0, -4.0, -6.0], dtype=jnp.float32)

        def dequant_nvfp4(W_packed, scales, block=BLOCK_SIZE):
            N = W_packed.shape[0]
            low = W_packed & 15
            high = W_packed >> 4 & 15
            idx = jnp.stack([low, high], axis=-1).reshape(N, -1)
            vals = NVFP4_LUT[idx]
            K = vals.shape[1]
            vals = vals.reshape(N, K // block, block) * scales[:, :, None]
            return vals.reshape(N, K)
        key = jax.random.key(seed)
        ks = jax.random.split(key, 7)
        x = jax.random.normal(ks[0], (4, 32, HIDDEN_SIZE), dtype=jnp.float32)
        gate_W_packed = jax.random.randint(ks[1], (MLP_DIM, HIDDEN_SIZE // 2), 0, 32, dtype=jnp.int32)
        gate_scales = jax.random.uniform(ks[2], (MLP_DIM, HIDDEN_SIZE // BLOCK_SIZE), dtype=jnp.float32) * 0.1 + 0.001
        up_W_packed = jax.random.randint(ks[3], (MLP_DIM, HIDDEN_SIZE // 2), 0, 32, dtype=jnp.int32)
        up_scales = jax.random.uniform(ks[4], (MLP_DIM, HIDDEN_SIZE // BLOCK_SIZE), dtype=jnp.float32) * 0.1 + 0.001
        down_W_packed = jax.random.randint(ks[5], (HIDDEN_SIZE, MLP_DIM // 2), 0, 32, dtype=jnp.int32)
        down_scales = jax.random.uniform(ks[6], (HIDDEN_SIZE, MLP_DIM // BLOCK_SIZE), dtype=jnp.float32) * 0.1 + 0.001
        return {'x': x, 'gate_W_packed': gate_W_packed, 'gate_scales': gate_scales, 'up_W_packed': up_W_packed, 'up_scales': up_scales, 'down_W_packed': down_W_packed, 'down_scales': down_scales}
    _L0_ffn_in = _L0_ffn_setup()
    _d = {'L0_attn_u': _L0_attn_in['u'], 'L0_attn_in_proj_w': _L0_attn_in['in_proj_w'], 'L0_attn_conv_w': _L0_attn_in['conv_w'], 'L0_attn_conv_b': _L0_attn_in['conv_b'], 'L0_attn_dt_bias': _L0_attn_in['dt_bias'], 'L0_attn_A_log': _L0_attn_in['A_log'], 'L0_attn_D_skip': _L0_attn_in['D_skip'], 'L0_attn_norm_w': _L0_attn_in['norm_w'], 'L0_attn_out_proj_w': _L0_attn_in['out_proj_w'], 'L0_ffn_gate_W_packed': _L0_ffn_in['gate_W_packed'], 'L0_ffn_gate_scales': _L0_ffn_in['gate_scales'], 'L0_ffn_up_W_packed': _L0_ffn_in['up_W_packed'], 'L0_ffn_up_scales': _L0_ffn_in['up_scales'], 'L0_ffn_down_W_packed': _L0_ffn_in['down_W_packed'], 'L0_ffn_down_scales': _L0_ffn_in['down_scales']}
    _x0 = _d['L0_attn_u']
    _d['L0_attn_u'] = jax.random.normal(jax.random.fold_in(jax.random.key(seed), 1), (1, 1024, 256), dtype=_x0.dtype)
    del _x0
    return _d

def reference(L0_attn_u, L0_attn_in_proj_w, L0_attn_conv_w, L0_attn_conv_b, L0_attn_dt_bias, L0_attn_A_log, L0_attn_D_skip, L0_attn_norm_w, L0_attn_out_proj_w, L0_ffn_gate_W_packed, L0_ffn_gate_scales, L0_ffn_up_W_packed, L0_ffn_up_scales, L0_ffn_down_W_packed, L0_ffn_down_scales):

    def _L0_attn_ref(u, in_proj_w, conv_w, conv_b, dt_bias, A_log, D_skip, norm_w, out_proj_w):
        import jax, jax.numpy as jnp
        import numpy as np
        D_MODEL = 256
        D_STATE = 128
        D_CONV = 4
        EXPAND = 2
        HEADDIM = 64
        NGROUPS = 1
        CHUNK = 32
        D_INNER = EXPAND * D_MODEL
        NHEADS = D_INNER // HEADDIM
        HG = NHEADS // NGROUPS
        CONV_DIM = D_INNER + 2 * NGROUPS * D_STATE
        D_IN_PROJ = 2 * D_INNER + 2 * NGROUPS * D_STATE + NHEADS
        BATCH = 2
        SEQLEN = 256
        EPS = 1e-05

        def _mamba2(u, in_proj_w, conv_w, conv_b, dt_bias, A_log, D_skip, norm_w, out_proj_w):
            b, l, _ = u.shape
            nc = l // CHUNK
            zxbcdt = u @ in_proj_w.T
            z = zxbcdt[..., :D_INNER]
            xBC = zxbcdt[..., D_INNER:D_INNER + CONV_DIM]
            dt = jax.nn.softplus(zxbcdt[..., D_INNER + CONV_DIM:] + dt_bias)
            xp = jnp.pad(xBC, ((0, 0), (D_CONV - 1, 0), (0, 0)))
            conv = conv_b + sum((conv_w[:, k] * xp[:, k:k + l, :] for k in range(D_CONV)))
            xBC = jax.nn.silu(conv)
            x = xBC[..., :D_INNER].reshape(b, l, NHEADS, HEADDIM)
            Bm = xBC[..., D_INNER:D_INNER + NGROUPS * D_STATE].reshape(b, l, NGROUPS, D_STATE)
            Cm = xBC[..., D_INNER + NGROUPS * D_STATE:].reshape(b, l, NGROUPS, D_STATE)
            A = -jnp.exp(A_log)
            xc = x.reshape(b, nc, CHUNK, NGROUPS, HG, HEADDIM)
            dtc = dt.reshape(b, nc, CHUNK, NGROUPS, HG)
            Bc = Bm.reshape(b, nc, CHUNK, NGROUPS, D_STATE)
            Cc = Cm.reshape(b, nc, CHUNK, NGROUPS, D_STATE)
            dA = jnp.transpose(dtc * A.reshape(NGROUPS, HG), (0, 3, 4, 1, 2))
            dA_cs = jnp.cumsum(dA, axis=-1)
            seg = dA_cs[..., :, None] - dA_cs[..., None, :]
            tri = jnp.tril(jnp.ones((CHUNK, CHUNK), bool))
            Lmat = jnp.where(tri, jnp.exp(seg), 0.0)
            xdt = xc * dtc[..., None]
            CB = jnp.einsum('bclgn,bcsgn->bcgls', Cc, Bc)
            Y_diag = jnp.einsum('bcgls,bgHcls,bcsgHp->bclgHp', CB, Lmat, xdt)
            decay_states = jnp.exp(dA_cs[..., -1:] - dA_cs)
            states = jnp.einsum('bcsgn,bgHcs,bcsgHp->bcgHpn', Bc, decay_states, xdt)
            chunk_decay = jnp.exp(dA_cs[..., -1])

            def step(carry, inp):
                st, dec = inp
                return (carry * dec[..., None, None] + st, carry)
            _, prev = jax.lax.scan(step, jnp.zeros_like(states[:, 0]), (jnp.moveaxis(states, 1, 0), jnp.moveaxis(chunk_decay, -1, 0)))
            prev = jnp.moveaxis(prev, 0, 1)
            Y_off = jnp.einsum('bclgn,bcgHpn,bgHcl->bclgHp', Cc, prev, jnp.exp(dA_cs))
            y = (Y_diag + Y_off).reshape(b, l, NHEADS, HEADDIM) + x * D_skip[None, None, :, None]
            y = y.reshape(b, l, D_INNER)
            y = y * jax.nn.silu(z)
            yg = y.reshape(b, l, NGROUPS, D_INNER // NGROUPS)
            yg = yg * jax.lax.rsqrt(jnp.mean(yg * yg, axis=-1, keepdims=True) + EPS)
            y = yg.reshape(b, l, D_INNER) * norm_w
            return y @ out_proj_w.T
        return _mamba2(u, in_proj_w, conv_w, conv_b, dt_bias, A_log, D_skip, norm_w, out_proj_w)

    def _L0_ffn_ref(x, gate_W_packed, gate_scales, up_W_packed, up_scales, down_W_packed, down_scales):
        import jax, jax.numpy as jnp
        import numpy as np
        BLOCK_SIZE = 32
        HIDDEN_SIZE = 256
        MLP_DIM = 2048
        NVFP4_LUT = jnp.array([0.0, 0.5, 1.0, 1.5, 2.0, 3.0, 4.0, 6.0, 0.0, -0.5, -1.0, -1.5, -2.0, -3.0, -4.0, -6.0], dtype=jnp.float32)

        def dequant_nvfp4(W_packed, scales, block=BLOCK_SIZE):
            N = W_packed.shape[0]
            low = W_packed & 15
            high = W_packed >> 4 & 15
            idx = jnp.stack([low, high], axis=-1).reshape(N, -1)
            vals = NVFP4_LUT[idx]
            K = vals.shape[1]
            vals = vals.reshape(N, K // block, block) * scales[:, :, None]
            return vals.reshape(N, K)
        B, S, H = x.shape
        xt = x.reshape(B * S, H)
        Wg = dequant_nvfp4(gate_W_packed, gate_scales)
        Wu = dequant_nvfp4(up_W_packed, up_scales)
        Wd = dequant_nvfp4(down_W_packed, down_scales)
        gate = jnp.einsum('th,nh->tn', xt, Wg)
        up = jnp.einsum('th,nh->tn', xt, Wu)
        gelu = jnp.tanh(0.7978845608028654 * (gate + 0.044715 * gate ** 3)) * gate * 0.5 + gate * 0.5
        inter = gelu * up
        out = jnp.einsum('tn,hn->th', inter, Wd)
        return out.reshape(B, S, H)
    x = L0_attn_u
    x = x + 0.5 * _L0_ffn_ref(_layernorm(x, axis=-1), L0_ffn_gate_W_packed, L0_ffn_gate_scales, L0_ffn_up_W_packed, L0_ffn_up_scales, L0_ffn_down_W_packed, L0_ffn_down_scales)
    x = x + _L0_attn_ref(_layernorm(x, axis=-1), L0_attn_in_proj_w, L0_attn_conv_w, L0_attn_conv_b, L0_attn_dt_bias, L0_attn_A_log, L0_attn_D_skip, L0_attn_norm_w, L0_attn_out_proj_w)
    x = x + 0.5 * _L0_ffn_ref(_layernorm(x, axis=-1), L0_ffn_gate_W_packed, L0_ffn_gate_scales, L0_ffn_up_W_packed, L0_ffn_up_scales, L0_ffn_down_W_packed, L0_ffn_down_scales)
    return x

_drawn_inputs = setup_inputs


def setup_inputs(seed=0):
    import zlib

    import numpy as np

    out = dict(_drawn_inputs(seed))
    spreads = {'L0_attn_D_skip': (1.0, 0.6), 'L0_attn_norm_w': (1.0, 0.2)}
    factors = {'L0_attn_conv_b': 2.766}
    for name, (base, spread) in spreads.items():
        noise = np.random.default_rng([zlib.crc32(name.encode()), seed]).standard_normal(out[name].shape)
        drawn = base * np.exp(spread * noise) if base else spread * noise
        out[name] = jnp.asarray(drawn.astype(out[name].dtype))
    for name, factor in factors.items():
        out[name] = (out[name] * factor).astype(out[name].dtype)
    return out
```

```python
from contextlib import ExitStack

import numpy as np

import concourse.bass as bass
from concourse import mybir

P = 128
SEQ = 1024
D = 256
TILE = 256
TT = TILE // P
NT = SEQ // TILE
MLP = 2048
UNITS = MLP // P
CH = UNITS // 2
WCOL = 256
DI = 512
NH = 8
HD = DI // NH
CT = 6
TAPS = 4
NPROJ = 2 * DI + 2 * P + NH
EPS = 1e-5

F32 = mybir.dt.float32
F16 = mybir.dt.float16
I32 = mybir.dt.int32
U32 = mybir.dt.uint32
ALU = mybir.AluOpType
ACT = mybir.ActivationFunctionType
AX = mybir.AxisListType

ACTIVATION_BITS = 10
FFN_BITS = 12
PROJ_BITS = 14
HIDDEN_BITS = -8
SMALLEST = 2.0 ** -30
CODE_BITS = 14
LOG_TERMS = 6
DECAY_FLOOR = -60000.0

UNIT_BANK = [n % 3 for n in range(UNITS - 1)] + [1]
LAST_IN_BANK = [max(n for n in range(UNITS) if UNIT_BANK[n] == b) - UNITS for b in range(3)]


def before_in_bank(n):
    earlier = [u for u in range(n) if UNIT_BANK[u] == UNIT_BANK[n]]
    return earlier[-1] if earlier else LAST_IN_BANK[UNIT_BANK[n]]


DOWN_LAG = 3
RING = 4

A, M, B = "a", "m", "b"


class Order:

    def __init__(self, names):
        self.names = names.split()
        assert len(set(self.names)) == len(self.names)

    def after(self, name, tile):
        return tile * len(self.names) + self.names.index(name) + 1

    def all(self, tiles):
        return tiles * len(self.names)


PE_M = Order("xc0 xc1 xc2 dt z0 z1 "
             "cum0 cb0 xt0 seg0a seg0b off0 diag0 state0 "
             "cum1 cb1 xt1 seg1a seg1b off1 diag1 state1 yt0 out0 yt1 out1")
ACT_M = Order("xc0 xc1 xc2 th0 spe th1 zt0 zh0 zt1 zh1 th2 "
              "ex0 bt0 xt0 La0 Lb0 ex1 bt1 sq0 xt1 La1 Lb1 yh0 sq1 yh1")
DVE_M = Order(" ".join([f"cv0_{k}" for k in range(8)] + [f"cv1_{k}" for k in range(8)]
                       + ["v", "na"] + [f"cv2_{k}" for k in range(8)] + ["halo", "xs0"]
                       + ["e2", "er", "r", "r2"] + [f"q{k}" for k in range(LOG_TERMS)]
                       + ["l", "mv", "dt", "dA", "dh", "dl", "xs1", "zg0", "zg1", "xs2",
                          "cb0", "xd0", "off0", "y0", "st0", "cb1", "xd1", "off1", "y1", "st1",
                          "yl0", "out0", "yl1", "out1"]))
POOL_M = Order("hand Rh0 Rl0 xD0 xe0 M0 sd0 yx0 yz0 Rh1 Rl1 ve0 rs0 yn0 xD1 xe1 M1 sd1 yx1 yz1 "
               "ve1 rs1 yn1")
DVE_LN = Order("stats0 stats1 aggr0 aggr1 xn0 xn1 lo")
POOL_LN = Order("ve rstd")

SLOTS = 32
PE_AT = {0: "xc0", 1: "xc1", 2: "xc2", 3: "dt", 4: "z0", 5: "z1", 8: "cum0 cb0", 9: "xt0",
         10: "seg0a", 11: "seg0b", 12: "off0", 13: "diag0", 14: "state0", 15: "cum1 cb1",
         17: "xt1", 18: "seg1a", 19: "seg1b", 20: "off1", 21: "diag1", 22: "state1", 23: "yt0",
         24: "out0", 27: "yt1", 29: "out1"}
ACT_AT = {0: "xc0", 1: "xc1", 2: "xc2 th0", 4: "spe th1 zt0 zh0", 5: "zt1 zh1", 6: "th2",
          8: "ex0 bt0", 9: "xt0", 10: "La0", 11: "Lb0", 15: "ex1 bt1", 17: "sq0 xt1", 18: "La1",
          19: "Lb1", 23: "yh0", 25: "sq1", 27: "yh1"}
DVE_AT = {1: "cv0", 2: "cv1", 3: "v na", 4: "cv2 halo xs0", 5: "soft", 6: "xs1 zg0", 7: "zg1 xs2",
          8: "cb0", 10: "xd0", 12: "off0", 13: "y0", 14: "st0", 15: "cb1", 18: "xd1", 20: "off1",
          21: "y1", 22: "st1", 23: "yl0", 24: "out0", 28: "yl1", 29: "out1"}
POOL_AT = {0: "hand", 6: "Rh0 Rl0", 10: "xD0 xe0", 11: "M0", 13: "sd0", 14: "yx0 yz0",
           15: "Rh1 Rl1", 18: "ve0 rs0 yn0 xD1 xe1", 19: "M1", 21: "sd1", 22: "yx1 yz1",
           25: "ve1 rs1 yn1"}
LN_B_AT, LN_M_AT, LN_A_AT = 3, 24, 27


class Step:

    def __init__(self, i, a, m, b, stretch=False):
        self.i = i
        self.a = i if a else None
        self.m = i - 1 if m else None
        self.b = i - 2 if b else None
        self.units = []
        if a:
            pass_a = i if not b else 2 * i - 2
            last = 22 if stretch else UNITS - 1
            self.units += [(n * last // (UNITS - 1), A, pass_a, n) for n in range(UNITS)]
        if b:
            pass_b = 2 * i - 1 if a else i + 2
            first, last = (6, SLOTS - 1) if stretch else (SLOTS - UNITS, SLOTS - 1)
            if not a and not m:
                first, last = 6, 6 + UNITS - 1
            self.units += [(first + n * (last - first) // (UNITS - 1), B, pass_b, n)
                           for n in range(UNITS)]
        self.next_a = True if a and (not isinstance(i, int) or i < NT - 1) else False

    def unit_at(self, slot):
        found = [q for q, u in enumerate(self.units) if u[0] == slot]
        return found[0] if found else None

    def a_ends_at(self):
        if self.a is None:
            return None
        slot = self.units[UNITS - 1][0] + DOWN_LAG + 1
        return slot


def steps(engine, body):
    body(Step(0, True, False, False))
    body(Step(1, True, True, False, stretch=True))
    with engine.Fori(2, NT) as i:
        body(Step(i, True, True, True))
    body(Step(NT, False, True, True, stretch=True))
    body(Step(NT + 1, False, False, True))


def macaron(nc, x, packed, scales, w_in, conv_w, conv_b, dt_bias, A_log, D_skip, norm_w, w_out,
            consts, out):
    with ExitStack() as ctx:
        def sb(name, shape, dt=F32):
            return ctx.enter_context(nc.sbuf_tensor(name, shape, dt))

        def sem(name):
            return ctx.enter_context(nc.semaphore(name))

        gate_up = [ctx.enter_context(nc.psum_tensor(f"gate_up{b}", [P, 2, TILE], F32)) for b in range(3)]
        down = ctx.enter_context(nc.psum_tensor("down", [P, TT, D], F32))
        R = [ctx.enter_context(nc.psum_tensor(f"mixed{b}", [P, 512], F32)) for b in range(4)]

        cst = sb("cst", [P, 4, P])
        ident, incl, later, ones = (cst[:, n, :] for n in range(4))
        incl16 = sb("incl16", [P, P], F16)
        later16 = sb("later16", [P, P], F16)
        half = sb("half", [P, 1])
        spare_dve, spare_pool = sb("spare_dve", [P, 64]), sb("spare_pool", [P, 64])
        spare_cells = iter(range(64))
        pk = sb("pk", [P, 2, 3 * WCOL], U32)
        sc = sb("sc", [P, 2, 3 * WCOL])
        t0 = sb("t0", [P, 3 * WCOL], U32)
        t1 = sb("t1", [P, 3 * WCOL], U32)
        codes = sb("codes", [P, 3 * WCOL], U32)
        wfull = sb("wfull", [P, 2, 3 * WCOL * 2])
        whi = sb("whi", [P, CH, 3, 2, WCOL], F16)
        wlo = sb("wlo", [P, CH, 3, 2, WCOL], F16)
        sflat = sb("sflat", [P, 3 * P])
        mx = sb("mx", [P, 4])
        mrow = sb("mrow", [4, 4])
        mdiag = sb("mdiag", [4, 4])
        pw = sb("pw", [P, 16])
        early = sb("early", [P, 2 * NPROJ])
        win = early[:, :].rearrange("p (k n) -> p k n", k=2)
        win_hi = sb("win_hi", [P, 2, NPROJ], F16)
        win_lo = sb("win_lo", [P, 2, NPROJ], F16)
        early2 = sb("early2", [P, 4 * D])
        wout = early2[:, :].rearrange("p (k n) -> p k n", k=4)
        wout_hi = sb("wout_hi", [P, 4, D], F16)
        wout_lo = sb("wout_lo", [P, 4, D], F16)
        cw = sb("cw", [P, CT, TAPS])
        cb = sb("cb", [P, CT])
        nw = sb("nw", [P, 4])
        dtb = sb("dtb", [P, TT, NH])
        negA = sb("negA", [P, TT, NH])
        dsk = sb("dsk", [P, NH])

        x_in = sb("x_in", [P, TT, D])
        x_a = sb("x_a", [P, TT, D])
        x_1 = sb("x_1", [P, TT, D])
        x_m = sb("x_m", [P, TT, D])
        x_2 = sb("x_2", [P, TT, D])
        x_b = sb("x_b", [P, TT, D])
        x_o = sb("x_o", [P, TT, D])
        ln_src = {A: x_in, M: x_1, B: x_2}
        stats = {s: sb(f"stats_{s}", [P, TT, 6]) for s in (A, M, B)}
        aggr = {s: sb(f"aggr_{s}", [P, TT, 2]) for s in (A, M, B)}
        ve = {s: sb(f"ve_{s}", [P, TT]) for s in (A, M, B)}
        rstd = {s: sb(f"rstd_{s}", [P, TT]) for s in (A, M, B)}
        xn = {s: sb(f"xn_{s}", [P, TT, D]) for s in (A, M, B)}
        xT_hi = {s: sb(f"xT_hi_{s}", [P, 2, TILE], F16) for s in (A, M, B)}
        xT_lo = {s: sb(f"xT_lo_{s}", [P, 2, TILE], F16) for s in (A, M, B)}

        gelu = [sb(f"gelu{b}", [P, TILE]) for b in range(3)]
        hidden = [sb(f"hidden{b}", [P, TILE]) for b in range(3)]
        hid_hi = sb("hid_hi", [P, RING, TILE], F16)
        hid_lo = sb("hid_lo", [P, RING, TILE], F16)

        HALO = TAPS - 1
        xc = sb("xc", [P, CT, HALO + TILE])
        cv = sb("cv", [P, CT, TILE])
        th = sb("th", [P, CT, TILE])
        xs = th
        BT, CTr = xs[:, 0, :], xs[:, 1, :]
        zt = sb("zt", [P, TT, DI])
        zh = sb("zh", [P, TT, DI])
        zg = zt
        sp = {n: sb(f"sp_{n}", [P, TT * NH]) for n in "v na e e2 er r r2 l mv dt dA".split()}
        spq = [sb(f"sp_q{k}", [P, TT * NH]) for k in range(LOG_TERMS)]
        dh = sb("dh", [P, TT * NH], F16)
        dl = sb("dl", [P, TT * NH], F16)
        Rh = sb("Rh", [P, NH, P], F16)
        Rl = sb("Rl", [P, NH, P], F16)
        ex = sb("ex", [P, TT, 3, NH])
        L = early[:, 0:NH * P].rearrange("p (h l) -> p h l", h=NH)
        cbm = sb("cbm", [P, P])
        Mm = early[:, NH * P:2 * NH * P].rearrange("p (h l) -> p h l", h=NH)
        Bs = sb("Bs", [P, P])
        xt = sb("xt", [P, DI])
        xd = sb("xd", [P, DI])
        xe = sb("xe", [P, DI])
        xD = sb("xD", [P, TT, DI])
        state = sb("state", [P, DI])
        yo = sb("yo", [P, DI])
        y = early2[:, :].rearrange("p (t d) -> p t d", t=TT)
        ysq = sb("ysq", [P, DI])
        yss = sb("yss", [P, TT])
        yve = sb("yve", [P, TT])
        yrs = sb("yrs", [P, TT])
        yn = sb("yn", [P, TT, DI])
        yT_hi = sb("yT_hi", [P, 4, P], F16)
        yT_lo = sb("yT_lo", [P, 4, P], F16)

        s_sflat, s_cst, s_small, s_win, s_wout = map(sem, "sflat_in cst_in small_in win_in wout_in".split())
        s_chunk = [sem("chunk_in0"), sem("chunk_in1")]
        s_x, s_out = sem("x_in_loaded"), sem("out_stored")
        set_dve, set_pe, set_act, set_pool = map(sem, "setup_dve setup_pe setup_act setup_pool".split())
        s_decoded, s_full, s_whi, s_wlo = map(sem, "codes_ready wfull_ready whi_ready wlo_ready".split())
        s_step = sem("decode_step")
        gu_done, gelu_done, hidden_done, hi_done, lo_done, down_done, pass_read = map(
            sem, "gate_up_done gelu_done hidden_done hidden_hi_done hidden_lo_done down_done pass_read".split())
        m_pe, m_act, m_dve, m_pool = map(sem, "mamba_pe mamba_act mamba_dve mamba_pool".split())
        ln_dve = {s: sem(f"ln_dve_{s}") for s in (A, M, B)}
        ln_pool = {s: sem(f"ln_pool_{s}") for s in (A, M, B)}
        ln_pe = {s: sem(f"ln_pe_{s}") for s in (A, M, B)}
        ln_act = {s: sem(f"ln_act_{s}") for s in (A, M, B)}
        kept_a, kept_b = sem("x_a_kept"), sem("x_b_kept")

        m_ffn, m_in, m_out = (pw[:, n:n + 1] for n in range(3))
        r_ffn, r_in, r_out = (pw[:, 3 + n:4 + n] for n in range(3))
        f_code = pw[:, 6:7]
        c_gate = pw[:, 7:8]
        c_up = pw[:, 8:9]
        c_down = pw[:, 9:10]
        c_in = pw[:, 10:11]
        c_in_half = pw[:, 11:12]
        c_out = pw[:, 12:13]
        f_in = pw[:, 13:14]
        f_out = pw[:, 14:15]
        m_cube = pw[:, 15:16]

        x_t = x.rearrange("o (n t p) d -> (o n) p t d", p=P, t=TT)
        out_t = out.rearrange("o (n t p) d -> (o n) p t d", p=P, t=TT)

        def unit_sum(f, n):
            return f * UNITS + n + 1

        block = ctx.enter_context(nc.Block())

        @block.sync
        def _(sp_):
            sp_.dma_start(sflat[:], scales.rearrange("b c m n -> (b c m n)").rearrange("(p f) -> p f", p=P)).then_inc(s_sflat, 16)
            sp_.dma_start(cst[:], consts).then_inc(s_cst, 16)

            def chunk(c):
                if c >= 2:
                    sp_.wait_ge(s_full, c - 1)
                sp_.dma_start(pk[:, c % 2, :].bitcast(I32), packed[:, c]).then_inc(s_chunk[c % 2], 16)
                for b in range(8):
                    sp_.dma_start(sc[16 * b:16 * b + 16, c % 2, :],
                                  scales[b, c].rearrange("m n -> (m n)").partition_broadcast(16)
                                  ).then_inc(s_chunk[c % 2], 16)

            sp_.dma_start(x_in[:], x_t[0]).then_inc(s_x, 16)
            chunk(0)
            sp_.dma_start(cw[:], conv_w).then_inc(s_small, 16)
            sp_.dma_start(cb[:], conv_b).then_inc(s_small, 16)
            sp_.dma_start(nw[:], norm_w).then_inc(s_small, 16)
            for t in range(TT):
                sp_.dma_start(dtb[:, t, :], dt_bias.partition_broadcast(P)).then_inc(s_small, 16)
                sp_.dma_start(negA[:, t, :], A_log.partition_broadcast(P)).then_inc(s_small, 16)
            sp_.dma_start(dsk[:], D_skip.partition_broadcast(P)).then_inc(s_small, 16)
            chunk(1)
            sp_.dma_start(win, w_in).then_inc(s_win, 16)
            sp_.dma_start(wout, w_out).then_inc(s_wout, 16)
            for c in range(2, CH):
                chunk(c)

            def step(st):
                if st.next_a:
                    sp_.wait_ge(kept_a, st.i + 1)
                    sp_.dma_start(x_in[:], x_t[st.i + 1] if isinstance(st.i, int) else
                                  x_t[bass.ds((st.i + 1) % NT, 1)].rearrange("o p t d -> p (o t) d")).then_inc(s_x, 16)
                if st.b is not None:
                    sp_.wait_ge(pass_read, st.units[-1][2] + 1)
                    sp_.dma_start(out_t[st.b] if isinstance(st.b, int) else
                                  out_t[bass.ds(st.b, 1)].rearrange("o p t d -> p (o t) d"), x_o[:]).then_inc(s_out, 16)

            steps(sp_, step)
            sp_.wait_ge(s_out, 16 * NT)

        @block.tensor
        def _(pe):
            def layer_norm_transpose(s, tile, bank_free):
                pe.wait_ge(ln_dve[s], DVE_LN.after("xn1", tile))
                for sm, value in bank_free:
                    pe.wait_ge(sm, value)
                for t in range(TT):
                    for kk in range(2):
                        mm = nc.tensor.transpose(R[3][:, kk * TILE + t * P:kk * TILE + (t + 1) * P],
                                                 xn[s][:, t, kk::2], ident)
                mm.then_inc(ln_pe[s], 1)

            def gate_up_unit(s, tile, f, n):
                first = isinstance(f, int) and f == 0
                if n == 0:
                    pe.wait_ge(ln_dve[s], DVE_LN.after("lo", tile))
                prev = before_in_bank(n)
                if not (first and prev < 0):
                    pe.wait_ge(hidden_done, unit_sum(f, prev))
                if first and n % 2 == 0:
                    pe.wait_ge(s_wlo, n // 2 + 1)
                c, e = n // 2, n % 2
                for mat in range(2):
                    o = gate_up[UNIT_BANK[n]][:, mat, :]
                    for kk in range(2):
                        hi = whi[:, c, mat, kk, e * P:(e + 1) * P]
                        lo = wlo[:, c, mat, kk, e * P:(e + 1) * P]
                        nc.tensor.matmul(o, hi, xT_hi[s][:, kk, :], start=(kk == 0), stop=False)
                        nc.tensor.matmul(o, hi, xT_lo[s][:, kk, :], start=False, stop=False)
                        mm = nc.tensor.matmul(o, lo, xT_hi[s][:, kk, :], start=False, stop=(kk == 1))
                mm.then_inc(gu_done, 1)

            def down_unit(f, n):
                first = isinstance(f, int) and f == 0
                pe.wait_ge(lo_done, unit_sum(f, n))
                if n == 0 and not first:
                    pe.wait_ge(pass_read, f)
                c, e = n // 2, n % 2
                for t in range(TT):
                    hi = hid_hi[:, n % RING, t * P:(t + 1) * P]
                    lo = hid_lo[:, n % RING, t * P:(t + 1) * P]
                    o = down[:, t, :]
                    nc.tensor.matmul(o, hi, whi[:, c, 2, e, :], start=(n == 0 and t == 0), stop=False,
                                     skip_group_check=True)
                    nc.tensor.matmul(o, hi, wlo[:, c, 2, e, :], start=False, stop=False, skip_group_check=True)
                    mm = nc.tensor.matmul(o, lo, whi[:, c, 2, e, :], start=False,
                                          stop=(n == UNITS - 1), skip_group_check=True)
                mm.then_inc(down_done, 1)

            def three(o, lhs, rhs, start, stop):
                nc.tensor.matmul(o, lhs[0], rhs[0], start=start, stop=False)
                nc.tensor.matmul(o, lhs[0], rhs[1], start=False, stop=False)
                return nc.tensor.matmul(o, lhs[1], rhs[0], start=False, stop=stop)

            def mamba(name, j, st):
                inc = lambda mm: mm.then_inc(m_pe, 1)
                if name.startswith("xc"):
                    p = int(name[2])
                    bank = R[p % 2]
                    if p == 0:
                        pe.wait_ge(ln_dve[M], DVE_LN.after("lo", j))
                        if isinstance(j, int) and j == 0:
                            pe.wait_ge(set_act, 3)
                            pe.wait_ge(set_dve, SET_DVE_END)
                        else:
                            pe.wait_ge(m_act, ACT_M.after("yh1", j - 1))
                            pe.wait_ge(m_dve, DVE_M.after("yl1", j - 1))
                    if p == 1 and not (isinstance(j, int) and j == 0):
                        pe.wait_ge(m_dve, DVE_M.after("out1", j - 1))
                    if p == 2:
                        pe.wait_ge(m_act, ACT_M.after("xc0", j))
                    for c in range(2):
                        ct = (4 + c) if p == 0 else 2 * (p - 1) + c
                        cols = slice(DI + ct * P, DI + (ct + 1) * P)
                        for kk in range(2):
                            mm = three(bank[:, c * TILE:(c + 1) * TILE],
                                       (win_hi[:, kk, cols], win_lo[:, kk, cols]),
                                       (xT_hi[M][:, kk, :], xT_lo[M][:, kk, :]), kk == 0, kk == 1)
                    inc(mm)
                elif name == "dt":
                    if not (isinstance(j, int) and j == 0):
                        pe.wait_ge(m_dve, DVE_M.after("yl0", j - 1))
                    cols = slice(DI + CT * P, NPROJ)
                    for t in range(TT):
                        for kk in range(2):
                            tok = slice(t * P, (t + 1) * P)
                            mm = three(R[2][:, t * NH:(t + 1) * NH],
                                       (xT_hi[M][:, kk, tok], xT_lo[M][:, kk, tok]),
                                       (win_hi[:, kk, cols], win_lo[:, kk, cols]), kk == 0, kk == 1)
                    inc(mm)
                elif name in ("z0", "z1"):
                    t = int(name[1])
                    pe.wait_ge(m_act, ACT_M.after("xc1" if t == 0 else "xc2", j))
                    tok = slice(t * P, (t + 1) * P)
                    for kk in range(2):
                        mm = three(R[1 - t][:, :], (xT_hi[M][:, kk, tok], xT_lo[M][:, kk, tok]),
                                   (win_hi[:, kk, 0:DI], win_lo[:, kk, 0:DI]), kk == 0, kk == 1)
                    inc(mm)
                elif name.startswith("cum"):
                    q = int(name[3])
                    pe.wait_ge(m_dve, DVE_M.after("dA", j))
                    if q == 1:
                        pe.wait_ge(m_act, ACT_M.after("Lb0", j))
                    dA = sp["dA"][:, q * NH:(q + 1) * NH]
                    for n, mat in enumerate((incl, ones, later)):
                        nc.tensor.matmul(R[2][:, n * NH:(n + 1) * NH], mat, dA, start=True, stop=True)
                    inc(nc.tensor.transpose(R[2][:, P:2 * P], BT[:, q * P:(q + 1) * P], ident))
                elif name.startswith("cb"):
                    q = int(name[2])
                    if q == 0:
                        if st.b is not None:
                            pe.wait_ge(ln_dve[B], DVE_LN.after("lo", st.b))
                        if isinstance(st.a, int) and st.a < NT or st.a is not None:
                            pe.wait_ge(ln_dve[A], DVE_LN.after("lo", st.a))
                        pe.wait_ge(ln_dve[M], DVE_LN.after("lo", j))
                    else:
                        pe.wait_ge(m_dve, DVE_M.after("off0", j))
                    tok = slice(q * P, (q + 1) * P)
                    inc(nc.tensor.matmul(R[3][:, 0:P], BT[:, tok], CTr[:, tok], start=True, stop=True))
                elif name.startswith("xt"):
                    q = int(name[2])
                    pe.wait_ge(m_dve, DVE_M.after("xs2" if q == 0 else "y0", j))
                    pe.wait_ge(m_act, ACT_M.after("zh0", j))
                    for c in range(4):
                        mm = nc.tensor.transpose(R[1][:, c * P:(c + 1) * P],
                                                 xs[:, 2 + c, q * P:(q + 1) * P], ident)
                    inc(mm)
                elif name.startswith("seg"):
                    q, ab = int(name[3]), name[4]
                    g = 0 if ab == "a" else 1
                    pe.wait_ge(m_pool, POOL_M.after(f"Rl{q}", j))
                    if ab == "a":
                        if q == 0:
                            pe.wait_ge(m_act, ACT_M.after("zh1", j))
                        else:
                            pe.wait_ge(m_dve, DVE_M.after("st0", j))
                    else:
                        pe.wait_ge(m_act, ACT_M.after(f"bt{q}", j))
                    o = R[0 if ab == "a" else 2][:, :].rearrange("p (h l) -> p h l", h=4)
                    nc.tensor.matmul(o, later16[:], Rh[:, 4 * g:4 * g + 4, :], start=True, stop=False)
                    inc(nc.tensor.matmul(o, later16[:], Rl[:, 4 * g:4 * g + 4, :], start=False, stop=True))
                elif name.startswith("off"):
                    q = int(name[3])
                    pe.wait_ge(m_dve, DVE_M.after(f"cb{q}", j))
                    if q == 1:
                        pe.wait_ge(m_dve, DVE_M.after("st0", j))
                    elif isinstance(j, int) and j == 0:
                        pe.wait_ge(set_pool, 1)
                    else:
                        pe.wait_ge(m_dve, DVE_M.after("st1", j - 1))
                    inc(nc.tensor.matmul(R[3][:, :], CTr[:, q * P:(q + 1) * P], state[:], start=True, stop=True))
                elif name.startswith("diag"):
                    q = int(name[4])
                    pe.wait_ge(m_pool, POOL_M.after(f"M{q}", j))
                    pe.wait_ge(m_dve, DVE_M.after(f"xd{q}", j))
                    for h in range(NH):
                        mm = nc.tensor.matmul(R[1][:, h * HD:(h + 1) * HD], Mm[:, h, :],
                                              xd[:, h * HD:(h + 1) * HD], start=True, stop=True)
                    inc(mm)
                elif name.startswith("state"):
                    q = int(name[5])
                    pe.wait_ge(m_pool, POOL_M.after(f"xe{q}", j))
                    pe.wait_ge(m_act, ACT_M.after(f"La{q}", j))
                    inc(nc.tensor.matmul(R[0][:, :], Bs[:], xe[:], start=True, stop=True))
                elif name.startswith("yt"):
                    q = int(name[2])
                    bank = R[2] if q == 0 else R[0]
                    pe.wait_ge(m_pool, POOL_M.after(f"yn{q}", j))
                    if q == 0:
                        pe.wait_ge(m_act, ACT_M.after("Lb1", j))
                    else:
                        pe.wait_ge(m_dve, DVE_M.after("st1", j))
                    for c in range(4):
                        mm = nc.tensor.transpose(bank[:, c * P:(c + 1) * P], yn[:, q, c * P:(c + 1) * P], ident)
                    inc(mm)
                elif name.startswith("out"):
                    q = int(name[3])
                    pe.wait_ge(m_dve, DVE_M.after(f"yl{q}", j))
                    pe.wait_ge(m_dve, DVE_M.after("y1" if q == 0 else "out0", j))
                    for c in range(4):
                        mm = three(R[1][:, 0:D], (yT_hi[:, c, :], yT_lo[:, c, :]),
                                   (wout_hi[:, c, :], wout_lo[:, c, :]), c == 0, c == 3)
                    inc(mm)

            pe.wait_ge(s_cst, 16)
            for g in range(2):
                pe.wait_ge(set_dve, SET_DVE_MAX[g])
                w = 1 if g == 0 else 2
                nc.tensor.transpose(R[0][0:w, 0:P], mx[:, g:g + w], ident).then_inc(set_pe, 1)
                pe.wait_ge(set_dve, SET_DVE_DIAG[g])
                nc.tensor.matmul(R[0][:, 256:256 + w], ones[0:w, :], mdiag[0:w, 0:w],
                                 start=True, stop=True).then_inc(set_pe, 1)
                if g == 0:
                    layer_norm_transpose(A, 0, [])

            def step(st):
                for slot in range(SLOTS + 1):
                    if slot == LN_B_AT and st.b is not None:
                        waits = [(ln_dve[M], DVE_LN.after("lo", st.b + 1))] if st.m is not None else \
                                [(m_dve, DVE_M.after("off1", NT - 1))]
                        if st.a is not None:
                            waits.append((ln_dve[A], DVE_LN.after("lo", st.a)))
                        layer_norm_transpose(B, st.b, waits)
                    q = st.unit_at(slot)
                    if q is not None:
                        _, s, f, n = st.units[q]
                        gate_up_unit(s, st.a if s == A else st.b, f, n)
                        if q >= DOWN_LAG:
                            down_unit(*st.units[q - DOWN_LAG][2:])
                    if q is not None and q == len(st.units) - 1:
                        for u in st.units[-DOWN_LAG:]:
                            down_unit(*u[2:])
                    if st.m is not None:
                        for name in PE_AT.get(slot, "").split():
                            mamba(name, st.m, st)
                    if slot == LN_M_AT + 1 and st.a is not None and st.a_ends_at() < LN_M_AT - 1 or \
                            slot == SLOTS and st.a is not None and st.a_ends_at() >= LN_M_AT - 1:
                        waits = [(m_dve, DVE_M.after("off1", st.m))] if st.m is not None else []
                        if st.m is None:
                            waits.append((ln_dve[A], DVE_LN.after("lo", st.a)))
                        layer_norm_transpose(M, st.a, waits)
                        if st.next_a:
                            layer_norm_transpose(A, st.i + 1, [(ln_dve[M], DVE_LN.after("lo", st.a))])

            steps(pe, step)

        @block.scalar
        def _(act):
            def layer_norm_hi(s, tile, free):
                act.wait_ge(ln_pe[s], tile + 1)
                for sm, value in free:
                    act.wait_ge(sm, value)
                nc.scalar.activation(xT_hi[s][:].rearrange("p k t -> p (k t)"), R[3][:, :], ACT.Copy).then_inc(ln_act[s], 1)

            def mamba(name, j):
                inc = lambda a: a.then_inc(m_act, 1)
                q = int(name[-1]) if name[-1] in "0123456789" else 0
                if name.startswith("xc"):
                    act.wait_ge(m_pe, PE_M.after(name, j))
                    if q == 0 and not (isinstance(j, int) and j == 0):
                        act.wait_ge(m_dve, DVE_M.after("halo", j - 1))
                    inc(nc.scalar.activation(xc[:, 2 * q:2 * q + 2, HALO:], R[q % 2][:, :].rearrange("p (c t) -> p c t", c=2),
                                             ACT.Copy if False else ACT.Identity, scale=c_in))
                elif name.startswith("th"):
                    act.wait_ge(m_dve, DVE_M.after(f"cv{q}_7", j))
                    inc(nc.scalar.activation(th[:, 2 * q:2 * q + 2, :], cv[:, 2 * q:2 * q + 2, :], ACT.Tanh))
                elif name == "spe":
                    act.wait_ge(m_dve, DVE_M.after("na", j))
                    inc(nc.scalar.activation(sp["e"][:], sp["na"][:], ACT.Exp))
                elif name.startswith("zt"):
                    act.wait_ge(m_pe, PE_M.after(f"z{q}", j))
                    if not (isinstance(j, int) and j == 0):
                        act.wait_ge(m_dve, DVE_M.after(f"zg{q}", j - 1))
                    inc(nc.scalar.activation(zt[:, q, :], R[1 - q][:, :], ACT.Tanh, scale=c_in_half))
                elif name.startswith("zh"):
                    inc(nc.scalar.activation(zh[:, q, :], R[1 - q][:, :], ACT.Identity, scale=c_in_half))
                elif name.startswith("ex"):
                    act.wait_ge(m_pe, PE_M.after(f"cum{q}", j))
                    inc(nc.scalar.activation(ex[:, q, :, :].rearrange("p n h -> p (n h)"), R[2][:, 0:3 * NH], ACT.Exp))
                elif name.startswith("bt"):
                    if q == 1:
                        act.wait_ge(m_pe, PE_M.after("state0", j))
                    elif not (isinstance(j, int) and j == 0):
                        act.wait_ge(m_pe, PE_M.after("state1", j - 1))
                    inc(nc.scalar.activation(Bs[:], R[2][:, P:2 * P], ACT.Copy))
                elif name.startswith("xt"):
                    act.wait_ge(m_pe, PE_M.after(f"xt{q}", j))
                    if q == 1:
                        act.wait_ge(m_pool, POOL_M.after("xD0", j))
                        act.wait_ge(m_dve, DVE_M.after("xd0", j))
                    inc(nc.scalar.activation(xt[:], R[1][:, :], ACT.Copy))
                elif name.startswith("L"):
                    ab = name[1]
                    act.wait_ge(m_pe, PE_M.after(f"seg{q}{ab}", j))
                    if q == 1:
                        act.wait_ge(m_pool, POOL_M.after("M0", j))
                    g = 0 if ab == "a" else 4
                    inc(nc.scalar.activation(L[:, g:g + 4, :], R[0 if ab == "a" else 2][:, :].rearrange("p (h l) -> p h l", h=4),
                                             ACT.Exp))
                elif name.startswith("sq"):
                    act.wait_ge(m_pool, POOL_M.after(f"yz{q}", j))
                    inc(nc.scalar.activation(ysq[:], y[:, q, :], ACT.Square, accum_out=yss[:, q:q + 1]))
                elif name.startswith("yh"):
                    act.wait_ge(m_pe, PE_M.after(f"yt{q}", j))
                    if q == 1:
                        act.wait_ge(m_pe, PE_M.after("out0", j))
                    inc(nc.scalar.activation(yT_hi[:].rearrange("p c l -> p (c l)"), R[2 if q == 0 else 0][:, :], ACT.Copy))

            def weight_hi(c):
                act.wait_ge(s_full, c + 1)
                nc.scalar.activation(whi[:, c, :, :, :].rearrange("p m k n -> p m n k"),
                                     wfull[:, c % 2, :].rearrange("p (m n k) -> p m n k", m=3, k=2), ACT.Copy).then_inc(s_whi, 1)

            def gelu_unit(f, n):
                act.wait_ge(gu_done, unit_sum(f, n))
                b = UNIT_BANK[n]
                nc.scalar.activation(gelu[b][:], gate_up[b][:, 0, :], ACT.Gelu_apprx_tanh, scale=c_gate).then_inc(gelu_done, 1)

            def hi_unit(f, n):
                act.wait_ge(hidden_done, unit_sum(f, n))
                if n >= RING or not (isinstance(f, int) and f == 0):
                    act.wait_ge(down_done, unit_sum(f, n - RING))
                nc.scalar.activation(hid_hi[:, n % RING, :], hidden[UNIT_BANK[n]][:], ACT.Copy).then_inc(hi_done, 1)

            layer_norm_hi(A, 0, [])
            act.wait_ge(s_small, 16 * (4 + 2 * TT))
            weight_hi(0)
            act.wait_ge(set_dve, SET_DVE_POW[1])
            act.wait_ge(set_dve, SET_DVE_POW[1])
            nc.scalar.activation(negA[:], negA[:], ACT.Exp).then_inc(set_act, 1)
            nc.scalar.activation(win_hi[:].rearrange("p k n -> p (k n)"), win.rearrange("p k n -> p (k n)"), ACT.Identity, scale=f_in).then_inc(set_act, 1)
            nc.scalar.activation(wout_hi[:].rearrange("p k n -> p (k n)"), wout.rearrange("p k n -> p (k n)"), ACT.Identity, scale=f_out).then_inc(set_act, 1)

            def step(st):
                first = isinstance(st.i, int) and st.i == 0
                for slot in range(SLOTS + 1):
                    if slot == LN_B_AT and st.b is not None:
                        layer_norm_hi(B, st.b, [] if isinstance(st.i, int) and st.i < 2 else
                                      [(gu_done, st.units[0][2] * UNITS)])
                    q = st.unit_at(slot)
                    if q is not None:
                        gelu_unit(*st.units[q][2:])
                        if first and slot % 2 == 0 and slot // 2 + 1 < CH:
                            weight_hi(slot // 2 + 1)
                        if q >= 1:
                            hi_unit(*st.units[q - 1][2:])
                        if q == len(st.units) - 1:
                            hi_unit(*st.units[q][2:])
                    if st.m is not None:
                        for name in ACT_AT.get(slot, "").split():
                            mamba(name, st.m)
                    if slot == LN_M_AT + 1 and st.a is not None and st.a_ends_at() < LN_M_AT - 1 or \
                            slot == SLOTS and st.a is not None and st.a_ends_at() >= LN_M_AT - 1:
                        layer_norm_hi(M, st.a, [(m_pe, PE_M.after("z1", st.m))] if st.m is not None else [])
                        if st.next_a:
                            layer_norm_hi(A, st.i + 1, [(gu_done, unit_sum(st.units[0][2], UNITS - 1))])

            steps(act, step)

        @block.vector
        def _(dve):
            def wait_apart(semaphore, value):
                dve.wait_ge(semaphore, value)
                if not isinstance(value, int):
                    cell = next(spare_cells)
                    nc.vector.memset(spare_dve[:, cell:cell + 1], 0.0)

            def layer_norm_stats(s, tile):
                for t in range(TT):
                    nc.vector.bn_stats(stats[s][:, t, :], ln_src[s][:, t, :]).then_inc(ln_dve[s], 1)
                for t in range(TT):
                    wait_apart(ln_dve[s], DVE_LN.after(f"stats{t}", tile))
                    nc.vector.bn_aggr(aggr[s][:, t, :], stats[s][:, t, :]).then_inc(ln_dve[s], 1)

            def layer_norm_scale(s, tile):
                dve.wait_ge(ln_pool[s], POOL_LN.after("rstd", tile))
                for t in range(TT):
                    nc.vector.tensor_scalar(xn[s][:, t, :], ln_src[s][:, t, :], aggr[s][:, t, 0:1], rstd[s][:, t:t + 1],
                                            ALU.subtract, ALU.mult).then_inc(ln_dve[s], 1)

            def layer_norm_lo(s, tile):
                dve.wait_ge(ln_act[s], tile + 1)
                nc.vector.tensor_tensor(xT_lo[s][:].rearrange("p k t -> p (k t)"), R[3][:, :],
                                        xT_hi[s][:].rearrange("p k t -> p (k t)"), ALU.subtract).then_inc(ln_dve[s], 1)

            def own(name, j):
                dve.wait_ge(m_dve, DVE_M.after(name, j))

            def conv(p, j):
                dve.wait_ge(m_act, ACT_M.after(f"xc{p}", j))
                for k in range(TAPS):
                    for c in range(2):
                        blk = 2 * p + c
                        ct = (4 + c) if p == 0 else 2 * (p - 1) + c
                        src = xc[:, blk, k:k + TILE]
                        if k == 0:
                            ins = nc.vector.tensor_scalar(cv[:, blk, :], src, cw[:, ct, 0:1], cb[:, ct:ct + 1], ALU.mult, ALU.add)
                        else:
                            own(f"cv{p}_{2 * (k - 1) + c}", j)
                            ins = nc.vector.scalar_tensor_tensor(cv[:, blk, :], src, cw[:, ct, k:k + 1], cv[:, blk, :], ALU.mult, ALU.add)
                        ins.then_inc(m_dve, 1)

            def soft_plus(j):
                inc = lambda a: a.then_inc(m_dve, 1)
                dve.wait_ge(m_act, ACT_M.after("spe", j))
                inc(nc.vector.tensor_scalar(sp["e2"][:], sp["e"][:], 2.0, None, ALU.add))
                own("e2", j)
                inc(nc.vector.reciprocal(sp["er"][:], sp["e2"][:]))
                own("er", j)
                inc(nc.vector.tensor_tensor(sp["r"][:], sp["e"][:], sp["er"][:], ALU.mult))
                own("r", j)
                inc(nc.vector.tensor_tensor(sp["r2"][:], sp["r"][:], sp["r"][:], ALU.mult))
                own("r2", j)
                inc(nc.vector.tensor_scalar(spq[0][:], sp["r2"][:], 1.0 / (2 * LOG_TERMS + 1), None, ALU.mult))
                for k in range(1, LOG_TERMS):
                    own(f"q{k - 1}", j)
                    inc(nc.vector.scalar_tensor_tensor(spq[k][:], spq[k - 1][:], 1.0 / (2 * (LOG_TERMS - k) + 1),
                                                       sp["r2"][:], ALU.add, ALU.mult))
                own(f"q{LOG_TERMS - 1}", j)
                inc(nc.vector.scalar_tensor_tensor(sp["l"][:], spq[-1][:], 1.0, sp["r"][:], ALU.add, ALU.mult))
                inc(nc.vector.tensor_scalar(sp["mv"][:], sp["v"][:], 0.0, None, ALU.max))
                own("mv", j)
                inc(nc.vector.scalar_tensor_tensor(sp["dt"][:], sp["l"][:], 2.0, sp["mv"][:], ALU.mult, ALU.add))
                own("dt", j)
                inc(nc.vector.scalar_tensor_tensor(sp["dA"][:], sp["dt"][:], -1.0, negA[:].rearrange("p t h -> p (t h)"),
                                                   ALU.mult, ALU.mult))
                own("dA", j)
                inc(nc.vector.tensor_scalar(dh[:], sp["dA"][:], DECAY_FLOOR, None, ALU.max))
                own("dh", j)
                inc(nc.vector.scalar_tensor_tensor(dl[:], sp["dA"][:], DECAY_FLOOR, dh[:], ALU.max, ALU.subtract))

            def heads(ap, q):
                return ap.rearrange("p (h o) -> p h o", o=1).to_broadcast([P, NH, HD])

            def mamba(name, j):
                inc = lambda a: a.then_inc(m_dve, 1)
                q = int(name[-1]) if name[-1] in "0123456789" else 0
                by_head = lambda ap: ap.rearrange("p (h d) -> p h d", h=NH)
                if name.startswith("cv"):
                    conv(q, j)
                elif name == "halo":
                    for p in range(3):
                        own(f"cv{p}_7", j)
                    inc(nc.vector.tensor_copy(xc[:, :, 0:HALO], xc[:, :, TILE:TILE + HALO]))
                elif name.startswith("xs"):
                    dve.wait_ge(m_act, ACT_M.after(f"th{q}", j))
                    sl = slice(2 * q, 2 * q + 2)
                    inc(nc.vector.scalar_tensor_tensor(xs[:, sl, :].rearrange("p c t -> p (c t)"), th[:, sl, :].rearrange("p c t -> p (c t)"),
                                                       1.0, cv[:, sl, :].rearrange("p c t -> p (c t)"), ALU.add, ALU.mult))
                elif name == "v":
                    dve.wait_ge(m_pe, PE_M.after("dt", j))
                    inc(nc.vector.scalar_tensor_tensor(sp["v"][:], R[2][:, 0:TT * NH], c_in, dtb[:].rearrange("p t h -> p (t h)"),
                                                       ALU.mult, ALU.add))
                elif name == "na":
                    own("v", j)
                    inc(nc.vector.scalar_tensor_tensor(sp["na"][:], sp["v"][:], -1.0, sp["v"][:], ALU.mult, ALU.min))
                elif name == "soft":
                    soft_plus(j)
                elif name.startswith("zg"):
                    dve.wait_ge(m_act, ACT_M.after(f"zh{q}", j))
                    inc(nc.vector.scalar_tensor_tensor(zg[:, q, :], zt[:, q, :], 1.0, zh[:, q, :], ALU.add, ALU.mult))
                elif name.startswith("cb"):
                    dve.wait_ge(m_pe, PE_M.after(f"cb{q}", j))
                    if q == 1:
                        dve.wait_ge(m_pool, POOL_M.after("M0", j))
                    inc(nc.vector.tensor_tensor(cbm[:], R[3][:, 0:P], incl, ALU.mult))
                elif name.startswith("xd"):
                    dve.wait_ge(m_act, ACT_M.after(f"xt{q}", j))
                    if q == 1:
                        dve.wait_ge(m_pe, PE_M.after("diag0", j))
                        dve.wait_ge(m_pool, POOL_M.after("xe0", j))
                    inc(nc.vector.tensor_tensor(by_head(xd[:]), by_head(xt[:]), heads(sp["dt"][:, q * NH:(q + 1) * NH], q), ALU.mult))
                elif name.startswith("off"):
                    dve.wait_ge(m_pe, PE_M.after(f"off{q}", j))
                    dve.wait_ge(m_act, ACT_M.after(f"ex{q}", j))
                    inc(nc.vector.tensor_tensor(by_head(yo[:]), by_head(R[3][:, :]), heads(ex[:, q, 0, :], q), ALU.mult))
                elif name in ("y0", "y1"):
                    dve.wait_ge(m_pe, PE_M.after(f"diag{q}", j))
                    own(f"off{q}", j)
                    inc(nc.vector.tensor_tensor(y[:, q, :], R[1][:, :], yo[:], ALU.add))
                elif name.startswith("st"):
                    dve.wait_ge(m_pe, PE_M.after(f"state{q}", j))
                    dve.wait_ge(m_pool, POOL_M.after(f"sd{q}", j))
                    inc(nc.vector.tensor_tensor(state[:], R[0][:, :], state[:], ALU.add))
                elif name.startswith("yl"):
                    dve.wait_ge(m_act, ACT_M.after(f"yh{q}", j))
                    inc(nc.vector.tensor_tensor(yT_lo[:].rearrange("p c l -> p (c l)"), R[2 if q == 0 else 0][:, :],
                                                yT_hi[:].rearrange("p c l -> p (c l)"), ALU.subtract))
                elif name.startswith("out"):
                    dve.wait_ge(m_pe, PE_M.after(f"out{q}", j))
                    if q == 0 and not (isinstance(j, int) and j == 0):
                        dve.wait_ge(kept_b, j)
                    inc(nc.vector.scalar_tensor_tensor(x_2[:, q, :], R[1][:, 0:D], c_out, x_m[:, q, :], ALU.mult, ALU.add))

            def decode(c):
                dve.wait_ge(s_chunk[c % 2], 16 * 9 * (c // 2 + 1))
                nc.vector.tensor_scalar(t0[:], pk[:, c % 2, :], 0xFF, 12, ALU.bitwise_and, ALU.logical_shift_left).then_inc(s_step, 1)
                dve.wait_ge(s_step, 3 * c + 1)
                nc.vector.scalar_tensor_tensor(t1[:], pk[:, c % 2, :], 24, t0[:], ALU.logical_shift_left, ALU.bitwise_or).then_inc(s_step, 1)
                dve.wait_ge(s_step, 3 * c + 2)
                nc.vector.tensor_scalar(t0[:], t1[:], 3, 0x0E000E00, ALU.logical_shift_right, ALU.bitwise_and).then_inc(s_step, 1)
                dve.wait_ge(s_step, 3 * c + 3)
                nc.vector.scalar_tensor_tensor(codes[:], t1[:], 0x80008000, t0[:], ALU.bitwise_and, ALU.bitwise_or).then_inc(s_decoded, 1)

            def weight_full(c):
                dve.wait_ge(s_decoded, c + 1)
                if c >= 2:
                    dve.wait_ge(s_wlo, c - 1)
                nc.vector.scalar_tensor_tensor(
                    wfull[:, c % 2, :].rearrange("p (n k) -> p n k", k=2),
                    codes[:].bitcast(F16).rearrange("p (n k) -> p n k", k=2), f_code,
                    sc[:, c % 2, :].rearrange("p (n o) -> p n o", o=1).to_broadcast([P, 3 * WCOL, 2]),
                    ALU.mult, ALU.mult).then_inc(s_full, 1)

            def hidden_unit(f, n):
                b = UNIT_BANK[n]
                dve.wait_ge(gelu_done, unit_sum(f, n))
                prev = before_in_bank(n)
                if not (isinstance(f, int) and f == 0 and prev < 0):
                    dve.wait_ge(lo_done, unit_sum(f, prev))
                nc.vector.scalar_tensor_tensor(hidden[b][:], gate_up[b][:, 1, :], c_up, gelu[b][:], ALU.mult, ALU.mult).then_inc(hidden_done, 1)

            def pass_end(s, f):
                dve.wait_ge(down_done, f * UNITS + UNITS)
                src, dst = (x_a, x_1) if s == A else (x_b, x_o)
                if s == B and not (isinstance(f, int) and f < 4):
                    pass
                nc.vector.scalar_tensor_tensor(dst[:].rearrange("p t d -> p (t d)"), down[:].rearrange("p t d -> p (t d)"), c_down,
                                               src[:].rearrange("p t d -> p (t d)"), ALU.mult, ALU.add).then_inc(pass_read, 1)

            done = [0]

            def chained(ins):
                done[0] += 1
                ins.then_inc(set_dve, 1)
                dve.wait_ge(set_dve, done[0])

            chained(nc.vector.memset(half[:], -0.5))
            chained(nc.vector.memset(xc[:, :, 0:HALO], 0.0))
            dve.wait_ge(s_x, 16)
            layer_norm_stats(A, 0)
            dve.wait_ge(s_sflat, 16)
            chained(nc.vector.tensor_reduce(mx[:, 0:1], sflat[:], AX.X, ALU.max, apply_absolute_value=True))
            assert done[0] == SET_DVE_MAX[0]

            def powers(g, w):
                dve.wait_ge(set_pe, 2 * g + 1)
                chained(nc.vector.tensor_reduce(mrow[0:w, 0:1], R[0][0:w, 0:P], AX.X, ALU.max))
                chained(nc.vector.tensor_scalar(mdiag[0:w, 0:w], ident[0:w, 0:w], mrow[0:w, 0:1], None, ALU.mult))
                assert done[0] == SET_DVE_DIAG[g]
                dve.wait_ge(set_pe, 2 * g + 2)
                chained(nc.vector.tensor_scalar(pw[:, g:g + w], R[0][:, 256:256 + w], SMALLEST, None, ALU.max))
                chained(nc.vector.tensor_scalar(pw[:, g:g + w].bitcast(U32), pw[:, g:g + w].bitcast(U32), 0x7F800000, None, ALU.bitwise_and))
                chained(nc.vector.reciprocal(pw[:, 3 + g:3 + g + w], pw[:, g:g + w]))

            dve.wait_ge(s_cst, 16)
            powers(0, 1)
            chained(nc.vector.tensor_scalar(f_code, r_ffn, 2.0 ** (CODE_BITS + FFN_BITS), None, ALU.mult))
            chained(nc.vector.tensor_scalar(c_gate, m_ffn, 2.0 ** -(FFN_BITS + ACTIVATION_BITS), None, ALU.mult))
            chained(nc.vector.tensor_scalar(c_up, r_ffn, 2.0 ** (HIDDEN_BITS - FFN_BITS - ACTIVATION_BITS), None, ALU.mult))
            chained(nc.vector.tensor_tensor(m_cube, m_ffn, m_ffn, ALU.mult))
            chained(nc.vector.tensor_tensor(m_cube, m_cube, m_ffn, ALU.mult))
            chained(nc.vector.tensor_scalar(c_down, m_cube, 0.5 * 2.0 ** -(FFN_BITS + HIDDEN_BITS), None, ALU.mult))
            assert done[0] == SET_DVE_POW[0], done
            layer_norm_scale(A, 0)
            decode(0)
            layer_norm_lo(A, 0)
            weight_full(0)
            decode(1)
            dve.wait_ge(s_small, 16 * (4 + 2 * TT))
            dve.wait_ge(s_win, 16)
            dve.wait_ge(s_wout, 16)
            for k in range(4):
                chained(nc.vector.tensor_scalar(wout[:, k, :], wout[:, k, :], nw[:, k:k + 1], None, ALU.mult))
            chained(nc.vector.tensor_scalar(cw[:], cw[:], 0.5, None, ALU.mult))
            chained(nc.vector.tensor_scalar(cb[:], cb[:], 0.5, None, ALU.mult))
            chained(nc.vector.tensor_copy(incl16[:], incl))
            chained(nc.vector.tensor_copy(later16[:], later))
            chained(nc.vector.tensor_reduce(mx[:, 1:2], win.rearrange("p k n -> p (k n)"), AX.X, ALU.max, apply_absolute_value=True))
            chained(nc.vector.tensor_reduce(mx[:, 2:3], wout.rearrange("p k n -> p (k n)"), AX.X, ALU.max, apply_absolute_value=True))
            assert done[0] == SET_DVE_MAX[1], done
            weight_full(1)
            powers(1, 2)
            chained(nc.vector.tensor_scalar(pw[:, 13:15], pw[:, 4:6], 2.0 ** PROJ_BITS, None, ALU.mult))
            chained(nc.vector.tensor_scalar(c_in, m_in, 2.0 ** -(PROJ_BITS + ACTIVATION_BITS), None, ALU.mult))
            chained(nc.vector.tensor_scalar(c_in_half, m_in, 2.0 ** -(PROJ_BITS + ACTIVATION_BITS + 1), None, ALU.mult))
            chained(nc.vector.tensor_scalar(c_out, m_out, 2.0 ** -(PROJ_BITS + ACTIVATION_BITS), None, ALU.mult))
            assert done[0] == SET_DVE_POW[1], done

            def step(st):
                first = isinstance(st.i, int) and st.i == 0
                for slot in range(SLOTS + 1):
                    if slot == LN_B_AT - 3 and st.b is not None:
                        dve.wait_ge(m_dve, DVE_M.after("out1", st.b))
                        layer_norm_stats(B, st.b)
                    if slot == LN_B_AT - 1 and st.b is not None:
                        layer_norm_scale(B, st.b)
                    if slot == LN_B_AT and st.b is not None:
                        layer_norm_lo(B, st.b)
                    if st.a is not None and slot == st.a_ends_at():
                        pass_end(A, st.units[0][2])
                    q = st.unit_at(slot)
                    if first and q is not None and slot % 2 == 0:
                        c = slot // 2 + 2
                        if c < CH:
                            decode(c)
                            weight_full(c)
                    if q is not None:
                        hidden_unit(*st.units[q][2:])
                    if first and slot == 6:
                        dve.wait_ge(set_act, 3)
                        flat = lambda ap: ap.rearrange("p k n -> p (k n)")
                        chained(nc.vector.scalar_tensor_tensor(flat(win_lo[:]), flat(win), f_in, flat(win_hi[:]), ALU.mult, ALU.subtract))
                        chained(nc.vector.scalar_tensor_tensor(flat(wout_lo[:]), flat(wout), f_out, flat(wout_hi[:]), ALU.mult, ALU.subtract))
                        assert done[0] == SET_DVE_END
                    if q is not None and q == len(st.units) - 1 and st.b is not None:
                        if not (isinstance(st.i, int) and st.i < 3) and True:
                            pass
                        if not isinstance(st.b, int) or st.b > 0:
                            pass
                        pass
                    if st.m is not None:
                        for name in DVE_AT.get(slot, "").split():
                            mamba(name, st.m)
                    late = st.a is not None and st.a_ends_at() >= LN_M_AT - 1
                    if st.a is not None and (slot == LN_M_AT and not late or slot == SLOTS and late):
                        dve.wait_ge(pass_read, st.units[0][2] + 1)
                        layer_norm_stats(M, st.a)
                        if st.next_a:
                            dve.wait_ge(s_x, (st.i + 2) * 16)
                            layer_norm_stats(A, st.i + 1)
                    if st.a is not None and (slot == LN_M_AT + 1 and not late or slot == SLOTS and late):
                        layer_norm_scale(M, st.a)
                        if st.next_a:
                            layer_norm_scale(A, st.i + 1)
                        layer_norm_lo(M, st.a)
                        if st.next_a:
                            layer_norm_lo(A, st.i + 1)
                if st.b is not None:
                    if not isinstance(st.b, int) or st.b > 0:
                        dve.wait_ge(s_out, st.b * 16)
                    pass_end(B, st.units[-1][2])

            steps(dve, step)

        @block.gpsimd
        def _(pool):
            def wait_apart(semaphore, value):
                pool.wait_ge(semaphore, value)
                if not isinstance(value, int):
                    cell = next(spare_cells)
                    nc.gpsimd.tensor_tensor(spare_pool[:, cell:cell + 1], half[:], half[:], ALU.add)

            def layer_norm_rstd(s, tile):
                wait_apart(ln_dve[s], DVE_LN.after("aggr1", tile))
                g = 2.0 ** (-2 * ACTIVATION_BITS)
                nc.gpsimd.tensor_scalar(ve[s][:], aggr[s][:, :, 1], EPS, g, ALU.add, ALU.mult).then_inc(ln_pool[s], 1)
                pool.wait_ge(ln_pool[s], POOL_LN.after("ve", tile))
                nc.gpsimd.tensor_tensor(rstd[s][:], ve[s][:], half[:].to_broadcast([P, TT]), ALU.pow).then_inc(ln_pool[s], 1)

            def mamba(name, j, st):
                inc = lambda a: a.then_inc(m_pool, 1)
                own = lambda name: pool.wait_ge(m_pool, POOL_M.after(name, j))
                q = int(name[-1]) if name[-1] in "0123456789" else 0
                by_head = lambda ap: ap.rearrange("p (h d) -> p h d", h=NH)
                heads = lambda ap, n: ap.rearrange("p (h o) -> p h o", o=1).to_broadcast([P, NH, n])
                over = lambda ap: ap.rearrange("p (o l) -> p o l", o=1).to_broadcast([P, NH, P])
                if name == "hand":
                    if not (isinstance(j, int) and j == 0):
                        pool.wait_ge(m_dve, DVE_M.after("out1", j - 1))
                    wait_apart(ln_dve[M], DVE_LN.after("stats1", j))
                    inc(nc.gpsimd.tensor_copy(x_m[:], x_1[:]))
                elif name[0] == "R":
                    part = Rh if name[1] == "h" else Rl
                    pool.wait_ge(m_dve, DVE_M.after("dl", j))
                    if q == 1:
                        pool.wait_ge(m_pe, PE_M.after("seg0b", j))
                    d = (dh if name[1] == "h" else dl)[:, q * NH:(q + 1) * NH]
                    inc(nc.gpsimd.tensor_tensor(part[:], over(incl16[:]), heads(d, P), ALU.mult))
                elif name[:2] == "xD":
                    pool.wait_ge(m_act, ACT_M.after(f"xt{q}", j))
                    inc(nc.gpsimd.tensor_tensor(by_head(xD[:, q, :]), by_head(xt[:]), heads(dsk[:], HD), ALU.mult))
                elif name[:2] == "xe":
                    pool.wait_ge(m_dve, DVE_M.after(f"xd{q}", j))
                    pool.wait_ge(m_act, ACT_M.after(f"ex{q}", j))
                    if q == 1:
                        pool.wait_ge(m_pe, PE_M.after("state0", j))
                    inc(nc.gpsimd.tensor_tensor(by_head(xe[:]), by_head(xd[:]), heads(ex[:, q, 2, :], HD), ALU.mult))
                elif name[0] == "M":
                    pool.wait_ge(m_act, ACT_M.after(f"Lb{q}", j))
                    pool.wait_ge(m_dve, DVE_M.after(f"cb{q}", j))
                    if q == 1:
                        pool.wait_ge(m_pe, PE_M.after("diag0", j))
                    inc(nc.gpsimd.tensor_tensor(Mm, L, over(cbm[:]), ALU.mult))
                elif name[:2] == "sd":
                    pool.wait_ge(m_pe, PE_M.after(f"off{q}", j))
                    if q == 1:
                        pool.wait_ge(m_dve, DVE_M.after("st0", j))
                    elif not (isinstance(j, int) and j == 0):
                        pool.wait_ge(m_dve, DVE_M.after("st1", j - 1))
                    inc(nc.gpsimd.tensor_tensor(by_head(state[:]), by_head(state[:]), heads(ex[:, q, 1, :], HD), ALU.mult))
                elif name[:2] == "yx":
                    pool.wait_ge(m_dve, DVE_M.after(f"y{q}", j))
                    own(f"xD{q}")
                    inc(nc.gpsimd.tensor_tensor(y[:, q, :], y[:, q, :], xD[:, q, :], ALU.add))
                elif name[:2] == "yz":
                    own(f"yx{q}")
                    inc(nc.gpsimd.tensor_tensor(y[:, q, :], y[:, q, :], zg[:, q, :], ALU.mult))
                elif name[:2] == "ve":
                    wait_apart(m_act, ACT_M.after(f"sq{q}", j))
                    inc(nc.gpsimd.tensor_scalar(yve[:, q:q + 1], yss[:, q:q + 1], 1.0 / DI, EPS, ALU.mult, ALU.add))
                elif name[:2] == "rs":
                    own(f"ve{q}")
                    inc(nc.gpsimd.tensor_tensor(yrs[:, q:q + 1], yve[:, q:q + 1], half[:], ALU.pow))
                elif name[:2] == "yn":
                    wait_apart(m_pool, POOL_M.after(f"rs{q}", j))
                    inc(nc.gpsimd.tensor_scalar(yn[:, q, :], y[:, q, :], yrs[:, q:q + 1], 2.0 ** ACTIVATION_BITS, ALU.mult, ALU.mult))

            def lo_unit(f, n):
                pool.wait_ge(hi_done, unit_sum(f, n))
                nc.gpsimd.tensor_tensor(hid_lo[:, n % RING, :], hidden[UNIT_BANK[n]][:], hid_hi[:, n % RING, :],
                                        ALU.subtract).then_inc(lo_done, 1)

            def weight_lo(c):
                pool.wait_ge(s_whi, c + 1)
                for mat in range(3):
                    ins = nc.gpsimd.tensor_tensor(
                        wlo[:, c, mat, :, :].rearrange("p k n -> p n k"),
                        wfull[:, c % 2, :].rearrange("p (m n k) -> p m n k", m=3, k=2)[:, mat, :, :],
                        whi[:, c, mat, :, :].rearrange("p k n -> p n k"), ALU.subtract)
                ins.then_inc(s_wlo, 1)

            nc.gpsimd.memset(state[:], 0.0).then_inc(set_pool, 1)
            pool.wait_ge(set_dve, 1)
            layer_norm_rstd(A, 0)
            weight_lo(0)

            def step(st):
                first = isinstance(st.i, int) and st.i == 0
                for slot in range(SLOTS + 1):
                    if slot == 0 and st.a is not None:
                        if not first:
                            pool.wait_ge(pass_read, st.units[0][2] if isinstance(st.i, int) else st.units[0][2] - 1)
                        wait_apart(ln_dve[A], DVE_LN.after("xn1", st.a))
                        nc.gpsimd.tensor_copy(x_a[:], x_in[:]).then_inc(kept_a, 1)
                    if slot == LN_B_AT - 3 and st.b is not None:
                        layer_norm_rstd(B, st.b)
                    if slot == 2 and st.b is not None:
                        pool.wait_ge(pass_read, st.units[-1][2] - 1 if st.a is not None else st.units[-1][2])
                        wait_apart(ln_dve[B], DVE_LN.after("xn1", st.b))
                        nc.gpsimd.tensor_copy(x_b[:], x_2[:]).then_inc(kept_b, 1)
                    q = st.unit_at(slot)
                    if q is not None:
                        if q >= 1:
                            lo_unit(*st.units[q - 1][2:])
                        if first and slot % 2 == 0 and slot // 2 + 1 < CH:
                            weight_lo(slot // 2 + 1)
                        if q == len(st.units) - 1:
                            lo_unit(*st.units[q][2:])
                    if st.m is not None:
                        for name in POOL_AT.get(slot, "").split():
                            mamba(name, st.m, st)
                    late = st.a is not None and st.a_ends_at() >= LN_M_AT - 1
                    if st.a is not None and (slot == LN_M_AT and not late or slot == SLOTS and late):
                        layer_norm_rstd(M, st.a)
                        if st.next_a:
                            layer_norm_rstd(A, st.i + 1)

            steps(pool, step)


SET_DVE_MAX = (3, 24)
SET_DVE_DIAG = (5, 26)
SET_DVE_POW = (14, 33)
SET_DVE_END = 35


def kernel(L0_attn_u, L0_attn_in_proj_w, L0_attn_conv_w, L0_attn_conv_b, L0_attn_dt_bias, L0_attn_A_log,
           L0_attn_D_skip, L0_attn_norm_w, L0_attn_out_proj_w, L0_ffn_gate_W_packed, L0_ffn_gate_scales,
           L0_ffn_up_W_packed, L0_ffn_up_scales, L0_ffn_down_W_packed, L0_ffn_down_scales):
    import concourse.bacc as bacc
    from concourse.bass_utils import run_bass_kernel_spmd

    def rows(a, last):
        return np.asarray(a).reshape(CH, P, 2, last).transpose(3, 0, 2, 1).reshape(last, CH, 2 * P)

    def cols(a, per):
        return np.asarray(a).reshape(D, CH, per).transpose(2, 1, 0)

    packed = np.stack([rows(L0_ffn_gate_W_packed, P), rows(L0_ffn_up_W_packed, P),
                       cols(L0_ffn_down_W_packed, P)], axis=2)
    scales = np.stack([rows(L0_ffn_gate_scales, 8), rows(L0_ffn_up_scales, 8),
                       cols(L0_ffn_down_scales, 8)], axis=2)
    w_in = np.asarray(L0_attn_in_proj_w).T.reshape(P, 2, NPROJ)
    at = np.arange(P)
    consts = np.stack([at[:, None] == at, at[:, None] <= at, at[:, None] > at, np.ones((P, P), bool)], axis=1).astype(np.float32)
    arrays = {
        "x": np.asarray(L0_attn_u),
        "packed": packed,
        "scales": scales,
        "w_in": w_in,
        "conv_w": np.asarray(L0_attn_conv_w).reshape(CT, P, TAPS).transpose(1, 0, 2),
        "conv_b": np.asarray(L0_attn_conv_b).reshape(CT, P).T,
        "dt_bias": np.asarray(L0_attn_dt_bias),
        "A_log": np.asarray(L0_attn_A_log),
        "D_skip": np.asarray(L0_attn_D_skip),
        "norm_w": np.asarray(L0_attn_norm_w).reshape(4, P).T,
        "w_out": np.asarray(L0_attn_out_proj_w).T.reshape(4, P, D).transpose(1, 0, 2),
        "consts": consts,
    }
    arrays = {k: np.ascontiguousarray(v) for k, v in arrays.items()}
    nc = bacc.Bacc("TRN2", target_bir_lowering=False, num_devices=1)
    args = [nc.dram_tensor(k, v.shape, mybir.dt.from_np(v.dtype), kind="ExternalInput").ap() for k, v in arrays.items()]
    out = nc.dram_tensor("out", (1, SEQ, D), F32, kind="ExternalOutput").ap()
    macaron(nc, *args, out)
    result = run_bass_kernel_spmd(nc, [arrays], core_ids=[0])
    return result.results[0]["out"]
```

```python
from contextlib import ExitStack

import numpy as np

import concourse.bass as bass
from concourse import mybir

P = 128
SEQ = 1024
D = 256
TILE = 256
TT = TILE // P
NT = SEQ // TILE
MLP = 2048
UNITS = MLP // P
CH = UNITS // 2
WCOL = 256
DI = 512
NH = 8
HD = DI // NH
CT = 6
TAPS = 4
NPROJ = 2 * DI + 2 * P + NH
EPS = 1e-5

F32 = mybir.dt.float32
F16 = mybir.dt.float16
I32 = mybir.dt.int32
U32 = mybir.dt.uint32
ALU = mybir.AluOpType
ACT = mybir.ActivationFunctionType
AX = mybir.AxisListType

ACTIVATION_BITS = 10
FFN_BITS = 12
PROJ_BITS = 14
HIDDEN_BITS = -8
SMALLEST = 2.0 ** -30
CODE_BITS = 14
LOG_TERMS = 6
DECAY_FLOOR = -60000.0

START_LEAD = 2
START_UNITS = ([(0, n) for n in range(START_LEAD)]
               + [u for n in range(START_LEAD, UNITS) for u in ((0, n), (1, n - START_LEAD))]
               + [(1, n) for n in range(UNITS - START_LEAD, UNITS)])


def unit_bank(q):
    return 1 if q == UNITS - 1 else q % 3


def start_bank(q):
    return q % 3


def before_in_bank(q, bank):
    earlier = [u for u in range(q) if bank(u) == bank(q)]
    return earlier[-1] if earlier else (-2, -1, -2)[bank(q)]


DOWN_LAG = 3
LARGEST_AT = 24
RING = 4

F, M = "f", "m"


class Order:

    def __init__(self, names):
        self.names = names.split()
        assert len(set(self.names)) == len(self.names)

    def after(self, name, tile):
        return tile * len(self.names) + self.names.index(name) + 1

    def all(self, tiles):
        return tiles * len(self.names)


PE_M = Order("dt xc0 xc1 xc2 cum z0 z1 seg0a seg0b bt cb seg1a seg1b xt0 off0 xt1 diag0 "
             "state0 off1 diag1 state1 yt0 out0 yt1 out1")
ACT_M = Order("xc0 spe xc1 xc2 th0 zt0 zh0 th1 zt1 zh1 th2 ex La0 Lb0 bt La1 Lb1 xt0 xt1 sq0 "
              "yh0 sq1 yh1")
CONV = [f"cv{p}_{k}" for p in range(3) for k in range(2 * TAPS)]
DVE_M = Order(" ".join(["v", "na"] + CONV[:8] + ["e2", "er", "r", "r2"]
                       + [f"q{k}" for k in range(LOG_TERMS)] + ["l", "mv", "dt", "dA", "dh", "dl"]
                       + ["xs0"] + CONV[8:] + ["halo", "xs1", "xs2", "zg0", "zg1", "cb",
                          "xd0", "off0", "xd1", "y0", "g0", "st0", "off1", "y1", "g1", "st1",
                          "yl0", "out0", "yl1", "out1"]))
POOL_M = Order("Rh0 Rl0 Rh1 Rl1 M0 xD0 xe0 yx0 sd0 M1 xD1 xe1 yx1 sd1 ve0 rs0 yn0 ve1 rs1 yn1")
DVE_LN = Order("stats0 stats1 aggr0 aggr1 xn0 xn1 lo")
POOL_LN = Order("ve rstd")

PE_AT = {0: "dt xc0", 1: "xc1", 2: "xc2 cum", 3: "z0", 4: "z1", 5: "seg0a seg0b bt",
         6: "cb seg1a seg1b", 7: "xt0 off0", 8: "xt1 diag0", 9: "state0 off1", 10: "diag1 state1",
         12: "yt0", 13: "out0 LN_m", 14: "yt1 LN_f", 15: "out1"}
ACT_AT = {0: "xc0", 1: "spe xc1", 2: "xc2 th0", 3: "zt0 zh0 th1", 4: "zt1 zh1 th2",
          5: "ex La0 Lb0 bt", 6: "La1 Lb1", 7: "xt0", 8: "xt1", 10: "sq0", 12: "yh0 sq1",
          14: "LN_m yh1"}
DVE_AT = {0: "v na", 1: "cv0", 2: "soft xs0", 3: "cv1", 4: "cv2 halo xs1", 5: "xs2 zg0 zg1",
          6: "cb", 7: "xd0", 8: "off0 xd1", 9: "y0 g0 st0", 10: "off1 y1 g1 st1",
          11: "stats", 12: "scale", 13: "yl0 out0", 14: "LN_m yl1", 15: "out1"}
POOL_AT = {3: "Rh0 Rl0", 4: "Rh1 Rl1", 6: "M0", 7: "xD0 xe0", 8: "yx0 sd0 M1", 9: "xD1 xe1",
           10: "yx1 sd1", 11: "ve0 rs0 yn0 rstd", 12: "ve1 rs1 yn1"}


def steps(engine, step):
    with engine.Fori(1, NT + 1) as s:
        step(s, True, True)
    step(NT + 1, False, True)
    step(NT + 2, False, False)


def macaron(nc, x, packed, scales, w_in, conv_w, conv_b, dt_bias, A_log, D_skip, norm_w, w_out,
            consts, out):
    with ExitStack() as ctx:
        def sb(name, shape, dt=F32):
            return ctx.enter_context(nc.sbuf_tensor(name, shape, dt))

        def sem(name):
            return ctx.enter_context(nc.semaphore(name))

        gate_up = [ctx.enter_context(nc.psum_tensor(f"gate_up{b}", [P, 2, TILE], F32)) for b in range(3)]
        down = ctx.enter_context(nc.psum_tensor("down", [P, TT, D], F32))
        R = [ctx.enter_context(nc.psum_tensor(f"mixed{b}", [P, 512], F32)) for b in range(4)]

        cst = sb("cst", [P, 4, P])
        ident, incl, later, ones = (cst[:, n, :] for n in range(4))
        incl16 = sb("incl16", [P, P], F16)
        later16 = sb("later16", [P, P], F16)
        half = sb("half", [P, 1])
        spare_dve, spare_pool = sb("spare_dve", [P, 64]), sb("spare_pool", [P, 64])
        spare_cells = iter(range(64))
        WORDS = 3 * WCOL
        early = sb("early", [P, 11 * WORDS])

        def part(at, n, dt=F32):
            return early[:, at:at + n].bitcast(dt) if dt != F32 else early[:, at:at + n]

        pk = part(0, 2 * WORDS, U32).rearrange("p (c n) -> p c n", c=2)
        sc = part(2 * WORDS, 2 * WORDS).rearrange("p (c n) -> p c n", c=2)
        t0, t1 = part(4 * WORDS, WORDS, U32), part(5 * WORDS, WORDS, U32)
        codes = part(6 * WORDS, WORDS, U32)
        wfull = part(7 * WORDS, 4 * WORDS).rearrange("p (c n) -> p c n", c=2)
        whi = sb("whi", [P, CH, 3, 2, WCOL], F16)
        wlo = sb("wlo", [P, CH, 3, 2, WCOL], F16)
        sflat = sb("sflat", [P, 3 * P])
        mx = sb("mx", [P, 4])
        mrow = sb("mrow", [4, 4])
        mdiag = sb("mdiag", [4, 4])
        pw = sb("pw", [P, 16])
        early1 = sb("early1", [P, 2 * NPROJ])
        win = early1[:, :].rearrange("p (k n) -> p k n", k=2)
        win_hi = sb("win_hi", [P, 2, NPROJ], F16)
        win_lo = sb("win_lo", [P, 2, NPROJ], F16)
        early2 = sb("early2", [P, 4 * D])
        wout = early2[:, :].rearrange("p (k n) -> p k n", k=4)
        wout_hi = sb("wout_hi", [P, 4, D], F16)
        wout_lo = sb("wout_lo", [P, 4, D], F16)
        cw = sb("cw", [P, CT, TAPS])
        cb = sb("cb", [P, CT])
        nw = sb("nw", [P, 4])
        dtb = sb("dtb", [P, TT, NH])
        negA = sb("negA", [P, TT, NH])
        dsk = sb("dsk", [P, NH])

        ffn_in = sb("ffn_in", [P, NT * TT * D])
        ffn_out = sb("ffn_out", [P, NT * TT * D])

        def of_tile(buffer, t):
            at = (t % NT) * (TT * D)
            cols = buffer[:, at:at + TT * D] if isinstance(t, int) else buffer[:, bass.ds(at, TT * D)]
            return cols.rearrange("p (t d) -> p t d", t=TT)

        ln_src = {F: ffn_in, M: ffn_out}
        stats = {s: sb(f"stats_{s}", [P, TT, 6]) for s in (F, M)}
        aggr = {s: sb(f"aggr_{s}", [P, TT, 2]) for s in (F, M)}
        ve = {s: sb(f"ve_{s}", [P, TT]) for s in (F, M)}
        rstd = {s: sb(f"rstd_{s}", [P, TT]) for s in (F, M)}
        xn = {s: sb(f"xn_{s}", [P, TT, D]) for s in (F, M)}
        xT_hi = {s: sb(f"xT_hi_{s}", [P, 2, TILE], F16) for s in (F, M)}
        xT_lo = {s: sb(f"xT_lo_{s}", [P, 2, TILE], F16) for s in (F, M)}

        gelu = [sb(f"gelu{b}", [P, TILE]) for b in range(3)]
        hidden = [sb(f"hidden{b}", [P, TILE]) for b in range(3)]
        hid_hi = sb("hid_hi", [P, RING, TILE], F16)
        hid_lo = sb("hid_lo", [P, RING, TILE], F16)

        HALO = TAPS - 1
        xc = sb("xc", [P, CT, HALO + TILE])
        cv = part(0, CT * TILE).rearrange("p (c t) -> p c t", c=CT)
        th = part(CT * TILE, CT * TILE).rearrange("p (c t) -> p c t", c=CT)
        xs = th
        BT, CTr = xs[:, 0, :], xs[:, 1, :]
        MORE = 2 * CT * TILE
        zt = part(MORE, TT * DI).rearrange("p (t d) -> p t d", t=TT)
        zh = part(MORE + TT * DI, TT * DI).rearrange("p (t d) -> p t d", t=TT)
        MORE += 2 * TT * DI
        zg = zt
        sp = {n: sb(f"sp_{n}", [P, TT * NH]) for n in "v na e e2 er r r2 l mv dt dA".split()}
        spq = [sb(f"sp_q{k}", [P, TT * NH]) for k in range(LOG_TERMS)]
        dh = sb("dh", [P, TT * NH], F16)
        dl = sb("dl", [P, TT * NH], F16)
        Rh = sb("Rh", [P, TT, NH, P], F16)
        Rl = sb("Rl", [P, TT, NH, P], F16)
        ex = sb("ex", [P, 3, TT, NH])
        L = part(MORE, TT * NH * P).rearrange("p (q h l) -> p q h l", q=TT, h=NH)
        MORE += TT * NH * P
        assert MORE <= 11 * WORDS
        cbm = sb("cbm", [P, TT, P])
        Mm = early1[:, 0:TT * NH * P].rearrange("p (q h l) -> p q h l", q=TT, h=NH)
        Bs = sb("Bs", [P, TT, P])
        xt = sb("xt", [P, TT, DI])
        xd = sb("xd", [P, TT, DI])
        xe = sb("xe", [P, TT, DI])
        xD = sb("xD", [P, TT, DI])
        state = sb("state", [P, DI])
        yo = sb("yo", [P, TT, DI])
        y = early2[:, :].rearrange("p (t d) -> p t d", t=TT)
        ysq = sb("ysq", [P, DI])
        yss = sb("yss", [P, TT])
        yve = sb("yve", [P, TT])
        yrs = sb("yrs", [P, TT])
        yn = sb("yn", [P, TT, DI])
        yT_hi = sb("yT_hi", [P, 4, P], F16)
        yT_lo = sb("yT_lo", [P, 4, P], F16)

        s_sflat, s_cst, s_small, s_win, s_wout = map(sem, "sflat_in cst_in small_in win_in wout_in".split())
        s_chunk = [sem("chunk_in0"), sem("chunk_in1")]
        s_x = [sem("x0_in"), sem("x1_in"), sem("x_rest_in")]
        s_out = sem("out_stored")
        set_dve, set_pe, set_act, set_pool = map(sem, "setup_dve setup_pe setup_act setup_pool".split())
        s_decoded, s_full, s_whi, s_wlo, s_wlo_down = map(
            sem, "codes_ready wfull_ready whi_ready wlo_gate_up_ready wlo_down_ready".split())
        s_step = sem("decode_step")
        gu_done, gelu_done, hidden_done, hi_done, lo_done, down_done, pass_read = map(
            sem, "gate_up_done gelu_done hidden_done hidden_hi_done hidden_lo_done down_done pass_read".split())
        m_pe, m_act, m_dve, m_pool = map(sem, "mamba_pe mamba_act mamba_dve mamba_pool".split())
        ln_dve = {s: sem(f"ln_dve_{s}") for s in (F, M)}
        ln_pool = {s: sem(f"ln_pool_{s}") for s in (F, M)}
        ln_pe = {s: sem(f"ln_pe_{s}") for s in (F, M)}
        ln_act = {s: sem(f"ln_act_{s}") for s in (F, M)}

        m_ffn, m_in, m_out = (pw[:, n:n + 1] for n in range(3))
        r_ffn, r_in, r_out = (pw[:, 3 + n:4 + n] for n in range(3))
        f_code = pw[:, 6:7]
        c_gate = pw[:, 7:8]
        c_up = pw[:, 8:9]
        c_down = pw[:, 9:10]
        c_in = pw[:, 10:11]
        c_in_half = pw[:, 11:12]
        c_out = pw[:, 12:13]
        f_in = pw[:, 13:14]
        f_out = pw[:, 14:15]
        m_cube = pw[:, 15:16]

        x_t = x.rearrange("o (n t p) d -> (o n) p t d", p=P, t=TT)
        out_t = out.rearrange("o (n t p) d -> (o n) p t d", p=P, t=TT)

        down_bank = [down, R[3][:, :].rearrange("p (t d) -> p t d", t=TT)]

        def unit_number(f, n):
            return START_UNITS.index((f, n)) if isinstance(f, int) and f < 2 else f * UNITS + n

        block = ctx.enter_context(nc.Block())

        @block.sync
        def _(sync):
            def chunk(c):
                if c >= 2:
                    sync.wait_ge(s_full, c - 1)
                sync.dma_start(pk[:, c % 2, :].bitcast(I32), packed[:, c]).then_inc(s_chunk[c % 2], 16)
                for b in range(8):
                    sync.dma_start(sc[16 * b:16 * b + 16, c % 2, :],
                                   scales[b, c].rearrange("m n -> (m n)").partition_broadcast(16)).then_inc(s_chunk[c % 2], 16)

            sync.dma_start(sflat[:], scales.rearrange("b c m n -> (b c m n)").rearrange("(p f) -> p f", p=P)).then_inc(s_sflat, 16)
            sync.dma_start(of_tile(ffn_in, 0), x_t[0]).then_inc(s_x[0], 16)
            sync.dma_start(cst[:], consts).then_inc(s_cst, 16)
            chunk(0)
            sync.dma_start(of_tile(ffn_in, 1), x_t[1]).then_inc(s_x[1], 16)
            chunk(1)
            for t in range(2, NT):
                sync.dma_start(of_tile(ffn_in, t), x_t[t]).then_inc(s_x[2], 16)
            sync.dma_start(cw[:], conv_w).then_inc(s_small, 16)
            sync.dma_start(cb[:], conv_b).then_inc(s_small, 16)
            sync.dma_start(nw[:], norm_w).then_inc(s_small, 16)
            for t in range(TT):
                sync.dma_start(dtb[:, t, :], dt_bias.partition_broadcast(P)).then_inc(s_small, 16)
                sync.dma_start(negA[:, t, :], A_log.partition_broadcast(P)).then_inc(s_small, 16)
            sync.dma_start(dsk[:], D_skip.partition_broadcast(P)).then_inc(s_small, 16)
            chunk(2)
            sync.dma_start(win, w_in).then_inc(s_win, 16)
            sync.dma_start(wout, w_out).then_inc(s_wout, 16)
            for c in range(3, CH):
                chunk(c)
            with sync.Fori(0, NT) as t:
                sync.wait_ge(pass_read, NT + 1 + t)
                sync.dma_start(out_t[bass.ds(t, 1)].rearrange("o p t d -> p (o t) d"), of_tile(ffn_out, t)).then_inc(s_out, 16)
            sync.wait_ge(s_out, 16 * NT)

        @block.tensor
        def _(pe):
            def layer_norm_transpose(s, index, bank, free, use=None):
                use = use or s
                pe.wait_ge(ln_dve[s], DVE_LN.after("xn1", index))
                for semaphore, value in free:
                    pe.wait_ge(semaphore, value)
                for t in range(TT):
                    for kk in range(2):
                        mm = nc.tensor.transpose(R[bank][:, kk * TILE + t * P:kk * TILE + (t + 1) * P],
                                                 xn[use][:, t, kk::2], ident)
                mm.then_inc(ln_pe[s], 1)

            def gate_up_unit(f, n, q, base, bank):
                start = base is None
                tokens = M if start and f == 1 else F
                if n == 0:
                    pe.wait_ge(ln_dve[F], DVE_LN.after("lo", f))
                before = before_in_bank(q, bank)
                if not start:
                    pe.wait_ge(hidden_done, base + before + 1)
                elif before >= 0:
                    pe.wait_ge(hidden_done, before + 1)
                if start and f == 0 and n % 2 == 0:
                    pe.wait_ge(s_wlo, n // 2 + 1)
                    pe.wait_ge(s_wlo_down, n // 2 + 1)
                c, e = n // 2, n % 2
                for mat in range(2):
                    o = gate_up[bank(q)][:, mat, :]
                    for kk in range(2):
                        hi = whi[:, c, mat, kk, e * P:(e + 1) * P]
                        lo = wlo[:, c, mat, kk, e * P:(e + 1) * P]
                        nc.tensor.matmul(o, hi, xT_hi[tokens][:, kk, :], start=(kk == 0), stop=False)
                        nc.tensor.matmul(o, hi, xT_lo[tokens][:, kk, :], start=False, stop=False)
                        mm = nc.tensor.matmul(o, lo, xT_hi[tokens][:, kk, :], start=False, stop=(kk == 1))
                mm.then_inc(gu_done, 1)

            def down_unit(f, n):
                pe.wait_ge(lo_done, unit_number(f, n) + 1)
                start = isinstance(f, int) and f < 2
                if n == 0 and not start:
                    pe.wait_ge(pass_read, f)
                c, e, place = n // 2, n % 2, unit_number(f, n) % RING if start else n % RING
                for t in range(TT):
                    hi = hid_hi[:, place, t * P:(t + 1) * P]
                    lo = hid_lo[:, place, t * P:(t + 1) * P]
                    o = down_bank[1 if start and f == 1 else 0][:, t, :]
                    nc.tensor.matmul(o, hi, whi[:, c, 2, e, :], start=(n == 0 and t == 0), stop=False,
                                     skip_group_check=True)
                    nc.tensor.matmul(o, hi, wlo[:, c, 2, e, :], start=False, stop=False, skip_group_check=True)
                    mm = nc.tensor.matmul(o, lo, whi[:, c, 2, e, :], start=False,
                                          stop=(n == UNITS - 1), skip_group_check=True)
                mm.then_inc(down_done, 1)

            def three(o, lhs, rhs, start, stop):
                nc.tensor.matmul(o, lhs[0], rhs[0], start=start, stop=False)
                nc.tensor.matmul(o, lhs[0], rhs[1], start=False, stop=False)
                return nc.tensor.matmul(o, lhs[1], rhs[0], start=False, stop=stop)

            def mamba(name, s):
                t = s - 1

                def act_did(event):
                    pe.wait_ge(m_act, ACT_M.after(event, t))

                def dve_did(event):
                    pe.wait_ge(m_dve, DVE_M.after(event, t))

                def pool_did(event):
                    pe.wait_ge(m_pool, POOL_M.after(event, t))

                q = int(name.rstrip("ab")[-1]) if name.rstrip("ab")[-1] in "0123456789" else 0
                tok = slice(q * P, (q + 1) * P)
                tokens = (xT_hi[M], xT_lo[M])
                if name == "dt":
                    pe.wait_ge(ln_dve[M], DVE_LN.after("lo", t))
                    cols = slice(DI + CT * P, NPROJ)
                    for b in range(TT):
                        for kk in range(2):
                            mm = three(R[2][:, b * NH:(b + 1) * NH],
                                       [x[:, kk, b * P:(b + 1) * P] for x in tokens],
                                       (win_hi[:, kk, cols], win_lo[:, kk, cols]), kk == 0, kk == 1)
                elif name.startswith("xc"):
                    if q == 0:
                        pe.wait_ge(ln_dve[F], DVE_LN.after("lo", s + 1))
                    elif q == 2:
                        act_did("xc0")
                    for c in range(2):
                        ct = (4 + c) if q == 0 else 2 * (q - 1) + c
                        cols = slice(DI + ct * P, DI + (ct + 1) * P)
                        for kk in range(2):
                            mm = three(R[q % 2][:, c * TILE:(c + 1) * TILE],
                                       (win_hi[:, kk, cols], win_lo[:, kk, cols]),
                                       [x[:, kk, :] for x in tokens], kk == 0, kk == 1)
                elif name == "cum":
                    dve_did("dA")
                    pe.wait_ge(pass_read, s + 1)
                    for n, mat in enumerate((incl, ones, later)):
                        mm = nc.tensor.matmul(R[3][:, n * TT * NH:(n + 1) * TT * NH], mat, sp["dA"][:], start=True, stop=True)
                elif name.startswith("z"):
                    if q == 0:
                        act_did("xc1")
                    else:
                        dve_did("v")
                    for kk in range(2):
                        mm = three(R[1 + q][:, :], [x[:, kk, tok] for x in tokens],
                                   (win_hi[:, kk, 0:DI], win_lo[:, kk, 0:DI]), kk == 0, kk == 1)
                elif name.startswith("seg"):
                    ab = name[-1]
                    pool_did(f"Rl{q}")
                    act_did(("xc2" if q == 0 else "La0") if ab == "a" else ("zh0" if q == 0 else "Lb0"))
                    g = 0 if ab == "a" else 4
                    o = R[0 if ab == "a" else 1][:, :].rearrange("p (h l) -> p h l", h=4)
                    nc.tensor.matmul(o, later16[:], Rh[:, q, g:g + 4, :], start=True, stop=False)
                    mm = nc.tensor.matmul(o, later16[:], Rl[:, q, g:g + 4, :], start=False, stop=True)
                elif name == "bt":
                    dve_did("xs0")
                    act_did("zh1")
                    for b in range(TT):
                        mm = nc.tensor.transpose(R[2][:, b * P:(b + 1) * P], BT[:, b * P:(b + 1) * P], ident)
                elif name == "cb":
                    act_did("ex")
                    for b in range(TT):
                        cols = slice(b * P, (b + 1) * P)
                        mm = nc.tensor.matmul(R[3][:, cols], BT[:, cols], CTr[:, cols], start=True, stop=True)
                elif name.startswith("xt"):
                    dve_did("xs2")
                    act_did("bt" if q == 0 else "La1")
                    for c in range(4):
                        mm = nc.tensor.transpose(R[2 if q == 0 else 0][:, c * P:(c + 1) * P], xs[:, 2 + c, tok], ident)
                elif name.startswith("off"):
                    if q == 0:
                        dve_did("cb")
                        pe.wait_ge(set_pool, 1)
                    else:
                        dve_did("st0")
                    mm = nc.tensor.matmul(R[3][:, :], CTr[:, tok], state[:], start=True, stop=True)
                elif name.startswith("diag"):
                    pool_did(f"M{q}")
                    dve_did("xd0" if q == 0 else "y0")
                    if q == 0:
                        act_did("Lb1")
                    else:
                        dve_did("xd1")
                    for h in range(NH):
                        cols = slice(h * HD, (h + 1) * HD)
                        mm = nc.tensor.matmul(R[1][:, cols], Mm[:, q, h, :], xd[:, q, cols], start=True, stop=True)
                elif name.startswith("state"):
                    pool_did(f"xe{q}")
                    if q == 0:
                        act_did("xt0")
                    else:
                        dve_did("st0")
                    mm = nc.tensor.matmul(R[2][:, :], Bs[:, q, :], xe[:, q, :], start=True, stop=True)
                elif name.startswith("yt"):
                    pool_did(f"yn{q}")
                    if q == 0:
                        act_did("xt1")
                    else:
                        dve_did("y1")
                    for c in range(4):
                        mm = nc.tensor.transpose(R[q][:, c * P:(c + 1) * P], yn[:, q, c * P:(c + 1) * P], ident)
                elif name.startswith("out"):
                    dve_did(f"yl{q}")
                    dve_did("off1" if q == 0 else "out0")
                    for c in range(4):
                        mm = three(R[3][:, 0:D], (yT_hi[:, c, :], yT_lo[:, c, :]),
                                   (wout_hi[:, c, :], wout_lo[:, c, :]), c == 0, c == 3)
                mm.then_inc(m_pe, 1)

            def largest(g):
                w = 1 if g == 0 else 2
                pe.wait_ge(set_dve, SET_DVE_MAX[g])
                nc.tensor.transpose(R[1][0:w, 0:P], mx[:, g:g + w], ident).then_inc(set_pe, 1)
                pe.wait_ge(set_dve, SET_DVE_DIAG[g])
                nc.tensor.matmul(R[1][:, 256:256 + w], ones[0:w, :], mdiag[0:w, 0:w],
                                 start=True, stop=True).then_inc(set_pe, 1)

            pe.wait_ge(s_cst, 16)
            largest(0)
            layer_norm_transpose(F, 0, 0, [])
            for q, (f, n) in enumerate(START_UNITS):
                if (f, n) == (1, 0):
                    layer_norm_transpose(F, 1, 2, [], use=M)
                gate_up_unit(f, n, q, None, start_bank)
                if q >= DOWN_LAG:
                    down_unit(*START_UNITS[q - DOWN_LAG])
                if q == LARGEST_AT:
                    largest(1)
            layer_norm_transpose(F, 2, 0, [])
            for u in START_UNITS[-DOWN_LAG:]:
                down_unit(*u)
            layer_norm_transpose(M, 0, 2, [(ln_dve[F], DVE_LN.after("lo", 1))])

            def step(s, with_mamba, next_ffn):
                f = s + 1
                for n in range(UNITS):
                    gate_up_unit(f, n, n, f * UNITS, unit_bank)
                    if n >= DOWN_LAG:
                        down_unit(f, n - DOWN_LAG)
                    for name in PE_AT.get(n, "").split():
                        if name == "LN_f":
                            if next_ffn:
                                layer_norm_transpose(F, f + 1, 0, [(m_dve, DVE_M.after("yl0", s - 1))] if with_mamba
                                                     else [(ln_dve[F], DVE_LN.after("lo", f))])
                        elif name == "LN_m":
                            if with_mamba:
                                layer_norm_transpose(M, s, 2, [(m_dve, DVE_M.after("st1", s - 1))])
                        elif with_mamba:
                            mamba(name, s)
                for n in range(UNITS - DOWN_LAG, UNITS):
                    down_unit(f, n)

            steps(pe, step)

        @block.scalar
        def _(act):
            def layer_norm_hi(s, index, bank, free, use=None):
                for semaphore, value in free:
                    act.wait_ge(semaphore, value)
                act.wait_ge(ln_pe[s], index + 1)
                nc.scalar.activation(xT_hi[use or s][:].rearrange("p k t -> p (k t)"), R[bank][:, :], ACT.Copy).then_inc(ln_act[s], 1)

            def mamba(name, t):
                def pe_did(event):
                    act.wait_ge(m_pe, PE_M.after(event, t))

                def dve_did(event, tile=t):
                    act.wait_ge(m_dve, DVE_M.after(event, tile))

                q = int(name[-1]) if name[-1] in "0123456789" else 0
                four = lambda ap: ap.rearrange("p (h l) -> p h l", h=4)
                if name.startswith("xc"):
                    if q == 0:
                        dve_did("v")
                    pe_did(name)
                    ins = nc.scalar.activation(xc[:, 2 * q:2 * q + 2, HALO:], R[q % 2][:, :].rearrange("p (c t) -> p c t", c=2),
                                               ACT.Identity, scale=c_in)
                elif name == "spe":
                    dve_did("na")
                    ins = nc.scalar.activation(sp["e"][:], sp["na"][:], ACT.Exp)
                elif name.startswith("th"):
                    dve_did(f"cv{q}_7")
                    ins = nc.scalar.activation(th[:, 2 * q:2 * q + 2, :], cv[:, 2 * q:2 * q + 2, :], ACT.Tanh)
                elif name.startswith("zt"):
                    pe_did(f"z{q}")
                    ins = nc.scalar.activation(zt[:, q, :], R[1 + q][:, :], ACT.Tanh, scale=c_in_half)
                elif name.startswith("zh"):
                    ins = nc.scalar.activation(zh[:, q, :], R[1 + q][:, :], ACT.Identity, scale=c_in_half)
                elif name == "ex":
                    pe_did("cum")
                    ins = nc.scalar.activation(ex[:].rearrange("p n q h -> p (n q h)"), R[3][:, 0:3 * TT * NH], ACT.Exp)
                elif name[0] == "L":
                    g = 0 if name[1] == "a" else 4
                    pe_did(f"seg{q}{name[1]}")
                    ins = nc.scalar.activation(L[:, q, g:g + 4, :], four(R[0 if g == 0 else 1][:, :]), ACT.Exp)
                elif name == "bt":
                    pe_did("bt")
                    ins = nc.scalar.activation(Bs[:].rearrange("p q n -> p (q n)"), R[2][:, 0:TT * P], ACT.Copy)
                elif name.startswith("xt"):
                    pe_did(name)
                    ins = nc.scalar.activation(xt[:, q, :], R[2 if q == 0 else 0][:, :], ACT.Copy)
                elif name.startswith("sq"):
                    dve_did(f"g{q}")
                    ins = nc.scalar.activation(ysq[:], y[:, q, :], ACT.Square, accum_out=yss[:, q:q + 1])
                elif name.startswith("yh"):
                    pe_did(f"yt{q}")
                    if q == 1:
                        pe_did("out0")
                    ins = nc.scalar.activation(yT_hi[:].rearrange("p c l -> p (c l)"), R[q][:, :], ACT.Copy)
                ins.then_inc(m_act, 1)

            def weight_hi(c):
                act.wait_ge(s_full, c + 1)
                nc.scalar.activation(whi[:, c, :, :, :].rearrange("p m k n -> p m n k"),
                                     wfull[:, c % 2, :].rearrange("p (m n k) -> p m n k", m=3, k=2), ACT.Copy).then_inc(s_whi, 1)

            def gelu_unit(number, bank):
                act.wait_ge(gu_done, number + 1)
                nc.scalar.activation(gelu[bank][:], gate_up[bank][:, 0, :], ACT.Gelu_apprx_tanh, scale=c_gate).then_inc(gelu_done, 1)

            def hi_unit(number, place, bank, first):
                act.wait_ge(hidden_done, number + 1)
                if not first:
                    act.wait_ge(down_done, number + 1 - RING)
                nc.scalar.activation(hid_hi[:, place, :], hidden[bank][:], ACT.Copy).then_inc(hi_done, 1)

            layer_norm_hi(F, 0, 0, [])
            weight_hi(0)
            for q, (f, n) in enumerate(START_UNITS):
                if (f, n) == (1, 0):
                    layer_norm_hi(F, 1, 2, [], use=M)
                for c in range(1, CH):
                    if q == max(0, 4 * c - 5):
                        weight_hi(c)
                gelu_unit(q, start_bank(q))
                if q >= 1:
                    hi_unit(q - 1, (q - 1) % RING, start_bank(q - 1), q - 1 < RING)
                if q == LARGEST_AT + 2:
                    act.wait_ge(set_dve, SET_DVE_POW[1])
                    act.wait_ge(s_small, 16 * (4 + 2 * TT))
                    nc.scalar.activation(negA[:], negA[:], ACT.Exp).then_inc(set_act, 1)
                    flat = lambda ap: ap.rearrange("p k n -> p (k n)")
                    nc.scalar.activation(flat(win_hi[:]), flat(win), ACT.Identity, scale=f_in).then_inc(set_act, 1)
                    nc.scalar.activation(flat(wout_hi[:]), flat(wout), ACT.Identity, scale=f_out).then_inc(set_act, 1)
            last = 2 * UNITS - 1
            layer_norm_hi(F, 2, 0, [(gu_done, START_UNITS.index((0, UNITS - 1)) + 1)])
            hi_unit(last, last % RING, start_bank(last), False)
            layer_norm_hi(M, 0, 2, [(gu_done, 2 * UNITS)])

            def step(s, with_mamba, next_ffn):
                f = s + 1
                for n in range(UNITS):
                    gelu_unit(f * UNITS + n, unit_bank(n))
                    if n >= 1:
                        hi_unit(f * UNITS + n - 1, (n - 1) % RING, unit_bank(n - 1), False)
                    for name in ACT_AT.get(n, "").split():
                        if with_mamba:
                            if name == "LN_m":
                                layer_norm_hi(M, s, 2, [(m_pe, PE_M.after("z1", s - 1))])
                            else:
                                mamba(name, s - 1)
                if next_ffn:
                    layer_norm_hi(F, f + 1, 0, [(gu_done, f * UNITS + UNITS)])
                hi_unit(f * UNITS + UNITS - 1, (UNITS - 1) % RING, unit_bank(UNITS - 1), False)

            steps(act, step)

        @block.vector
        def _(dve):
            def wait_apart(semaphore, value):
                dve.wait_ge(semaphore, value)
                if not isinstance(value, int):
                    cell = next(spare_cells)
                    nc.vector.memset(spare_dve[:, cell:cell + 1], 0.0)

            def layer_norm_stats(s, index, use=None):
                use = use or s
                for t in range(TT):
                    nc.vector.bn_stats(stats[use][:, t, :], of_tile(ln_src[s], index)[:, t, :]).then_inc(ln_dve[s], 1)

            def layer_norm_aggregate(s, index, use=None):
                use = use or s
                wait_apart(ln_dve[s], DVE_LN.after("stats1", index))
                for t in range(TT):
                    nc.vector.bn_aggr(aggr[use][:, t, :], stats[use][:, t, :]).then_inc(ln_dve[s], 1)

            def layer_norm_scale(s, index, use=None):
                use = use or s
                dve.wait_ge(ln_pool[s], POOL_LN.after("rstd", index))
                for t in range(TT):
                    nc.vector.tensor_scalar(xn[use][:, t, :], of_tile(ln_src[s], index)[:, t, :], aggr[use][:, t, 0:1],
                                            rstd[use][:, t:t + 1], ALU.subtract, ALU.mult).then_inc(ln_dve[s], 1)

            def layer_norm_lo(s, index, bank, use=None):
                use = use or s
                dve.wait_ge(ln_act[s], index + 1)
                nc.vector.tensor_tensor(xT_lo[use][:].rearrange("p k t -> p (k t)"), R[bank][:, :],
                                        xT_hi[use][:].rearrange("p k t -> p (k t)"), ALU.subtract).then_inc(ln_dve[s], 1)

            def own(name, t):
                dve.wait_ge(m_dve, DVE_M.after(name, t))

            def conv(p, t):
                dve.wait_ge(m_act, ACT_M.after(f"xc{p}", t))
                for k in range(TAPS):
                    for c in range(2):
                        blk = 2 * p + c
                        ct = (4 + c) if p == 0 else 2 * (p - 1) + c
                        src = xc[:, blk, k:k + TILE]
                        if k == 0:
                            ins = nc.vector.tensor_scalar(cv[:, blk, :], src, cw[:, ct, 0:1], cb[:, ct:ct + 1], ALU.mult, ALU.add)
                        else:
                            own(f"cv{p}_{2 * (k - 1) + c}", t)
                            ins = nc.vector.scalar_tensor_tensor(cv[:, blk, :], src, cw[:, ct, k:k + 1], cv[:, blk, :], ALU.mult, ALU.add)
                        ins.then_inc(m_dve, 1)

            def soft_plus(t):
                inc = lambda a: a.then_inc(m_dve, 1)
                dve.wait_ge(m_act, ACT_M.after("spe", t))
                inc(nc.vector.tensor_scalar(sp["e2"][:], sp["e"][:], 2.0, None, ALU.add))
                own("e2", t)
                inc(nc.vector.reciprocal(sp["er"][:], sp["e2"][:]))
                own("er", t)
                inc(nc.vector.tensor_tensor(sp["r"][:], sp["e"][:], sp["er"][:], ALU.mult))
                own("r", t)
                inc(nc.vector.tensor_tensor(sp["r2"][:], sp["r"][:], sp["r"][:], ALU.mult))
                own("r2", t)
                inc(nc.vector.tensor_scalar(spq[0][:], sp["r2"][:], 1.0 / (2 * LOG_TERMS + 1), None, ALU.mult))
                for k in range(1, LOG_TERMS):
                    own(f"q{k - 1}", t)
                    inc(nc.vector.scalar_tensor_tensor(spq[k][:], spq[k - 1][:], 1.0 / (2 * (LOG_TERMS - k) + 1),
                                                       sp["r2"][:], ALU.add, ALU.mult))
                own(f"q{LOG_TERMS - 1}", t)
                inc(nc.vector.scalar_tensor_tensor(sp["l"][:], spq[-1][:], 1.0, sp["r"][:], ALU.add, ALU.mult))
                inc(nc.vector.tensor_scalar(sp["mv"][:], sp["v"][:], 0.0, None, ALU.max))
                own("mv", t)
                inc(nc.vector.scalar_tensor_tensor(sp["dt"][:], sp["l"][:], 2.0, sp["mv"][:], ALU.mult, ALU.add))
                own("dt", t)
                inc(nc.vector.scalar_tensor_tensor(sp["dA"][:], sp["dt"][:], -1.0, negA[:].rearrange("p t h -> p (t h)"),
                                                   ALU.mult, ALU.mult))
                own("dA", t)
                inc(nc.vector.tensor_scalar(dh[:], sp["dA"][:], DECAY_FLOOR, None, ALU.max))
                own("dh", t)
                inc(nc.vector.scalar_tensor_tensor(dl[:], sp["dA"][:], DECAY_FLOOR, dh[:], ALU.max, ALU.subtract))

            def mamba(name, t):
                def pe_did(event):
                    dve.wait_ge(m_pe, PE_M.after(event, t))

                def act_did(event):
                    dve.wait_ge(m_act, ACT_M.after(event, t))

                q = int(name[-1]) if name[-1] in "0123456789" else 0
                by_head = lambda ap: ap.rearrange("p (h d) -> p h d", h=NH)
                heads = lambda ap: ap.rearrange("p (h o) -> p h o", o=1).to_broadcast([P, NH, HD])
                flat = lambda ap: ap.rearrange("p c t -> p (c t)")
                if name.startswith("cv"):
                    return conv(q, t)
                if name == "soft":
                    return soft_plus(t)
                if name == "v":
                    pe_did("dt")
                    ins = nc.vector.scalar_tensor_tensor(sp["v"][:], R[2][:, 0:TT * NH], c_in, dtb[:].rearrange("p t h -> p (t h)"),
                                                         ALU.mult, ALU.add)
                elif name == "na":
                    own("v", t)
                    ins = nc.vector.scalar_tensor_tensor(sp["na"][:], sp["v"][:], -1.0, sp["v"][:], ALU.mult, ALU.min)
                elif name == "halo":
                    own("cv2_7", t)
                    ins = nc.vector.tensor_copy(xc[:, :, 0:HALO], xc[:, :, TILE:TILE + HALO])
                elif name.startswith("xs"):
                    act_did(f"th{q}")
                    sl = slice(2 * q, 2 * q + 2)
                    ins = nc.vector.scalar_tensor_tensor(flat(xs[:, sl, :]), flat(th[:, sl, :]), 1.0, flat(cv[:, sl, :]),
                                                         ALU.add, ALU.mult)
                elif name.startswith("zg"):
                    act_did(f"zh{q}")
                    ins = nc.vector.scalar_tensor_tensor(zg[:, q, :], zt[:, q, :], 1.0, zh[:, q, :], ALU.add, ALU.mult)
                elif name == "cb":
                    pe_did("cb")
                    ins = nc.vector.tensor_tensor(cbm[:], R[3][:, 0:TT * P].rearrange("p (q l) -> p q l", q=TT),
                                                  incl.rearrange("p (o l) -> p o l", o=1).to_broadcast([P, TT, P]), ALU.mult)
                elif name.startswith("xd"):
                    act_did(f"xt{q}")
                    ins = nc.vector.tensor_tensor(by_head(xd[:, q, :]), by_head(xt[:, q, :]), heads(sp["dt"][:, q * NH:(q + 1) * NH]), ALU.mult)
                elif name.startswith("off"):
                    pe_did(f"off{q}")
                    ins = nc.vector.tensor_tensor(by_head(yo[:, q, :]), by_head(R[3][:, :]), heads(ex[:, 0, q, :]), ALU.mult)
                elif name in ("y0", "y1"):
                    pe_did(f"diag{q}")
                    dve.wait_ge(m_pool, POOL_M.after(f"yx{q}", t))
                    ins = nc.vector.tensor_tensor(y[:, q, :], R[1][:, :], yo[:, q, :], ALU.add)
                elif name[0] == "g":
                    own(f"y{q}", t)
                    ins = nc.vector.tensor_tensor(y[:, q, :], y[:, q, :], zg[:, q, :], ALU.mult)
                elif name.startswith("st"):
                    pe_did(f"state{q}")
                    dve.wait_ge(m_pool, POOL_M.after(f"sd{q}", t))
                    ins = nc.vector.tensor_tensor(state[:], R[2][:, :], state[:], ALU.add)
                elif name.startswith("yl"):
                    act_did(f"yh{q}")
                    ins = nc.vector.tensor_tensor(yT_lo[:].rearrange("p c l -> p (c l)"), R[q][:, :],
                                                  yT_hi[:].rearrange("p c l -> p (c l)"), ALU.subtract)
                elif name.startswith("out"):
                    pe_did(f"out{q}")
                    ins = nc.vector.scalar_tensor_tensor(of_tile(ffn_in, t)[:, q, :], R[3][:, 0:D], c_out,
                                                         of_tile(ffn_out, t)[:, q, :], ALU.mult, ALU.add)
                ins.then_inc(m_dve, 1)

            def decode(c):
                dve.wait_ge(s_chunk[c % 2], 16 * 9 * (c // 2 + 1))
                nc.vector.tensor_scalar(t0, pk[:, c % 2, :], 0xFF, 12, ALU.bitwise_and, ALU.logical_shift_left).then_inc(s_step, 1)
                dve.wait_ge(s_step, 3 * c + 1)
                nc.vector.scalar_tensor_tensor(t1, pk[:, c % 2, :], 24, t0, ALU.logical_shift_left, ALU.bitwise_or).then_inc(s_step, 1)
                dve.wait_ge(s_step, 3 * c + 2)
                nc.vector.tensor_scalar(t0, t1, 3, 0x0E000E00, ALU.logical_shift_right, ALU.bitwise_and).then_inc(s_step, 1)
                dve.wait_ge(s_step, 3 * c + 3)
                nc.vector.scalar_tensor_tensor(codes, t1, 0x80008000, t0, ALU.bitwise_and, ALU.bitwise_or).then_inc(s_decoded, 1)

            def weight_full(c):
                dve.wait_ge(s_decoded, c + 1)
                if c >= 2:
                    dve.wait_ge(s_wlo, c - 1)
                    dve.wait_ge(s_wlo_down, c - 1)
                nc.vector.scalar_tensor_tensor(
                    wfull[:, c % 2, :].rearrange("p (n k) -> p n k", k=2),
                    codes.bitcast(F16).rearrange("p (n k) -> p n k", k=2), f_code,
                    sc[:, c % 2, :].rearrange("p (n o) -> p n o", o=1).to_broadcast([P, 3 * WCOL, 2]),
                    ALU.mult, ALU.mult).then_inc(s_full, 1)

            def weight_lo_down(c):
                dve.wait_ge(s_whi, c + 1)
                nc.vector.tensor_tensor(
                    wlo[:, c, 2, :, :].rearrange("p k n -> p n k"),
                    wfull[:, c % 2, :].rearrange("p (m n k) -> p m n k", m=3, k=2)[:, 2, :, :],
                    whi[:, c, 2, :, :].rearrange("p k n -> p n k"), ALU.subtract).then_inc(s_wlo_down, 1)

            def hidden_unit(number, bank, before):
                dve.wait_ge(gelu_done, number + 1)
                if before is not None:
                    dve.wait_ge(lo_done, before + 1)
                nc.vector.scalar_tensor_tensor(hidden[bank][:], gate_up[bank][:, 1, :], c_up, gelu[bank][:], ALU.mult, ALU.mult).then_inc(hidden_done, 1)

            def pass_end(f, units_done, bank=0):
                dve.wait_ge(down_done, units_done)
                flat = lambda ap: ap.rearrange("p t d -> p (t d)")
                nc.vector.scalar_tensor_tensor(flat(of_tile(ffn_out, f)), flat(down_bank[bank][:]), c_down,
                                               flat(of_tile(ffn_in, f)), ALU.mult, ALU.add).then_inc(pass_read, 1)

            done = [0]

            def chained(ins):
                done[0] += 1
                ins.then_inc(set_dve, 1)
                dve.wait_ge(set_dve, done[0])

            chained(nc.vector.memset(half[:], -0.5))
            chained(nc.vector.memset(xc[:, :, 0:HALO], 0.0))
            dve.wait_ge(s_sflat, 16)
            chained(nc.vector.tensor_reduce(mx[:, 0:1], sflat[:], AX.X, ALU.max, apply_absolute_value=True))
            assert done[0] == SET_DVE_MAX[0]
            dve.wait_ge(s_x[0], 16)
            layer_norm_stats(F, 0)
            layer_norm_aggregate(F, 0)

            def powers(g, w):
                dve.wait_ge(set_pe, 2 * g + 1)
                chained(nc.vector.tensor_reduce(mrow[0:w, 0:1], R[1][0:w, 0:P], AX.X, ALU.max))
                chained(nc.vector.tensor_scalar(mdiag[0:w, 0:w], ident[0:w, 0:w], mrow[0:w, 0:1], None, ALU.mult))
                assert done[0] == SET_DVE_DIAG[g]
                dve.wait_ge(set_pe, 2 * g + 2)
                chained(nc.vector.tensor_scalar(pw[:, g:g + w], R[1][:, 256:256 + w], SMALLEST, None, ALU.max))
                chained(nc.vector.tensor_scalar(pw[:, g:g + w].bitcast(U32), pw[:, g:g + w].bitcast(U32), 0x7F800000, None, ALU.bitwise_and))
                chained(nc.vector.reciprocal(pw[:, 3 + g:3 + g + w], pw[:, g:g + w]))

            dve.wait_ge(s_cst, 16)
            powers(0, 1)
            chained(nc.vector.tensor_scalar(f_code, r_ffn, 2.0 ** (CODE_BITS + FFN_BITS), None, ALU.mult))
            layer_norm_scale(F, 0)
            decode(0)
            weight_full(0)
            chained(nc.vector.tensor_scalar(c_gate, m_ffn, 2.0 ** -(FFN_BITS + ACTIVATION_BITS), None, ALU.mult))
            chained(nc.vector.tensor_scalar(c_up, r_ffn, 2.0 ** (HIDDEN_BITS - FFN_BITS - ACTIVATION_BITS), None, ALU.mult))
            chained(nc.vector.tensor_tensor(m_cube, m_ffn, m_ffn, ALU.mult))
            chained(nc.vector.tensor_tensor(m_cube, m_cube, m_ffn, ALU.mult))
            chained(nc.vector.tensor_scalar(c_down, m_cube, 0.5 * 2.0 ** -(FFN_BITS + HIDDEN_BITS), None, ALU.mult))
            assert done[0] == SET_DVE_POW[0], done
            layer_norm_lo(F, 0, 0)
            dve.wait_ge(s_x[1], 16)
            layer_norm_stats(F, 1, use=M)
            weight_lo_down(0)
            layer_norm_aggregate(F, 1, use=M)
            decode(1)
            weight_full(1)
            layer_norm_scale(F, 1, use=M)

            def setup_largest():
                dve.wait_ge(s_small, 16 * (4 + 2 * TT))
                dve.wait_ge(s_win, 16)
                dve.wait_ge(s_wout, 16)
                for k in range(4):
                    chained(nc.vector.tensor_scalar(wout[:, k, :], wout[:, k, :], nw[:, k:k + 1], None, ALU.mult))
                chained(nc.vector.tensor_scalar(cw[:], cw[:], 0.5, None, ALU.mult))
                chained(nc.vector.tensor_scalar(cb[:], cb[:], 0.5, None, ALU.mult))
                chained(nc.vector.tensor_copy(incl16[:], incl))
                chained(nc.vector.tensor_copy(later16[:], later))
                chained(nc.vector.tensor_reduce(mx[:, 1:2], win.rearrange("p k n -> p (k n)"), AX.X, ALU.max, apply_absolute_value=True))
                chained(nc.vector.tensor_reduce(mx[:, 2:3], wout.rearrange("p k n -> p (k n)"), AX.X, ALU.max, apply_absolute_value=True))
                chained(nc.vector.memset(pw[:, 13:15], 0.0))
                assert done[0] == SET_DVE_MAX[1], done

            def setup_powers():
                powers(1, 2)
                chained(nc.vector.tensor_scalar(pw[:, 13:15], pw[:, 4:6], 2.0 ** PROJ_BITS, None, ALU.mult))
                chained(nc.vector.tensor_scalar(c_in, m_in, 2.0 ** -(PROJ_BITS + ACTIVATION_BITS), None, ALU.mult))
                chained(nc.vector.tensor_scalar(c_in_half, m_in, 2.0 ** -(PROJ_BITS + ACTIVATION_BITS + 1), None, ALU.mult))
                chained(nc.vector.tensor_scalar(c_out, m_out, 2.0 ** -(PROJ_BITS + ACTIVATION_BITS), None, ALU.mult))
                assert done[0] == SET_DVE_POW[1], done

            def setup_lo():
                dve.wait_ge(set_act, 3)
                flat = lambda ap: ap.rearrange("p k n -> p (k n)")
                chained(nc.vector.scalar_tensor_tensor(flat(win_lo[:]), flat(win), f_in, flat(win_hi[:]), ALU.mult, ALU.subtract))
                chained(nc.vector.scalar_tensor_tensor(flat(wout_lo[:]), flat(wout), f_out, flat(wout_hi[:]), ALU.mult, ALU.subtract))
                assert done[0] == SET_DVE_END

            first_out = START_UNITS.index((0, UNITS - 1)) + DOWN_LAG
            for q, (f, n) in enumerate(START_UNITS):
                if (f, n) == (1, 0):
                    layer_norm_lo(F, 1, 2, use=M)
                for c in range(2, CH):
                    if q == max(0, 4 * c - 9):
                        decode(c)
                    if q == max(1, 4 * c - 8):
                        weight_full(c)
                for c in range(1, CH):
                    if q == max(0, 4 * c - 5):
                        weight_lo_down(c)
                before = before_in_bank(q, start_bank)
                hidden_unit(q, start_bank(q), before if before >= 0 else None)
                if q == LARGEST_AT:
                    setup_largest()
                    setup_powers()
                if q == LARGEST_AT + 4:
                    setup_lo()
                    dve.wait_ge(s_x[2], 16 * (NT - 2))
                    layer_norm_stats(F, 2)
                    layer_norm_aggregate(F, 2)
                if q == LARGEST_AT + 5:
                    layer_norm_scale(F, 2)
                if q == first_out:
                    pass_end(0, START_UNITS.index((0, UNITS - 1)) + 1)
                    dve.wait_ge(pass_read, 1)
                    layer_norm_stats(M, 0)
                    layer_norm_aggregate(M, 0)
            layer_norm_lo(F, 2, 0)
            layer_norm_scale(M, 0)
            layer_norm_lo(M, 0, 2)
            pass_end(1, 2 * UNITS, bank=1)

            def step(s, with_mamba, next_ffn):
                f = s + 1
                for n in range(UNITS):
                    hidden_unit(f * UNITS + n, unit_bank(n), f * UNITS + before_in_bank(n, unit_bank))
                    for name in DVE_AT.get(n, "").split():
                        if name == "stats":
                            if with_mamba:
                                wait_apart(m_dve, DVE_M.after("st1", s - 1))
                                wait_apart(pass_read, s + 1)
                                layer_norm_stats(M, s)
                            elif next_ffn:
                                dve.wait_ge(m_dve, DVE_M.after("out1", NT - 1))
                            if next_ffn:
                                layer_norm_stats(F, f + 1)
                            if with_mamba:
                                layer_norm_aggregate(M, s)
                            if next_ffn:
                                layer_norm_aggregate(F, f + 1)
                        elif name == "scale":
                            if with_mamba:
                                layer_norm_scale(M, s)
                            if next_ffn:
                                layer_norm_scale(F, f + 1)
                        elif with_mamba:
                            if name == "LN_m":
                                layer_norm_lo(M, s, 2)
                            else:
                                mamba(name, s - 1)
                if next_ffn:
                    layer_norm_lo(F, f + 1, 0)
                pass_end(f, f * UNITS + UNITS)

            steps(dve, step)

        @block.gpsimd
        def _(pool):
            def wait_apart(semaphore, value):
                pool.wait_ge(semaphore, value)
                if not isinstance(value, int):
                    cell = next(spare_cells)
                    nc.gpsimd.tensor_tensor(spare_pool[:, cell:cell + 1], half[:], half[:], ALU.add)

            def layer_norm_rstd(s, index, use=None):
                use = use or s
                wait_apart(ln_dve[s], DVE_LN.after("aggr1", index))
                g = 2.0 ** (-2 * ACTIVATION_BITS)
                nc.gpsimd.tensor_scalar(ve[use][:], aggr[use][:, :, 1], EPS, g, ALU.add, ALU.mult).then_inc(ln_pool[s], 1)
                pool.wait_ge(ln_pool[s], POOL_LN.after("ve", index))
                nc.gpsimd.tensor_tensor(rstd[use][:], ve[use][:], half[:].to_broadcast([P, TT]), ALU.pow).then_inc(ln_pool[s], 1)

            def mamba(name, t):
                def pe_did(event):
                    pool.wait_ge(m_pe, PE_M.after(event, t))

                def act_did(event):
                    pool.wait_ge(m_act, ACT_M.after(event, t))

                def dve_did(event):
                    pool.wait_ge(m_dve, DVE_M.after(event, t))

                q = int(name[-1])
                by_head = lambda ap: ap.rearrange("p (h d) -> p h d", h=NH)
                heads = lambda ap, n: ap.rearrange("p (h o) -> p h o", o=1).to_broadcast([P, NH, n])
                over = lambda ap: ap.rearrange("p (o l) -> p o l", o=1).to_broadcast([P, NH, P])
                if name[0] == "R":
                    part = Rh if name[1] == "h" else Rl
                    dve_did("dl")
                    d = (dh if name[1] == "h" else dl)[:, q * NH:(q + 1) * NH]
                    ins = nc.gpsimd.tensor_tensor(part[:, q, :, :], over(incl16[:]), heads(d, P), ALU.mult)
                elif name[0] == "M":
                    act_did(f"Lb{q}")
                    dve_did("cb")
                    ins = nc.gpsimd.tensor_tensor(Mm[:, q, :, :], L[:, q, :, :], over(cbm[:, q, :]), ALU.mult)
                elif name[:2] == "xD":
                    act_did(f"xt{q}")
                    ins = nc.gpsimd.tensor_tensor(by_head(xD[:, q, :]), by_head(xt[:, q, :]), heads(dsk[:], HD), ALU.mult)
                elif name[:2] == "xe":
                    dve_did(f"xd{q}")
                    ins = nc.gpsimd.tensor_tensor(by_head(xe[:, q, :]), by_head(xd[:, q, :]), heads(ex[:, 2, q, :], HD), ALU.mult)
                elif name[:2] == "yx":
                    dve_did(f"off{q}")
                    pool.wait_ge(m_pool, POOL_M.after(f"xD{q}", t))
                    ins = nc.gpsimd.tensor_tensor(yo[:, q, :], yo[:, q, :], xD[:, q, :], ALU.add)
                elif name[:2] == "sd":
                    pe_did(f"off{q}")
                    ins = nc.gpsimd.tensor_tensor(by_head(state[:]), by_head(state[:]), heads(ex[:, 1, q, :], HD), ALU.mult)
                elif name[:2] == "ve":
                    wait_apart(m_act, ACT_M.after(f"sq{q}", t))
                    ins = nc.gpsimd.tensor_scalar(yve[:, q:q + 1], yss[:, q:q + 1], 1.0 / DI, EPS, ALU.mult, ALU.add)
                elif name[:2] == "rs":
                    pool.wait_ge(m_pool, POOL_M.after(f"ve{q}", t))
                    ins = nc.gpsimd.tensor_tensor(yrs[:, q:q + 1], yve[:, q:q + 1], half[:], ALU.pow)
                elif name[:2] == "yn":
                    wait_apart(m_pool, POOL_M.after(f"rs{q}", t))
                    ins = nc.gpsimd.tensor_scalar(yn[:, q, :], y[:, q, :], yrs[:, q:q + 1], 2.0 ** ACTIVATION_BITS, ALU.mult, ALU.mult)
                ins.then_inc(m_pool, 1)

            def lo_unit(number, place, bank):
                pool.wait_ge(hi_done, number + 1)
                nc.gpsimd.tensor_tensor(hid_lo[:, place, :], hidden[bank][:], hid_hi[:, place, :],
                                        ALU.subtract).then_inc(lo_done, 1)

            def weight_lo(c):
                pool.wait_ge(s_whi, c + 1)
                for mat in range(2):
                    ins = nc.gpsimd.tensor_tensor(
                        wlo[:, c, mat, :, :].rearrange("p k n -> p n k"),
                        wfull[:, c % 2, :].rearrange("p (m n k) -> p m n k", m=3, k=2)[:, mat, :, :],
                        whi[:, c, mat, :, :].rearrange("p k n -> p n k"), ALU.subtract)
                ins.then_inc(s_wlo, 1)

            nc.gpsimd.memset(state[:], 0.0).then_inc(set_pool, 1)
            pool.wait_ge(set_dve, 1)
            layer_norm_rstd(F, 0)
            weight_lo(0)
            layer_norm_rstd(F, 1, use=M)
            for q in range(2 * UNITS):
                for c in range(1, CH):
                    if q == max(0, 4 * c - 5):
                        weight_lo(c)
                if q >= 1:
                    lo_unit(q - 1, (q - 1) % RING, start_bank(q - 1))
                if q == LARGEST_AT + 4:
                    layer_norm_rstd(F, 2)
            layer_norm_rstd(M, 0)
            last = 2 * UNITS - 1
            lo_unit(last, last % RING, start_bank(last))

            def step(s, with_mamba, next_ffn):
                f = s + 1
                for n in range(UNITS):
                    if n >= 1:
                        lo_unit(f * UNITS + n - 1, (n - 1) % RING, unit_bank(n - 1))
                    for name in POOL_AT.get(n, "").split():
                        if name == "rstd":
                            if with_mamba:
                                layer_norm_rstd(M, s)
                            if next_ffn:
                                layer_norm_rstd(F, f + 1)
                        elif with_mamba:
                            mamba(name, s - 1)
                lo_unit(f * UNITS + UNITS - 1, (UNITS - 1) % RING, unit_bank(UNITS - 1))

            steps(pool, step)


SET_DVE_MAX = (3, 25)
SET_DVE_DIAG = (5, 27)
SET_DVE_POW = (14, 34)
SET_DVE_END = 36


def kernel(L0_attn_u, L0_attn_in_proj_w, L0_attn_conv_w, L0_attn_conv_b, L0_attn_dt_bias, L0_attn_A_log,
           L0_attn_D_skip, L0_attn_norm_w, L0_attn_out_proj_w, L0_ffn_gate_W_packed, L0_ffn_gate_scales,
           L0_ffn_up_W_packed, L0_ffn_up_scales, L0_ffn_down_W_packed, L0_ffn_down_scales):
    import concourse.bacc as bacc
    from concourse.bass_utils import run_bass_kernel_spmd

    def rows(a, last):
        return np.asarray(a).reshape(CH, P, 2, last).transpose(3, 0, 2, 1).reshape(last, CH, 2 * P)

    def cols(a, per):
        return np.asarray(a).reshape(D, CH, per).transpose(2, 1, 0)

    packed = np.stack([rows(L0_ffn_gate_W_packed, P), rows(L0_ffn_up_W_packed, P),
                       cols(L0_ffn_down_W_packed, P)], axis=2)
    scales = np.stack([rows(L0_ffn_gate_scales, 8), rows(L0_ffn_up_scales, 8),
                       cols(L0_ffn_down_scales, 8)], axis=2)
    w_in = np.asarray(L0_attn_in_proj_w).T.reshape(P, 2, NPROJ)
    at = np.arange(P)
    consts = np.stack([at[:, None] == at, at[:, None] <= at, at[:, None] > at, np.ones((P, P), bool)], axis=1).astype(np.float32)
    arrays = {
        "x": np.asarray(L0_attn_u),
        "packed": packed,
        "scales": scales,
        "w_in": w_in,
        "conv_w": np.asarray(L0_attn_conv_w).reshape(CT, P, TAPS).transpose(1, 0, 2),
        "conv_b": np.asarray(L0_attn_conv_b).reshape(CT, P).T,
        "dt_bias": np.asarray(L0_attn_dt_bias),
        "A_log": np.asarray(L0_attn_A_log),
        "D_skip": np.asarray(L0_attn_D_skip),
        "norm_w": np.asarray(L0_attn_norm_w).reshape(4, P).T,
        "w_out": np.asarray(L0_attn_out_proj_w).T.reshape(4, P, D).transpose(1, 0, 2),
        "consts": consts,
    }
    arrays = {k: np.ascontiguousarray(v) for k, v in arrays.items()}
    nc = bacc.Bacc("TRN2", target_bir_lowering=False, num_devices=1)
    args = [nc.dram_tensor(k, v.shape, mybir.dt.from_np(v.dtype), kind="ExternalInput").ap() for k, v in arrays.items()]
    out = nc.dram_tensor("out", (1, SEQ, D), F32, kind="ExternalOutput").ap()
    macaron(nc, *args, out)
    result = run_bass_kernel_spmd(nc, [arrays], core_ids=[0])
    return result.results[0]["out"]
```

```python
from contextlib import ExitStack

import numpy as np

import concourse.bass as bass
from concourse import mybir

P = 128
SEQ = 1024
D = 256
TILE = 256
TT = TILE // P
NT = SEQ // TILE
MLP = 2048
UNITS = MLP // P
CH = UNITS // 2
WCOL = 256
DI = 512
NH = 8
HD = DI // NH
CT = 6
TAPS = 4
NPROJ = 2 * DI + 2 * P + NH
EPS = 1e-5

F32 = mybir.dt.float32
F16 = mybir.dt.float16
I32 = mybir.dt.int32
U32 = mybir.dt.uint32
ALU = mybir.AluOpType
ACT = mybir.ActivationFunctionType
AX = mybir.AxisListType

ACTIVATION_BITS = 10
FFN_BITS = 12
PROJ_BITS = 14
HIDDEN_BITS = -8
SMALLEST = 2.0 ** -30
CODE_BITS = 14
LOG_TERMS = 6
DECAY_FLOOR = -60000.0

START_UNITS = ([(f, n) for c in range(CH - 3) for f in range(2) for n in (2 * c, 2 * c + 1)]
               + [(0, UNITS - 6), (0, UNITS - 5), (1, UNITS - 6), (0, UNITS - 4), (0, UNITS - 3),
                  (1, UNITS - 5), (0, UNITS - 2), (0, UNITS - 1)]
               + [(1, n) for n in range(UNITS - 4, UNITS)])


def first_unit(c):
    return START_UNITS.index((0, 2 * c))


def pool_matrices(c):
    return min(c, 2)


def lo_parts_done(c):
    by_pool = sum(pool_matrices(b) for b in range(c + 1))
    return by_pool, 3 * (c + 1) - by_pool


def unit_bank(q):
    return 1 if q == UNITS - 1 else q % 3


def start_bank(q):
    return q % 3


def before_in_bank(q, bank):
    earlier = [u for u in range(q) if bank(u) == bank(q)]
    return earlier[-1] if earlier else (-2, -1, -2)[bank(q)]


DOWN_LAG = 3
FIRST_OUT = START_UNITS.index((0, UNITS - 1)) + DOWN_LAG
SCALE_AT = 10
LARGEST_AT = 25
RING = 4

F, M, E = "f", "m", "e"


def turn(kind, index):
    if kind == M:
        return index
    if kind == E or isinstance(index, int) and index == 0:
        return 0
    return index - 1


class Order:

    def __init__(self, names):
        self.names = names.split()
        assert len(set(self.names)) == len(self.names)

    def after(self, name, tile):
        return tile * len(self.names) + self.names.index(name) + 1


PE_M = Order("dt xc0 xc1 xc2 z0 cum z1 seg0a seg0b bt cb seg1a seg1b off0 xt0 xt1 diag0 "
             "state0 diag1 off1 state1 yt0 yt1 out0 out1")
ACT_M = Order("xc0 spe xc1 xc2 th0 zt0 zh0 th1 zt1 zh1 ex La0 Lb0 bt th2 La1 Lb1 xt0 xt1 sq0 "
              "sq1 yh0 yh1")
CONV = [f"cv{p}_{k}" for p in range(3) for k in range(2 * TAPS)]
DVE_M = Order(" ".join(["v", "na", "e2", "er", "r", "r2"]
                       + [f"q{k}" for k in range(LOG_TERMS)] + ["l", "mv", "dt", "dA", "dh", "dl"]
                       + CONV[:12] + ["xs0"] + CONV[12:] + ["halo", "xs1", "zg0", "zg1", "cb", "xs2",
                          "xd0", "xe0", "off0", "yx0", "xd1", "xe1", "y0", "st0", "g0",
                          "off1", "yx1", "y1", "g1", "st1",
                          "yl0", "yl1", "out0", "out1"]))
POOL_M = Order("Rh0 Rl0 Rh1 Rl1 M0 sd0 xD0 M1 xD1 sd1 ve0 rs0 yn0 ve1 rs1 yn1")
DVE_LN = Order("stats0 stats1 aggr0 aggr1 xn0 xn1 lo")
POOL_LN = Order("ve rstd")

PE_AT = {0: "dt xc0", 1: "xc1", 2: "xc2", 3: "z0 cum", 4: "z1", 5: "seg0a seg0b bt",
         6: "cb seg1a seg1b", 7: "off0 xt0", 8: "xt1", 9: "diag0 state0", 10: "diag1 off1",
         11: "state1", 12: "yt0", 13: "yt1", 14: "out0 LN_m LN_f", 15: "out1"}
ACT_AT = {0: "xc0 spe", 1: "xc1", 2: "xc2 th0", 3: "zt0 zh0 th1", 4: "zt1 zh1",
          5: "ex La0 Lb0 bt", 6: "th2 La1 Lb1", 7: "xt0", 8: "xt1", 10: "sq0", 11: "sq1", 12: "yh0",
          13: "yh1", 14: "LN_m"}
DVE_AT = {0: "v na soft", 2: "cv0a cv0b cv1a", 3: "xs0 cv1b cv2a", 4: "cv2b halo xs1", 5: "zg0 zg1",
          6: "cb xs2", 7: "xd0 xe0", 8: "off0 yx0 xd1 xe1", 9: "y0 st0 g0", 10: "off1 yx1 y1 g1",
          11: "st1 stats", 12: "scale yl0", 13: "yl1", 14: "out0 LN_m", 15: "out1"}
POOL_AT = {2: "Rh0 Rl0", 3: "Rh1 Rl1", 6: "M0", 7: "sd0 xD0", 8: "M1", 9: "xD1",
           10: "sd1 ve0 rs0 yn0", 11: "ve1 rs1 yn1 rstd"}


def steps(engine, step):
    with engine.Fori(1, NT + 1) as s:
        step(s, True, True)
    step(NT + 1, False, True)
    step(NT + 2, False, False)


def macaron(nc, x, packed, scales, w_in, conv_w, conv_b, dt_bias, A_log, D_skip, norm_w, w_out,
            consts, out):
    with ExitStack() as ctx:
        def sb(name, shape, dt=F32):
            return ctx.enter_context(nc.sbuf_tensor(name, shape, dt))

        def sem(name):
            return ctx.enter_context(nc.semaphore(name))

        gate_up = [ctx.enter_context(nc.psum_tensor(f"gate_up{b}", [P, 2, TILE], F32)) for b in range(3)]
        down = ctx.enter_context(nc.psum_tensor("down", [P, TT, D], F32))
        R = [ctx.enter_context(nc.psum_tensor(f"mixed{b}", [P, 512], F32)) for b in range(4)]

        cst = sb("cst", [P, 4, P])
        ident, incl, later, ones = (cst[:, n, :] for n in range(4))
        incl16 = sb("incl16", [P, P], F16)
        later16 = sb("later16", [P, P], F16)
        half = sb("half", [P, 1])
        spare_dve, spare_pool = sb("spare_dve", [P, 64]), sb("spare_pool", [P, 64])
        spare_cells = iter(range(64))
        WORDS = 3 * WCOL
        work_area = sb("work_area", [P, 11 * WORDS])

        def part(at, n, dt=F32):
            return work_area[:, at:at + n].bitcast(dt) if dt != F32 else work_area[:, at:at + n]

        pk = part(0, 2 * WORDS, U32).rearrange("p (c n) -> p c n", c=2)
        sc = part(2 * WORDS, 2 * WORDS).rearrange("p (c n) -> p c n", c=2)
        t0, t1 = part(4 * WORDS, WORDS, U32), part(5 * WORDS, WORDS, U32)
        codes = part(6 * WORDS, WORDS, U32)
        wfull = part(7 * WORDS, 4 * WORDS).rearrange("p (c n) -> p c n", c=2)
        whi = sb("whi", [P, CH, 3, 2, WCOL], F16)
        wlo = sb("wlo", [P, CH, 3, 2, WCOL], F16)
        sflat = sb("sflat", [P, 3 * P])
        mx = sb("mx", [P, 4])
        mrow = sb("mrow", [4, 4])
        mdiag = sb("mdiag", [4, 4])
        pw = sb("pw", [P, 16])
        w_in_area = sb("w_in_area", [P, 2 * NPROJ])
        win = w_in_area[:, :].rearrange("p (k n) -> p k n", k=2)
        win_hi = sb("win_hi", [P, 2, NPROJ], F16)
        win_lo = sb("win_lo", [P, 2, NPROJ], F16)
        w_out_area = sb("w_out_area", [P, 4 * D])
        wout = w_out_area[:, :].rearrange("p (k n) -> p k n", k=4)
        wout_hi = sb("wout_hi", [P, 4, D], F16)
        wout_lo = sb("wout_lo", [P, 4, D], F16)
        cw = sb("cw", [P, CT, TAPS])
        cb = sb("cb", [P, CT])
        nw = sb("nw", [P, 4])
        dtb = sb("dtb", [P, TT, NH])
        A_raw = sb("A_raw", [P, TT, NH])
        A_exp = sb("A_exp", [P, TT, NH])
        dsk = sb("dsk", [P, NH])

        ffn_in = sb("ffn_in", [P, NT * TT * D])
        ffn_out = sb("ffn_out", [P, NT * TT * D])

        def of_tile(buffer, t):
            at = (t % NT) * (TT * D)
            cols = buffer[:, at:at + TT * D] if isinstance(t, int) else buffer[:, bass.ds(at, TT * D)]
            return cols.rearrange("p (t d) -> p t d", t=TT)

        ln_src = {F: ffn_in, E: ffn_in, M: ffn_out}
        stats = {s: sb(f"stats_{s}", [P, TT, 6]) for s in (F, M)}
        aggr = {s: sb(f"aggr_{s}", [P, TT, 2]) for s in (F, M)}
        ve = {s: sb(f"ve_{s}", [P, TT]) for s in (F, M)}
        rstd = {s: sb(f"rstd_{s}", [P, TT]) for s in (F, M)}
        xn = {s: sb(f"xn_{s}", [P, TT, D]) for s in (F, M)}
        xT_hi = {s: sb(f"xT_hi_{s}", [P, 2, TILE], F16) for s in (F, M)}
        xT_lo = {s: sb(f"xT_lo_{s}", [P, 2, TILE], F16) for s in (F, M)}
        for buffers in (stats, aggr, ve, rstd, xn, xT_hi, xT_lo):
            buffers[E] = buffers[M]

        gelu = [sb(f"gelu{b}", [P, TILE]) for b in range(3)]
        hidden = [sb(f"hidden{b}", [P, TILE]) for b in range(3)]
        hid_hi = sb("hid_hi", [P, RING, TILE], F16)
        hid_lo = sb("hid_lo", [P, RING, TILE], F16)

        HALO = TAPS - 1
        xc = sb("xc", [P, CT, HALO + TILE])
        cv = part(0, CT * TILE).rearrange("p (c t) -> p c t", c=CT)
        th = part(CT * TILE, CT * TILE).rearrange("p (c t) -> p c t", c=CT)
        xs = th
        BT, CTr = xs[:, 0, :], xs[:, 1, :]
        MORE = 2 * CT * TILE
        zt = part(MORE, TT * DI).rearrange("p (t d) -> p t d", t=TT)
        zh = part(MORE + TT * DI, TT * DI).rearrange("p (t d) -> p t d", t=TT)
        MORE += 2 * TT * DI
        zg = zt
        sp = {n: sb(f"sp_{n}", [P, TT * NH]) for n in "v na e e2 er r r2 l mv dt dA".split()}
        spq = [sb(f"sp_q{k}", [P, TT * NH]) for k in range(LOG_TERMS)]
        dh = sb("dh", [P, TT * NH], F16)
        dl = sb("dl", [P, TT * NH], F16)
        Rh = sb("Rh", [P, TT, NH, P], F16)
        Rl = sb("Rl", [P, TT, NH, P], F16)
        ex = sb("ex", [P, 3, TT, NH])
        L = part(MORE, TT * NH * P).rearrange("p (q h l) -> p q h l", q=TT, h=NH)
        MORE += TT * NH * P
        assert MORE <= 11 * WORDS
        cbm = sb("cbm", [P, TT, P])
        Mm = w_in_area[:, 0:TT * NH * P].rearrange("p (q h l) -> p q h l", q=TT, h=NH)
        Bs = sb("Bs", [P, TT, P])
        xt = sb("xt", [P, TT, DI])
        xd = sb("xd", [P, TT, DI])
        xe = sb("xe", [P, TT, DI])
        xD = sb("xD", [P, TT, DI])
        state = sb("state", [P, DI])
        yo = sb("yo", [P, TT, DI])
        y = w_out_area[:, :].rearrange("p (t d) -> p t d", t=TT)
        ysq = sb("ysq", [P, TT, DI])
        yss = sb("yss", [P, TT])
        yve = sb("yve", [P, TT])
        yrs = sb("yrs", [P, TT])
        yn = sb("yn", [P, TT, DI])
        yT_hi = sb("yT_hi", [P, TT, 4, P], F16)
        yT_lo = sb("yT_lo", [P, TT, 4, P], F16)

        s_sflat, s_cst, s_small, s_win, s_wout = map(sem, "sflat_in cst_in small_in win_in wout_in".split())
        s_words = [sem("words_in0"), sem("words_in1")]
        s_scales = [sem("scales_in0"), sem("scales_in1")]
        s_x = [sem("x0_in"), sem("x1_in"), sem("x_rest_in")]
        s_out = sem("out_stored")
        set_dve, set_pe, set_act, set_pool = map(sem, "setup_dve setup_pe setup_act setup_pool".split())
        s_decoded, s_full, s_whi, s_wlo_pool, s_wlo_dve = map(
            sem, "codes_ready wfull_ready whi_ready wlo_by_pool wlo_by_dve".split())
        s_step = sem("decode_step")
        gu_done, gelu_done, hidden_done, hi_done, lo_done, down_done, pass_read = map(
            sem, "gate_up_done gelu_done hidden_done hidden_hi_done hidden_lo_done down_done pass_read".split())
        m_pe, m_act, m_dve, m_pool = map(sem, "mamba_pe mamba_act mamba_dve mamba_pool".split())
        ln_dve = {s: sem(f"ln_dve_{s}") for s in (F, M, E)}
        ln_pool = {s: sem(f"ln_pool_{s}") for s in (F, M, E)}
        ln_pe = {s: sem(f"ln_pe_{s}") for s in (F, M, E)}
        ln_act = {s: sem(f"ln_act_{s}") for s in (F, M, E)}

        m_ffn, m_in, m_out = (pw[:, n:n + 1] for n in range(3))
        r_ffn, r_in, r_out = (pw[:, 3 + n:4 + n] for n in range(3))
        f_code = pw[:, 6:7]
        c_gate = pw[:, 7:8]
        c_up = pw[:, 8:9]
        c_down = pw[:, 9:10]
        c_in = pw[:, 10:11]
        c_in_half = pw[:, 11:12]
        c_out = pw[:, 12:13]
        f_in = pw[:, 13:14]
        f_out = pw[:, 14:15]
        m_cube = pw[:, 15:16]

        x_t = x.rearrange("o (n t p) d -> (o n) p t d", p=P, t=TT)
        out_t = out.rearrange("o (n t p) d -> (o n) p t d", p=P, t=TT)

        down_bank = [down, R[3][:, :].rearrange("p (t d) -> p t d", t=TT)]

        def unit_number(f, n):
            return START_UNITS.index((f, n)) if isinstance(f, int) and f < 2 else f * UNITS + n

        block = ctx.enter_context(nc.Block())

        @block.sync
        def _(sync):
            def words(c):
                if c >= 2:
                    sync.wait_ge(s_decoded, c - 1)
                sync.dma_start(pk[:, c % 2, :].bitcast(I32), packed[:, c]).then_inc(s_words[c % 2], 16)

            def chunk_scales(c):
                if c >= 2:
                    sync.wait_ge(s_full, c - 1)
                sync.dma_start(sc[:, c % 2, :],
                               scales[:, c].rearrange("b m (o n) -> b o (m n)", o=1).to_broadcast([8, 16, 3 * WCOL])
                               ).then_inc(s_scales[c % 2], 16)

            sync.dma_start(sflat[:], scales.rearrange("b c m n -> (b c m n)").rearrange("(p f) -> p f", p=P)).then_inc(s_sflat, 16)
            words(0)
            sync.dma_start(cst[:], consts).then_inc(s_cst, 16)
            sync.dma_start(of_tile(ffn_in, 0), x_t[0]).then_inc(s_x[0], 16)
            chunk_scales(0)
            sync.dma_start(of_tile(ffn_in, 1), x_t[1]).then_inc(s_x[1], 16)
            words(1)
            chunk_scales(1)
            words(2)
            chunk_scales(2)
            words(3)
            for t in range(2, NT):
                sync.dma_start(of_tile(ffn_in, t), x_t[t]).then_inc(s_x[2], 16)
            sync.dma_start(cw[:], conv_w).then_inc(s_small, 16)
            sync.dma_start(cb[:], conv_b).then_inc(s_small, 16)
            sync.dma_start(nw[:], norm_w).then_inc(s_small, 16)
            for t in range(TT):
                sync.dma_start(dtb[:, t, :], dt_bias.partition_broadcast(P)).then_inc(s_small, 16)
                sync.dma_start(A_raw[:, t, :], A_log.partition_broadcast(P)).then_inc(s_small, 16)
            sync.dma_start(dsk[:], D_skip.partition_broadcast(P)).then_inc(s_small, 16)
            chunk_scales(3)
            sync.dma_start(win, w_in).then_inc(s_win, 16)
            sync.dma_start(wout, w_out).then_inc(s_wout, 16)
            for c in range(4, CH):
                words(c)
                chunk_scales(c)
            with sync.Fori(0, NT) as t:
                sync.wait_ge(pass_read, NT + 1 + t)
                sync.dma_start(out_t[bass.ds(t, 1)].rearrange("o p t d -> p (o t) d"), of_tile(ffn_out, t)).then_inc(s_out, 16)
            sync.wait_ge(s_out, 16 * NT)

        @block.tensor
        def _(pe):
            def layer_norm_transpose(s, index, bank, free):
                pe.wait_ge(ln_dve[s], DVE_LN.after("xn1", turn(s, index)))
                for semaphore, value in free:
                    pe.wait_ge(semaphore, value)
                for t in range(TT):
                    for kk in range(2):
                        mm = nc.tensor.transpose(R[bank][:, kk * TILE + t * P:kk * TILE + (t + 1) * P],
                                                 xn[s][:, t, kk::2], ident)
                mm.then_inc(ln_pe[s], 1)

            def gate_up_unit(f, n, q, base, bank):
                start = base is None
                kind = E if start and f == 1 else F
                if n == 0:
                    pe.wait_ge(ln_dve[kind], DVE_LN.after("lo", turn(kind, f)))
                before = before_in_bank(q, bank)
                if not start:
                    pe.wait_ge(hidden_done, base + before + 1)
                elif before >= 0:
                    pe.wait_ge(hidden_done, before + 1)
                if start and f == 0 and n % 2 == 0:
                    pool_lo, dve_lo = lo_parts_done(n // 2)
                    if pool_lo:
                        pe.wait_ge(s_wlo_pool, pool_lo)
                    pe.wait_ge(s_wlo_dve, dve_lo - 1)
                c, e = n // 2, n % 2
                for mat in range(2):
                    o = gate_up[bank(q)][:, mat, :]
                    for kk in range(2):
                        hi = whi[:, c, mat, kk, e * P:(e + 1) * P]
                        lo = wlo[:, c, mat, kk, e * P:(e + 1) * P]
                        nc.tensor.matmul(o, hi, xT_hi[kind][:, kk, :], start=(kk == 0), stop=False)
                        nc.tensor.matmul(o, hi, xT_lo[kind][:, kk, :], start=False, stop=False)
                        mm = nc.tensor.matmul(o, lo, xT_hi[kind][:, kk, :], start=False, stop=(kk == 1))
                mm.then_inc(gu_done, 1)

            def down_unit(f, n):
                pe.wait_ge(lo_done, unit_number(f, n) + 1)
                start = isinstance(f, int) and f < 2
                if n == 0 and not start:
                    pe.wait_ge(pass_read, f)
                c, e, place = n // 2, n % 2, unit_number(f, n) % RING if start else n % RING
                if start and f == 0 and e == 0:
                    pe.wait_ge(s_wlo_dve, lo_parts_done(c)[1])
                for t in range(TT):
                    hi = hid_hi[:, place, t * P:(t + 1) * P]
                    lo = hid_lo[:, place, t * P:(t + 1) * P]
                    o = down_bank[1 if start and f == 0 else 0][:, t, :]
                    nc.tensor.matmul(o, hi, whi[:, c, 2, e, :], start=(n == 0 and t == 0), stop=False,
                                     skip_group_check=True)
                    nc.tensor.matmul(o, hi, wlo[:, c, 2, e, :], start=False, stop=False, skip_group_check=True)
                    mm = nc.tensor.matmul(o, lo, whi[:, c, 2, e, :], start=False,
                                          stop=(n == UNITS - 1), skip_group_check=True)
                mm.then_inc(down_done, 1)

            def three(o, lhs, rhs, start, stop):
                nc.tensor.matmul(o, lhs[0], rhs[0], start=start, stop=False)
                nc.tensor.matmul(o, lhs[0], rhs[1], start=False, stop=False)
                return nc.tensor.matmul(o, lhs[1], rhs[0], start=False, stop=stop)

            def mamba(name, s):
                t = s - 1

                def act_did(event):
                    pe.wait_ge(m_act, ACT_M.after(event, t))

                def dve_did(event):
                    pe.wait_ge(m_dve, DVE_M.after(event, t))

                def pool_did(event):
                    pe.wait_ge(m_pool, POOL_M.after(event, t))

                q = int(name.rstrip("ab")[-1]) if name.rstrip("ab")[-1] in "0123456789" else 0
                tok = slice(q * P, (q + 1) * P)
                tokens = (xT_hi[M], xT_lo[M])
                if name == "dt":
                    pe.wait_ge(ln_dve[M], DVE_LN.after("lo", t))
                    cols = slice(DI + CT * P, NPROJ)
                    for b in range(TT):
                        for kk in range(2):
                            mm = three(R[2][:, b * NH:(b + 1) * NH],
                                       [x[:, kk, b * P:(b + 1) * P] for x in tokens],
                                       (win_hi[:, kk, cols], win_lo[:, kk, cols]), kk == 0, kk == 1)
                elif name.startswith("xc"):
                    if q == 0:
                        pe.wait_ge(ln_dve[F], DVE_LN.after("lo", turn(F, s + 1)))
                    elif q == 2:
                        act_did("xc0")
                    for c in range(2):
                        ct = (4 + c) if q == 0 else 2 * (q - 1) + c
                        cols = slice(DI + ct * P, DI + (ct + 1) * P)
                        for kk in range(2):
                            mm = three(R[q % 2][:, c * TILE:(c + 1) * TILE],
                                       (win_hi[:, kk, cols], win_lo[:, kk, cols]),
                                       [x[:, kk, :] for x in tokens], kk == 0, kk == 1)
                elif name == "cum":
                    dve_did("dA")
                    pe.wait_ge(pass_read, s + 1)
                    for n, mat in enumerate((incl, ones, later)):
                        mm = nc.tensor.matmul(R[3][:, n * TT * NH:(n + 1) * TT * NH], mat, sp["dA"][:], start=True, stop=True)
                elif name.startswith("z"):
                    if q == 0:
                        act_did("xc1")
                    else:
                        dve_did("v")
                    for kk in range(2):
                        mm = three(R[1 + q][:, :], [x[:, kk, tok] for x in tokens],
                                   (win_hi[:, kk, 0:DI], win_lo[:, kk, 0:DI]), kk == 0, kk == 1)
                elif name.startswith("seg"):
                    ab = name[-1]
                    pool_did(f"Rl{q}")
                    act_did(("xc2" if q == 0 else "La0") if ab == "a" else ("zh0" if q == 0 else "Lb0"))
                    g = 0 if ab == "a" else 4
                    o = R[0 if ab == "a" else 1][:, :].rearrange("p (h l) -> p h l", h=4)
                    nc.tensor.matmul(o, later16[:], Rh[:, q, g:g + 4, :], start=True, stop=False)
                    mm = nc.tensor.matmul(o, later16[:], Rl[:, q, g:g + 4, :], start=False, stop=True)
                elif name == "bt":
                    dve_did("xs0")
                    act_did("zh1")
                    for b in range(TT):
                        mm = nc.tensor.transpose(R[2][:, b * P:(b + 1) * P], BT[:, b * P:(b + 1) * P], ident)
                elif name == "cb":
                    act_did("ex")
                    for b in range(TT):
                        cols = slice(b * P, (b + 1) * P)
                        mm = nc.tensor.matmul(R[3][:, cols], BT[:, cols], CTr[:, cols], start=True, stop=True)
                elif name.startswith("xt"):
                    dve_did("xs2")
                    act_did("bt" if q == 0 else "La1")
                    for c in range(4):
                        mm = nc.tensor.transpose(R[2 if q == 0 else 0][:, c * P:(c + 1) * P], xs[:, 2 + c, tok], ident)
                elif name.startswith("off"):
                    if q == 0:
                        dve_did("cb")
                        pe.wait_ge(set_pool, 1)
                    else:
                        dve_did("st0")
                    mm = nc.tensor.matmul(R[3][:, :], CTr[:, tok], state[:], start=True, stop=True)
                elif name.startswith("diag"):
                    pool_did(f"M{q}")
                    dve_did("xd0" if q == 0 else "y0")
                    if q == 0:
                        act_did("Lb1")
                    else:
                        dve_did("xd1")
                    for h in range(NH):
                        cols = slice(h * HD, (h + 1) * HD)
                        mm = nc.tensor.matmul(R[1][:, cols], Mm[:, q, h, :], xd[:, q, cols], start=True, stop=True)
                elif name.startswith("state"):
                    dve_did(f"xe{q}")
                    if q == 0:
                        act_did("xt0")
                    else:
                        dve_did("st0")
                    mm = nc.tensor.matmul(R[2][:, :], Bs[:, q, :], xe[:, q, :], start=True, stop=True)
                elif name.startswith("yt"):
                    pool_did(f"yn{q}")
                    if q == 0:
                        act_did("xt1")
                    else:
                        dve_did("y1")
                    for c in range(4):
                        mm = nc.tensor.transpose(R[q][:, c * P:(c + 1) * P], yn[:, q, c * P:(c + 1) * P], ident)
                elif name.startswith("out"):
                    dve_did(f"yl{q}")
                    dve_did("off1" if q == 0 else "out0")
                    for c in range(4):
                        mm = three(R[3][:, 0:D], (yT_hi[:, q, c, :], yT_lo[:, q, c, :]),
                                   (wout_hi[:, c, :], wout_lo[:, c, :]), c == 0, c == 3)
                mm.then_inc(m_pe, 1)

            def largest_transposed(g):
                w = 1 if g == 0 else 2
                pe.wait_ge(set_dve, SET_DVE_MAX[g])
                nc.tensor.transpose(R[1][0:w, 0:P], mx[:, g:g + w], ident).then_inc(set_pe, 1)

            def largest_everywhere(g):
                w = 1 if g == 0 else 2
                pe.wait_ge(set_dve, SET_DVE_DIAG[g])
                nc.tensor.matmul(R[1][:, 256:256 + w], ones[0:w, :], mdiag[0:w, 0:w],
                                 start=True, stop=True).then_inc(set_pe, 1)

            pe.wait_ge(s_cst, 16)
            largest_transposed(0)
            largest_everywhere(0)
            layer_norm_transpose(F, 0, 0, [])
            for q, (f, n) in enumerate(START_UNITS):
                gate_up_unit(f, n, q, None, start_bank)
                if q == 0:
                    layer_norm_transpose(E, 1, 2, [])
                if q >= DOWN_LAG:
                    down_unit(*START_UNITS[q - DOWN_LAG])
                if q == LARGEST_AT:
                    largest_transposed(1)
                if q == LARGEST_AT + 1:
                    largest_everywhere(1)
            layer_norm_transpose(F, 2, 0, [])
            layer_norm_transpose(M, 0, 2, [(ln_dve[E], DVE_LN.after("lo", 0))])

            def step(s, with_mamba, next_ffn):
                f = s + 1
                for n in range(UNITS):
                    gate_up_unit(f, n, n, f * UNITS, unit_bank)
                    down_unit(*((f, n - DOWN_LAG) if n >= DOWN_LAG else (f - 1, UNITS + n - DOWN_LAG)))
                    for name in PE_AT.get(n, "").split():
                        if name == "LN_f":
                            if next_ffn:
                                layer_norm_transpose(F, f + 1, 0, [(m_dve, DVE_M.after("yl0", s - 1))] if with_mamba
                                                     else [(ln_dve[F], DVE_LN.after("lo", turn(F, f)))])
                        elif name == "LN_m":
                            if with_mamba:
                                layer_norm_transpose(M, s, 2, [(m_dve, DVE_M.after("st1", s - 1))])
                        elif with_mamba:
                            mamba(name, s)

            steps(pe, step)
            for n in range(UNITS - DOWN_LAG, UNITS):
                down_unit(2 * NT - 1, n)

        @block.scalar
        def _(act):
            def layer_norm_hi(s, index, bank, free):
                for semaphore, value in free:
                    act.wait_ge(semaphore, value)
                act.wait_ge(ln_pe[s], turn(s, index) + 1)
                nc.scalar.activation(xT_hi[s][:].rearrange("p k t -> p (k t)"), R[bank][:, :], ACT.Copy).then_inc(ln_act[s], 1)

            def mamba(name, t):
                def pe_did(event):
                    act.wait_ge(m_pe, PE_M.after(event, t))

                def dve_did(event, tile=t):
                    act.wait_ge(m_dve, DVE_M.after(event, tile))

                q = int(name[-1]) if name[-1] in "0123456789" else 0
                four = lambda ap: ap.rearrange("p (h l) -> p h l", h=4)
                if name.startswith("xc"):
                    if q == 0:
                        dve_did("v")
                    pe_did(name)
                    ins = nc.scalar.activation(xc[:, 2 * q:2 * q + 2, HALO:], R[q % 2][:, :].rearrange("p (c t) -> p c t", c=2),
                                               ACT.Identity, scale=c_in)
                elif name == "spe":
                    dve_did("na")
                    nc.scalar.activation(A_exp[:], A_raw[:], ACT.Exp)
                    ins = nc.scalar.activation(sp["e"][:], sp["na"][:], ACT.Exp)
                elif name.startswith("th"):
                    dve_did(f"cv{q}_7")
                    ins = nc.scalar.activation(th[:, 2 * q:2 * q + 2, :], cv[:, 2 * q:2 * q + 2, :], ACT.Tanh)
                elif name.startswith("zt"):
                    pe_did(f"z{q}")
                    ins = nc.scalar.activation(zt[:, q, :], R[1 + q][:, :], ACT.Tanh, scale=c_in_half)
                elif name.startswith("zh"):
                    ins = nc.scalar.activation(zh[:, q, :], R[1 + q][:, :], ACT.Identity, scale=c_in_half)
                elif name == "ex":
                    pe_did("cum")
                    ins = nc.scalar.activation(ex[:].rearrange("p n q h -> p (n q h)"), R[3][:, 0:3 * TT * NH], ACT.Exp)
                elif name[0] == "L":
                    g = 0 if name[1] == "a" else 4
                    pe_did(f"seg{q}{name[1]}")
                    ins = nc.scalar.activation(L[:, q, g:g + 4, :], four(R[0 if g == 0 else 1][:, :]), ACT.Exp)
                elif name == "bt":
                    pe_did("bt")
                    ins = nc.scalar.activation(Bs[:].rearrange("p q n -> p (q n)"), R[2][:, 0:TT * P], ACT.Copy)
                elif name.startswith("xt"):
                    pe_did(name)
                    ins = nc.scalar.activation(xt[:, q, :], R[2 if q == 0 else 0][:, :], ACT.Copy)
                elif name.startswith("sq"):
                    dve_did(f"g{q}")
                    ins = nc.scalar.activation(ysq[:, q, :], y[:, q, :], ACT.Square, accum_out=yss[:, q:q + 1])
                elif name.startswith("yh"):
                    pe_did(f"yt{q}")
                    ins = nc.scalar.activation(yT_hi[:, q].rearrange("p c l -> p (c l)"), R[q][:, :], ACT.Copy)
                ins.then_inc(m_act, 1)

            def weight_hi(c):
                act.wait_ge(s_full, c + 1)
                nc.scalar.activation(whi[:, c, :, :, :].rearrange("p m k n -> p m n k"),
                                     wfull[:, c % 2, :].rearrange("p (m n k) -> p m n k", m=3, k=2), ACT.Copy).then_inc(s_whi, 1)

            def gelu_unit(number, bank):
                act.wait_ge(gu_done, number + 1)
                nc.scalar.activation(gelu[bank][:], gate_up[bank][:, 0, :], ACT.Gelu_apprx_tanh, scale=c_gate).then_inc(gelu_done, 1)

            def hi_unit(number, place, bank, first):
                act.wait_ge(hidden_done, number + 1)
                if not first:
                    act.wait_ge(down_done, number + 1 - RING)
                nc.scalar.activation(hid_hi[:, place, :], hidden[bank][:], ACT.Copy).then_inc(hi_done, 1)

            weight_hi(0)
            layer_norm_hi(F, 0, 0, [])
            layer_norm_hi(E, 1, 2, [])
            for q, (f, n) in enumerate(START_UNITS):
                for c in range(1, CH):
                    if q == max(1 if c == 1 else 4, first_unit(c) - 4):
                        weight_hi(c)
                gelu_unit(q, start_bank(q))
                if q >= 1:
                    hi_unit(q - 1, (q - 1) % RING, start_bank(q - 1), q - 1 < RING)
                if q in range(SCALE_AT, SCALE_AT + 4):
                    k = q - SCALE_AT
                    if k == 0:
                        act.wait_ge(s_small, 16 * (4 + 2 * TT))
                        act.wait_ge(s_wout, 16)
                    nc.scalar.activation(wout[:, k, :], wout[:, k, :], ACT.Copy, scale=nw[:, k:k + 1]).then_inc(set_act, 1)
                if q == SCALE_AT + 4:
                    nc.scalar.activation(cw[:], cw[:], ACT.Copy, scale=0.5).then_inc(set_act, 1)
                    nc.scalar.activation(cb[:], cb[:], ACT.Copy, scale=0.5).then_inc(set_act, 1)
                    nc.scalar.activation(incl16[:], incl, ACT.Copy).then_inc(set_act, 1)
                    nc.scalar.activation(later16[:], later, ACT.Copy).then_inc(set_act, 1)
                if q in (LARGEST_AT + 2, LARGEST_AT + 3):
                    k = q - LARGEST_AT - 2
                    act.wait_ge(set_dve, SET_DVE_POW[1])
                    nc.scalar.activation(win_hi[:, k, :], win[:, k, :], ACT.Identity, scale=f_in).then_inc(set_act, 1)
                if q == LARGEST_AT + 4:
                    flat = lambda ap: ap.rearrange("p k n -> p (k n)")
                    nc.scalar.activation(flat(wout_hi[:]), flat(wout), ACT.Identity, scale=f_out).then_inc(set_act, 1)
            last = 2 * UNITS - 1
            layer_norm_hi(F, 2, 0, [(gu_done, START_UNITS.index((0, UNITS - 1)) + 1)])
            hi_unit(last, last % RING, start_bank(last), False)
            layer_norm_hi(M, 0, 2, [(gu_done, 2 * UNITS)])

            def step(s, with_mamba, next_ffn):
                f = s + 1
                for n in range(UNITS):
                    if n == UNITS - 1 and next_ffn:
                        layer_norm_hi(F, f + 1, 0, [(gu_done, f * UNITS + UNITS)])
                    gelu_unit(f * UNITS + n, unit_bank(n))
                    if n >= 1:
                        hi_unit(f * UNITS + n - 1, (n - 1) % RING, unit_bank(n - 1), False)
                    for name in ACT_AT.get(n, "").split():
                        if with_mamba:
                            if name == "LN_m":
                                layer_norm_hi(M, s, 2, [(m_pe, PE_M.after("z1", s - 1))])
                            else:
                                mamba(name, s - 1)
                hi_unit(f * UNITS + UNITS - 1, (UNITS - 1) % RING, unit_bank(UNITS - 1), False)

            steps(act, step)

        @block.vector
        def _(dve):
            def wait_apart(semaphore, value):
                dve.wait_ge(semaphore, value)
                if not isinstance(value, int):
                    cell = next(spare_cells)
                    nc.vector.memset(spare_dve[:, cell:cell + 1], 0.0)

            def layer_norm_stats(s, index):
                for t in range(TT):
                    nc.vector.bn_stats(stats[s][:, t, :], of_tile(ln_src[s], index)[:, t, :]).then_inc(ln_dve[s], 1)

            def layer_norm_aggregate(s, index):
                wait_apart(ln_dve[s], DVE_LN.after("stats1", turn(s, index)))
                for t in range(TT):
                    nc.vector.bn_aggr(aggr[s][:, t, :], stats[s][:, t, :]).then_inc(ln_dve[s], 1)

            def layer_norm_scale(s, index):
                dve.wait_ge(ln_pool[s], POOL_LN.after("rstd", turn(s, index)))
                for t in range(TT):
                    nc.vector.tensor_scalar(xn[s][:, t, :], of_tile(ln_src[s], index)[:, t, :], aggr[s][:, t, 0:1],
                                            rstd[s][:, t:t + 1], ALU.subtract, ALU.mult).then_inc(ln_dve[s], 1)

            def layer_norm_lo(s, index, bank):
                dve.wait_ge(ln_act[s], turn(s, index) + 1)
                nc.vector.tensor_tensor(xT_lo[s][:].rearrange("p k t -> p (k t)"), R[bank][:, :],
                                        xT_hi[s][:].rearrange("p k t -> p (k t)"), ALU.subtract).then_inc(ln_dve[s], 1)

            def own(name, t):
                dve.wait_ge(m_dve, DVE_M.after(name, t))

            def conv(p, half, t):
                if half == 0:
                    dve.wait_ge(m_act, ACT_M.after(f"xc{p}", t))
                for k in range(half * TAPS // 2, (half + 1) * TAPS // 2):
                    for c in range(2):
                        blk = 2 * p + c
                        ct = (4 + c) if p == 0 else 2 * (p - 1) + c
                        src = xc[:, blk, k:k + TILE]
                        if k == 0:
                            ins = nc.vector.tensor_scalar(cv[:, blk, :], src, cw[:, ct, 0:1], cb[:, ct:ct + 1], ALU.mult, ALU.add)
                        else:
                            own(f"cv{p}_{2 * (k - 1) + c}", t)
                            ins = nc.vector.scalar_tensor_tensor(cv[:, blk, :], src, cw[:, ct, k:k + 1], cv[:, blk, :], ALU.mult, ALU.add)
                        ins.then_inc(m_dve, 1)

            def soft_plus(t):
                inc = lambda a: a.then_inc(m_dve, 1)
                dve.wait_ge(m_act, ACT_M.after("spe", t))
                inc(nc.vector.tensor_scalar(sp["e2"][:], sp["e"][:], 2.0, None, ALU.add))
                own("e2", t)
                inc(nc.vector.reciprocal(sp["er"][:], sp["e2"][:]))
                own("er", t)
                inc(nc.vector.tensor_tensor(sp["r"][:], sp["e"][:], sp["er"][:], ALU.mult))
                own("r", t)
                inc(nc.vector.tensor_tensor(sp["r2"][:], sp["r"][:], sp["r"][:], ALU.mult))
                own("r2", t)
                inc(nc.vector.tensor_scalar(spq[0][:], sp["r2"][:], 1.0 / (2 * LOG_TERMS + 1), None, ALU.mult))
                for k in range(1, LOG_TERMS):
                    own(f"q{k - 1}", t)
                    inc(nc.vector.scalar_tensor_tensor(spq[k][:], spq[k - 1][:], 1.0 / (2 * (LOG_TERMS - k) + 1),
                                                       sp["r2"][:], ALU.add, ALU.mult))
                own(f"q{LOG_TERMS - 1}", t)
                inc(nc.vector.scalar_tensor_tensor(sp["l"][:], spq[-1][:], 1.0, sp["r"][:], ALU.add, ALU.mult))
                inc(nc.vector.tensor_scalar(sp["mv"][:], sp["v"][:], 0.0, None, ALU.max))
                own("mv", t)
                inc(nc.vector.scalar_tensor_tensor(sp["dt"][:], sp["l"][:], 2.0, sp["mv"][:], ALU.mult, ALU.add))
                own("dt", t)
                inc(nc.vector.scalar_tensor_tensor(sp["dA"][:], sp["dt"][:], -1.0, A_exp[:].rearrange("p t h -> p (t h)"),
                                                   ALU.mult, ALU.mult))
                own("dA", t)
                inc(nc.vector.tensor_scalar(dh[:], sp["dA"][:], DECAY_FLOOR, None, ALU.max))
                own("dh", t)
                inc(nc.vector.scalar_tensor_tensor(dl[:], sp["dA"][:], DECAY_FLOOR, dh[:], ALU.max, ALU.subtract))

            def mamba(name, t):
                def pe_did(event):
                    dve.wait_ge(m_pe, PE_M.after(event, t))

                def act_did(event):
                    dve.wait_ge(m_act, ACT_M.after(event, t))

                if name.startswith("cv"):
                    return conv(int(name[2]), "ab".index(name[3]), t)
                q = int(name[-1]) if name[-1] in "0123456789" else 0
                by_head = lambda ap: ap.rearrange("p (h d) -> p h d", h=NH)
                heads = lambda ap: ap.rearrange("p (h o) -> p h o", o=1).to_broadcast([P, NH, HD])
                flat = lambda ap: ap.rearrange("p c t -> p (c t)")
                if name == "soft":
                    return soft_plus(t)
                if name == "v":
                    pe_did("dt")
                    ins = nc.vector.scalar_tensor_tensor(sp["v"][:], R[2][:, 0:TT * NH], c_in, dtb[:].rearrange("p t h -> p (t h)"),
                                                         ALU.mult, ALU.add)
                elif name == "na":
                    own("v", t)
                    ins = nc.vector.scalar_tensor_tensor(sp["na"][:], sp["v"][:], -1.0, sp["v"][:], ALU.mult, ALU.min)
                elif name == "halo":
                    own("cv2_7", t)
                    ins = nc.vector.tensor_copy(xc[:, :, 0:HALO], xc[:, :, TILE:TILE + HALO])
                elif name.startswith("xs"):
                    act_did(f"th{q}")
                    sl = slice(2 * q, 2 * q + 2)
                    ins = nc.vector.scalar_tensor_tensor(flat(xs[:, sl, :]), flat(th[:, sl, :]), 1.0, flat(cv[:, sl, :]),
                                                         ALU.add, ALU.mult)
                elif name.startswith("zg"):
                    act_did(f"zh{q}")
                    ins = nc.vector.scalar_tensor_tensor(zg[:, q, :], zt[:, q, :], 1.0, zh[:, q, :], ALU.add, ALU.mult)
                elif name == "cb":
                    pe_did("cb")
                    ins = nc.vector.tensor_tensor(cbm[:], R[3][:, 0:TT * P].rearrange("p (q l) -> p q l", q=TT),
                                                  incl.rearrange("p (o l) -> p o l", o=1).to_broadcast([P, TT, P]), ALU.mult)
                elif name.startswith("xd"):
                    act_did(f"xt{q}")
                    ins = nc.vector.tensor_tensor(by_head(xd[:, q, :]), by_head(xt[:, q, :]), heads(sp["dt"][:, q * NH:(q + 1) * NH]), ALU.mult)
                elif name.startswith("off"):
                    pe_did(f"off{q}")
                    ins = nc.vector.tensor_tensor(by_head(yo[:, q, :]), by_head(R[3][:, :]), heads(ex[:, 0, q, :]), ALU.mult)
                elif name.startswith("xe"):
                    own(f"xd{q}", t)
                    ins = nc.vector.tensor_tensor(by_head(xe[:, q, :]), by_head(xd[:, q, :]), heads(ex[:, 2, q, :]), ALU.mult)
                elif name.startswith("yx"):
                    own(f"off{q}", t)
                    dve.wait_ge(m_pool, POOL_M.after(f"xD{q}", t))
                    ins = nc.vector.tensor_tensor(yo[:, q, :], yo[:, q, :], xD[:, q, :], ALU.add)
                elif name in ("y0", "y1"):
                    own(f"yx{q}", t)
                    pe_did(f"diag{q}")
                    ins = nc.vector.tensor_tensor(y[:, q, :], R[1][:, :], yo[:, q, :], ALU.add)
                elif name[0] == "g":
                    own(f"y{q}", t)
                    ins = nc.vector.tensor_tensor(y[:, q, :], y[:, q, :], zg[:, q, :], ALU.mult)
                elif name.startswith("st"):
                    pe_did(f"state{q}")
                    dve.wait_ge(m_pool, POOL_M.after(f"sd{q}", t))
                    ins = nc.vector.tensor_tensor(state[:], R[2][:, :], state[:], ALU.add)
                elif name.startswith("yl"):
                    act_did(f"yh{q}")
                    ins = nc.vector.tensor_tensor(yT_lo[:, q].rearrange("p c l -> p (c l)"), R[q][:, :],
                                                  yT_hi[:, q].rearrange("p c l -> p (c l)"), ALU.subtract)
                elif name.startswith("out"):
                    pe_did(f"out{q}")
                    ins = nc.vector.scalar_tensor_tensor(of_tile(ffn_in, t)[:, q, :], R[3][:, 0:D], c_out,
                                                         of_tile(ffn_out, t)[:, q, :], ALU.mult, ALU.add)
                ins.then_inc(m_dve, 1)

            def decode(c, steps):
                for step in steps:
                    if step == 0:
                        dve.wait_ge(s_words[c % 2], 16 * (c // 2 + 1))
                        ins = nc.vector.tensor_scalar(t0, pk[:, c % 2, :], 0xFF, 12, ALU.bitwise_and, ALU.logical_shift_left)
                    else:
                        dve.wait_ge(s_step, 3 * c + step)
                        if step == 1:
                            ins = nc.vector.scalar_tensor_tensor(t1, pk[:, c % 2, :], 24, t0, ALU.logical_shift_left, ALU.bitwise_or)
                        elif step == 2:
                            ins = nc.vector.tensor_scalar(t0, t1, 3, 0x0E000E00, ALU.logical_shift_right, ALU.bitwise_and)
                        else:
                            ins = nc.vector.scalar_tensor_tensor(codes, t1, 0x80008000, t0, ALU.bitwise_and, ALU.bitwise_or)
                    ins.then_inc(s_decoded if step == 3 else s_step, 1)

            def weight_full(c):
                dve.wait_ge(s_decoded, c + 1)
                dve.wait_ge(s_scales[c % 2], 16 * (c // 2 + 1))
                if c >= 2:
                    pool_lo, dve_lo = lo_parts_done(c - 2)
                    if pool_lo:
                        dve.wait_ge(s_wlo_pool, pool_lo)
                    dve.wait_ge(s_wlo_dve, dve_lo)
                nc.vector.scalar_tensor_tensor(
                    wfull[:, c % 2, :].rearrange("p (n k) -> p n k", k=2),
                    codes.bitcast(F16).rearrange("p (n k) -> p n k", k=2), f_code,
                    sc[:, c % 2, :].rearrange("p (n o) -> p n o", o=1).to_broadcast([P, 3 * WCOL, 2]),
                    ALU.mult, ALU.mult).then_inc(s_full, 1)

            def weight_lo_matrix(c, mat):
                nc.vector.tensor_tensor(
                    wlo[:, c, mat, :, :].rearrange("p k n -> p n k"),
                    wfull[:, c % 2, :].rearrange("p (m n k) -> p m n k", m=3, k=2)[:, mat, :, :],
                    whi[:, c, mat, :, :].rearrange("p k n -> p n k"), ALU.subtract).then_inc(s_wlo_dve, 1)

            def weight_lo_dve(c, down=True):
                dve.wait_ge(s_whi, c + 1)
                for mat in range(pool_matrices(c), 3 if down else 2):
                    weight_lo_matrix(c, mat)

            def hidden_unit(number, bank, before):
                dve.wait_ge(gelu_done, number + 1)
                if before is not None:
                    dve.wait_ge(lo_done, before + 1)
                nc.vector.scalar_tensor_tensor(hidden[bank][:], gate_up[bank][:, 1, :], c_up, gelu[bank][:], ALU.mult, ALU.mult).then_inc(hidden_done, 1)

            def pass_end(f, units_done, bank=0):
                dve.wait_ge(down_done, units_done)
                flat = lambda ap: ap.rearrange("p t d -> p (t d)")
                nc.vector.scalar_tensor_tensor(flat(of_tile(ffn_out, f)), flat(down_bank[bank][:]), c_down,
                                               flat(of_tile(ffn_in, f)), ALU.mult, ALU.add).then_inc(pass_read, 1)

            done = [0]

            def chained(ins):
                done[0] += 1
                ins.then_inc(set_dve, 1)
                dve.wait_ge(set_dve, done[0])

            chained(nc.vector.memset(half[:], -0.5))
            chained(nc.vector.memset(xc[:, :, 0:HALO], 0.0))
            dve.wait_ge(s_sflat, 16)
            chained(nc.vector.tensor_reduce(mx[:, 0:1], sflat[:], AX.X, ALU.max, apply_absolute_value=True))
            assert done[0] == SET_DVE_MAX[0]

            def counted(ins):
                done[0] += 1
                ins.then_inc(set_dve, 1)

            def largest_rows(g, w):
                dve.wait_ge(set_pe, 2 * g + 1)
                chained(nc.vector.tensor_reduce(mrow[0:w, 0:1], R[1][0:w, 0:P], AX.X, ALU.max))
                chained(nc.vector.tensor_scalar(mdiag[0:w, 0:w], ident[0:w, 0:w], mrow[0:w, 0:1], None, ALU.mult))
                assert done[0] == SET_DVE_DIAG[g]

            def powers(g, w):
                dve.wait_ge(set_pe, 2 * g + 2)
                chained(nc.vector.tensor_scalar(pw[:, g:g + w], R[1][:, 256:256 + w], SMALLEST, None, ALU.max))
                chained(nc.vector.tensor_scalar(pw[:, g:g + w].bitcast(U32), pw[:, g:g + w].bitcast(U32), 0x7F800000, None, ALU.bitwise_and))
                chained(nc.vector.reciprocal(pw[:, 3 + g:3 + g + w], pw[:, g:g + w]))

            decode(0, (0, 1))
            dve.wait_ge(s_cst, 16)
            largest_rows(0, 1)
            decode(0, (2, 3))
            powers(0, 1)
            chained(nc.vector.tensor_scalar(f_code, r_ffn, 2.0 ** (CODE_BITS + FFN_BITS), None, ALU.mult))
            dve.wait_ge(s_x[0], 16)
            layer_norm_stats(F, 0)
            layer_norm_aggregate(F, 0)
            weight_full(0)
            layer_norm_scale(F, 0)
            dve.wait_ge(s_x[1], 16)
            layer_norm_stats(E, 1)
            counted(nc.vector.tensor_scalar(c_gate, m_ffn, 2.0 ** -(FFN_BITS + ACTIVATION_BITS), None, ALU.mult))
            chained(nc.vector.tensor_tensor(m_cube, m_ffn, m_ffn, ALU.mult))
            layer_norm_aggregate(E, 1)
            weight_lo_dve(0, down=False)
            layer_norm_lo(F, 0, 0)
            chained(nc.vector.tensor_tensor(m_cube, m_cube, m_ffn, ALU.mult))
            counted(nc.vector.tensor_scalar(c_up, r_ffn, 2.0 ** (HIDDEN_BITS - FFN_BITS - ACTIVATION_BITS), None, ALU.mult))
            counted(nc.vector.tensor_scalar(c_down, m_cube, 0.5 * 2.0 ** -(FFN_BITS + HIDDEN_BITS), None, ALU.mult))
            layer_norm_scale(E, 1)
            assert done[0] == SET_DVE_POW[0], done
            dve.wait_ge(set_dve, SET_DVE_POW[0])
            decode(1, range(4))
            weight_full(1)
            layer_norm_lo(E, 1, 2)

            def projection_setup(q):
                largest = lambda column, ap: nc.vector.tensor_reduce(mx[:, column:column + 1], ap, AX.X, ALU.max,
                                                                     apply_absolute_value=True)
                flat = lambda ap: ap.rearrange("p k n -> p (k n)")
                if q == LARGEST_AT - 3:
                    dve.wait_ge(s_win, 16)
                    counted(largest(1, win[:, 0, :]))
                elif q == LARGEST_AT - 2:
                    counted(largest(3, win[:, 1, :]))
                elif q == LARGEST_AT - 1:
                    dve.wait_ge(set_act, 4)
                    chained(largest(2, flat(wout)))
                    chained(nc.vector.tensor_tensor(mx[:, 1:2], mx[:, 1:2], mx[:, 3:4], ALU.max))
                    assert done[0] == SET_DVE_MAX[1], done
                elif q == LARGEST_AT:
                    largest_rows(1, 2)
                elif q == LARGEST_AT + 1:
                    powers(1, 2)
                    counted(nc.vector.tensor_scalar(pw[:, 13:15], pw[:, 4:6], 2.0 ** PROJ_BITS, None, ALU.mult))
                    counted(nc.vector.tensor_scalar(c_in, m_in, 2.0 ** -(PROJ_BITS + ACTIVATION_BITS), None, ALU.mult))
                    counted(nc.vector.tensor_scalar(c_in_half, m_in, 2.0 ** -(PROJ_BITS + ACTIVATION_BITS + 1), None, ALU.mult))
                    counted(nc.vector.tensor_scalar(c_out, m_out, 2.0 ** -(PROJ_BITS + ACTIVATION_BITS), None, ALU.mult))
                    assert done[0] == SET_DVE_POW[1], done
                    dve.wait_ge(set_dve, SET_DVE_POW[1])
                elif q == LARGEST_AT + 4:
                    dve.wait_ge(set_act, SET_ACT_SCALED + 1)
                    counted(nc.vector.scalar_tensor_tensor(win_lo[:, 0, :], win[:, 0, :], f_in, win_hi[:, 0, :], ALU.mult, ALU.subtract))
                elif q == LARGEST_AT + 7:
                    dve.wait_ge(set_act, SET_ACT_SCALED + 2)
                    counted(nc.vector.scalar_tensor_tensor(win_lo[:, 1, :], win[:, 1, :], f_in, win_hi[:, 1, :], ALU.mult, ALU.subtract))
                elif q == LARGEST_AT + 8:
                    dve.wait_ge(set_act, SET_ACT_SCALED + 3)
                    counted(nc.vector.scalar_tensor_tensor(flat(wout_lo[:]), flat(wout), f_out, flat(wout_hi[:]), ALU.mult, ALU.subtract))

            for q, (f, n) in enumerate(START_UNITS):
                for c in range(2, CH):
                    if q == max(2, first_unit(c) - 9):
                        decode(c, (0, 1))
                    if q == max(3, first_unit(c) - 8):
                        decode(c, (2, 3))
                    if q == max(3, first_unit(c) - 7):
                        weight_full(c)
                for c in range(1, CH):
                    if q == max(1 if c == 1 else 4, first_unit(c) - 4):
                        weight_lo_dve(c)
                before = before_in_bank(q, start_bank)
                if q == FIRST_OUT:
                    pass_end(0, START_UNITS.index((0, UNITS - 1)) + 1, bank=1)
                    dve.wait_ge(pass_read, 1)
                    layer_norm_stats(M, 0)
                    layer_norm_aggregate(M, 0)
                if q == FIRST_OUT + 1:
                    layer_norm_scale(M, 0)
                hidden_unit(q, start_bank(q), before if before >= 0 else None)
                if q == 0:
                    weight_lo_matrix(0, 2)
                projection_setup(q)
                if q == LARGEST_AT + 2:
                    dve.wait_ge(s_x[2], 16 * (NT - 2))
                    layer_norm_stats(F, 2)
                    layer_norm_aggregate(F, 2)
                if q == LARGEST_AT + 3:
                    layer_norm_scale(F, 2)
            layer_norm_lo(F, 2, 0)
            projection_setup(LARGEST_AT + 7)
            layer_norm_lo(M, 0, 2)
            projection_setup(LARGEST_AT + 8)

            def step(s, with_mamba, next_ffn):
                f = s + 1
                for n in range(UNITS):
                    if n == UNITS - 1 and next_ffn:
                        layer_norm_lo(F, f + 1, 0)
                    hidden_unit(f * UNITS + n, unit_bank(n), f * UNITS + before_in_bank(n, unit_bank))
                    if n == DOWN_LAG - 1:
                        pass_end(f - 1, f * UNITS)
                    for name in DVE_AT.get(n, "").split():
                        if name == "stats":
                            if with_mamba:
                                wait_apart(m_dve, DVE_M.after("cb", s - 1))
                                wait_apart(pass_read, s + 1)
                                layer_norm_stats(M, s)
                            elif next_ffn:
                                dve.wait_ge(m_dve, DVE_M.after("out1", NT - 1))
                            if next_ffn:
                                layer_norm_stats(F, f + 1)
                            if with_mamba:
                                layer_norm_aggregate(M, s)
                            if next_ffn:
                                layer_norm_aggregate(F, f + 1)
                        elif name == "scale":
                            if with_mamba:
                                layer_norm_scale(M, s)
                            if next_ffn:
                                layer_norm_scale(F, f + 1)
                        elif with_mamba:
                            if name == "LN_m":
                                layer_norm_lo(M, s, 2)
                            else:
                                mamba(name, s - 1)

            steps(dve, step)
            pass_end(2 * NT - 1, 2 * NT * UNITS)

        @block.gpsimd
        def _(pool):
            def wait_apart(semaphore, value):
                pool.wait_ge(semaphore, value)
                if not isinstance(value, int):
                    cell = next(spare_cells)
                    nc.gpsimd.tensor_tensor(spare_pool[:, cell:cell + 1], half[:], half[:], ALU.add)

            def layer_norm_rstd(s, index):
                wait_apart(ln_dve[s], DVE_LN.after("aggr1", turn(s, index)))
                g = 2.0 ** (-2 * ACTIVATION_BITS)
                nc.gpsimd.tensor_scalar(ve[s][:], aggr[s][:, :, 1], EPS, g, ALU.add, ALU.mult).then_inc(ln_pool[s], 1)
                pool.wait_ge(ln_pool[s], POOL_LN.after("ve", turn(s, index)))
                nc.gpsimd.tensor_tensor(rstd[s][:], ve[s][:], half[:].to_broadcast([P, TT]), ALU.pow).then_inc(ln_pool[s], 1)

            def mamba(name, t):
                def pe_did(event):
                    pool.wait_ge(m_pe, PE_M.after(event, t))

                def act_did(event):
                    pool.wait_ge(m_act, ACT_M.after(event, t))

                def dve_did(event):
                    pool.wait_ge(m_dve, DVE_M.after(event, t))

                q = int(name[-1])
                by_head = lambda ap: ap.rearrange("p (h d) -> p h d", h=NH)
                heads = lambda ap, n: ap.rearrange("p (h o) -> p h o", o=1).to_broadcast([P, NH, n])
                over = lambda ap: ap.rearrange("p (o l) -> p o l", o=1).to_broadcast([P, NH, P])
                if name[0] == "R":
                    part = Rh if name[1] == "h" else Rl
                    dve_did("dl")
                    d = (dh if name[1] == "h" else dl)[:, q * NH:(q + 1) * NH]
                    ins = nc.gpsimd.tensor_tensor(part[:, q, :, :], over(incl16[:]), heads(d, P), ALU.mult)
                elif name[0] == "M":
                    act_did(f"Lb{q}")
                    dve_did("cb")
                    ins = nc.gpsimd.tensor_tensor(Mm[:, q, :, :], L[:, q, :, :], over(cbm[:, q, :]), ALU.mult)
                elif name[:2] == "xD":
                    act_did(f"xt{q}")
                    ins = nc.gpsimd.tensor_tensor(by_head(xD[:, q, :]), by_head(xt[:, q, :]), heads(dsk[:], HD), ALU.mult)
                elif name[:2] == "sd":
                    pe_did(f"off{q}")
                    ins = nc.gpsimd.tensor_tensor(by_head(state[:]), by_head(state[:]), heads(ex[:, 1, q, :], HD), ALU.mult)
                elif name[:2] == "ve":
                    wait_apart(m_act, ACT_M.after(f"sq{q}", t))
                    ins = nc.gpsimd.tensor_scalar(yve[:, q:q + 1], yss[:, q:q + 1], 1.0 / DI, EPS, ALU.mult, ALU.add)
                elif name[:2] == "rs":
                    pool.wait_ge(m_pool, POOL_M.after(f"ve{q}", t))
                    ins = nc.gpsimd.tensor_tensor(yrs[:, q:q + 1], yve[:, q:q + 1], half[:], ALU.pow)
                elif name[:2] == "yn":
                    wait_apart(m_pool, POOL_M.after(f"rs{q}", t))
                    ins = nc.gpsimd.tensor_scalar(yn[:, q, :], y[:, q, :], yrs[:, q:q + 1], 2.0 ** ACTIVATION_BITS, ALU.mult, ALU.mult)
                ins.then_inc(m_pool, 1)

            def lo_unit(number, place, bank):
                pool.wait_ge(hi_done, number + 1)
                nc.gpsimd.tensor_tensor(hid_lo[:, place, :], hidden[bank][:], hid_hi[:, place, :],
                                        ALU.subtract).then_inc(lo_done, 1)

            def weight_lo_pool(c, mat):
                if mat == 0:
                    pool.wait_ge(s_whi, c + 1)
                nc.gpsimd.tensor_tensor(
                    wlo[:, c, mat, :, :].rearrange("p k n -> p n k"),
                    wfull[:, c % 2, :].rearrange("p (m n k) -> p m n k", m=3, k=2)[:, mat, :, :],
                    whi[:, c, mat, :, :].rearrange("p k n -> p n k"), ALU.subtract).then_inc(s_wlo_pool, 1)

            nc.gpsimd.memset(state[:], 0.0).then_inc(set_pool, 1)
            pool.wait_ge(set_dve, 1)
            layer_norm_rstd(F, 0)
            layer_norm_rstd(E, 1)
            for q in range(2 * UNITS):
                for c in range(1, CH):
                    for mat in range(pool_matrices(c)):
                        if q == max(1 if c == 1 else 4 + mat, first_unit(c) - 4 + 1 * mat):
                            weight_lo_pool(c, mat)
                if q >= 1:
                    lo_unit(q - 1, (q - 1) % RING, start_bank(q - 1))
                if q == LARGEST_AT + 2:
                    layer_norm_rstd(F, 2)
                if q == FIRST_OUT:
                    layer_norm_rstd(M, 0)
            last = 2 * UNITS - 1
            lo_unit(last, last % RING, start_bank(last))

            def step(s, with_mamba, next_ffn):
                f = s + 1
                for n in range(UNITS):
                    if n >= 1:
                        lo_unit(f * UNITS + n - 1, (n - 1) % RING, unit_bank(n - 1))
                    for name in POOL_AT.get(n, "").split():
                        if name == "rstd":
                            if with_mamba:
                                layer_norm_rstd(M, s)
                            if next_ffn:
                                layer_norm_rstd(F, f + 1)
                        elif with_mamba:
                            mamba(name, s - 1)
                lo_unit(f * UNITS + UNITS - 1, (UNITS - 1) % RING, unit_bank(UNITS - 1))

            steps(pool, step)


SET_DVE_MAX = (3, 18)
SET_DVE_DIAG = (5, 20)
SET_DVE_POW = (14, 27)
SET_ACT_SCALED = 8


def kernel(L0_attn_u, L0_attn_in_proj_w, L0_attn_conv_w, L0_attn_conv_b, L0_attn_dt_bias, L0_attn_A_log,
           L0_attn_D_skip, L0_attn_norm_w, L0_attn_out_proj_w, L0_ffn_gate_W_packed, L0_ffn_gate_scales,
           L0_ffn_up_W_packed, L0_ffn_up_scales, L0_ffn_down_W_packed, L0_ffn_down_scales):
    import concourse.bacc as bacc
    from concourse.bass_utils import run_bass_kernel_spmd

    def rows(a, last):
        return np.asarray(a).reshape(CH, P, 2, last).transpose(3, 0, 2, 1).reshape(last, CH, 2 * P)

    def cols(a, per):
        return np.asarray(a).reshape(D, CH, per).transpose(2, 1, 0)

    packed = np.stack([rows(L0_ffn_gate_W_packed, P), rows(L0_ffn_up_W_packed, P),
                       cols(L0_ffn_down_W_packed, P)], axis=2)
    scales = np.stack([rows(L0_ffn_gate_scales, 8), rows(L0_ffn_up_scales, 8),
                       cols(L0_ffn_down_scales, 8)], axis=2)
    w_in = np.asarray(L0_attn_in_proj_w).T.reshape(P, 2, NPROJ)
    at = np.arange(P)
    consts = np.stack([at[:, None] == at, at[:, None] <= at, at[:, None] > at, np.ones((P, P), bool)], axis=1).astype(np.float32)
    arrays = {
        "x": np.asarray(L0_attn_u),
        "packed": packed,
        "scales": scales,
        "w_in": w_in,
        "conv_w": np.asarray(L0_attn_conv_w).reshape(CT, P, TAPS).transpose(1, 0, 2),
        "conv_b": np.asarray(L0_attn_conv_b).reshape(CT, P).T,
        "dt_bias": np.asarray(L0_attn_dt_bias),
        "A_log": np.asarray(L0_attn_A_log),
        "D_skip": np.asarray(L0_attn_D_skip),
        "norm_w": np.asarray(L0_attn_norm_w).reshape(4, P).T,
        "w_out": np.asarray(L0_attn_out_proj_w).T.reshape(4, P, D).transpose(1, 0, 2),
        "consts": consts,
    }
    arrays = {k: np.ascontiguousarray(v) for k, v in arrays.items()}
    nc = bacc.Bacc("TRN2", target_bir_lowering=False, num_devices=1)
    args = [nc.dram_tensor(k, v.shape, mybir.dt.from_np(v.dtype), kind="ExternalInput").ap() for k, v in arrays.items()]
    out = nc.dram_tensor("out", (1, SEQ, D), F32, kind="ExternalOutput").ap()
    macaron(nc, *args, out)
    result = run_bass_kernel_spmd(nc, [arrays], core_ids=[0])
    return result.results[0]["out"]
```
